# Optimizing a Trainium2 kernel written in Bass

```python
import numpy as np
import jax
import jax.numpy as jnp

def _softmax(x, axis=-1):
    return jax.nn.softmax(x, axis=axis)

def _gelu(x):
    return jax.nn.gelu(x, approximate=True)

def _silu(x):
    return jax.nn.silu(x)

def _sigmoid(x):
    return jax.nn.sigmoid(x)

def _layernorm(x, axis=-1, eps=1e-05):
    m = jnp.mean(x, axis=axis, keepdims=True)
    v = jnp.var(x, axis=axis, keepdims=True)
    return (x - m) / jnp.sqrt(v + eps)

def _scatter_add(tgt, idx, src, axis=0):
    return tgt.at[idx].add(src)

def _segment_sum(src, seg, n):
    return jax.ops.segment_sum(src, seg, n)
kernel_name = 'mk_decoder_preln_d2_seqx_r8_ee7254'

def setup_inputs(seed: int=0):
    np.random.seed(seed)
    _w = jnp.asarray

    def _rec_inputs():
        import jax
        import jax.numpy as jnp
        _rk = jax.random.key(seed)
        x = 7.22e-05 + 1 * jax.random.normal(jax.random.fold_in(_rk, 1), (32, 128, 128), jnp.float32)
        _lenS = 128 - jax.random.randint(jax.random.fold_in(_rk, 7), (32,), 0, max(1, 128 // 4) + 1, jnp.int32)
        _lenS2 = 128 - jax.random.randint(jax.random.fold_in(_rk, 8), (32,), 0, max(1, 128 // 4) + 1, jnp.int32)
        _ctx_768P = jax.random.normal(jax.random.fold_in(_rk, 11), (32, 16, 96), jnp.float32)
        _ctx_768c = jax.random.dirichlet(jax.random.fold_in(_rk, 511), 0.3 * jnp.ones((16,), jnp.float32), (32, 128))
        _ctx_768t = jnp.einsum('bsk,bkd->bsd', _ctx_768c, _ctx_768P)
        _ctx_768t = _ctx_768t * jax.lax.rsqrt(jnp.mean(jnp.square(_ctx_768t)) + 1e-12) * 0.953939
        ctx_768 = -0.000191848 + 0.999787 * (_ctx_768t + 0.3 * jax.random.normal(jax.random.fold_in(_rk, 611), (32, 128, 96), jnp.float32))
        _validS = jnp.arange(128)[None, :] < _lenS[:, None]
        _validS2 = jnp.arange(128)[None, :] < _lenS2[:, None]
        _causal = jnp.tril(jnp.ones((128, 128), dtype=bool))
        mask_BxS2_bk0 = jnp.logical_not(jnp.broadcast_to(_validS2[:, :], (32, 128)))
        return (x, ctx_768, mask_BxS2_bk0)
    x, ctx_768, mask_BxS2_bk0 = _rec_inputs()

    def _L0_attn_setup():
        import jax, jax.numpy as jnp
        import numpy as np
        D_MODEL = 128
        NHEAD = 16
        HEAD_DIM = D_MODEL // NHEAD

        def _rope(x, sin, cos):
            half = x.shape[-1] // 2
            x1, x2 = (x[..., :half], x[..., half:])
            rotated = jnp.concatenate([-x2, x1], axis=-1)
            return x * cos + rotated * sin
        key = jax.random.key(seed)
        ks = jax.random.split(key, 9)
        s = 0.02
        x = jax.random.normal(ks[0], (2, 256, D_MODEL), dtype=jnp.float32)
        Wq = jax.random.normal(ks[1], (D_MODEL, D_MODEL), dtype=jnp.float32) * s
        bq = jnp.zeros((D_MODEL,), jnp.float32)
        Wk = jax.random.normal(ks[2], (D_MODEL, D_MODEL), dtype=jnp.float32) * s
        bk = jnp.zeros((D_MODEL,), jnp.float32)
        Wv = jax.random.normal(ks[3], (D_MODEL, D_MODEL), dtype=jnp.float32) * s
        bv = jnp.zeros((D_MODEL,), jnp.float32)
        Wo = jax.random.normal(ks[4], (D_MODEL, D_MODEL), dtype=jnp.float32) * s
        bo = jnp.zeros((D_MODEL,), jnp.float32)
        return {'x': x, 'Wq': Wq, 'bq': bq, 'Wk': Wk, 'bk': bk, 'Wv': Wv, 'bv': bv, 'Wo': Wo, 'bo': bo}
    _L0_attn_all = _L0_attn_setup()
    _L0_attn_in = {k: v for k, v in _L0_attn_all.items() if k in ('Wq', 'bq', 'Wk', 'bk', 'Wv', 'bv', 'Wo', 'bo')}
    del _L0_attn_all

    def _L0_xattn_setup():
        import jax, jax.numpy as jnp
        import numpy as np
        NUM_HEADS = 16
        CLAMP = 10000.0
        key = jax.random.key(seed)
        ks = jax.random.split(key, 8)
        B, Nq, Nkv, Cq, Ckv = (4, 256, 256, 128, 96)
        s_q = 1.0 / np.sqrt(Cq)
        s_kv = 1.0 / np.sqrt(Ckv)
        return {'query': jax.random.normal(ks[0], (B, Nq, Cq), jnp.float32), 'key_value': jax.random.normal(ks[1], (B, Nkv, Ckv), jnp.float32), 'Wq': jax.random.normal(ks[2], (Cq, Cq), jnp.float32) * s_q, 'bq': jnp.zeros((Cq,), jnp.float32), 'Wk': jax.random.normal(ks[3], (Ckv, Cq), jnp.float32) * s_kv, 'bk': jnp.zeros((Cq,), jnp.float32), 'Wv': jax.random.normal(ks[4], (Ckv, Cq), jnp.float32) * s_kv, 'bv': jnp.zeros((Cq,), jnp.float32), 'Wo': jax.random.normal(ks[5], (Cq, Cq), jnp.float32) * s_q, 'bo': jnp.zeros((Cq,), jnp.float32)}
    _L0_xattn_all = _L0_xattn_setup()
    _L0_xattn_in = {k: v for k, v in _L0_xattn_all.items() if k in ('Wq', 'bq', 'Wk', 'bk', 'Wv', 'bv', 'Wo', 'bo')}
    del _L0_xattn_all

    def _L0_ffn_setup():
        import jax, jax.numpy as jnp
        import numpy as np
        BEST_K = 2

        def _expert(xf, w1, w3, w2):
            return jax.nn.silu(xf @ w1) * (xf @ w3) @ w2
        key = jax.random.key(seed)
        ks = jax.random.split(key, 9)
        E, S_sh, D, H = (8, 2, 128, 64)
        B, S = (2, 256)
        w = lambda k, shape: jax.random.normal(k, shape, dtype=jnp.float32) * 0.02
        return {'x': jax.random.normal(ks[0], (B, S, D), dtype=jnp.float32), 'router_w': w(ks[1], (D, E)), 'router_b': jnp.zeros((E,), dtype=jnp.float32), 'routed_w1': w(ks[2], (E, D, H)), 'routed_w3': w(ks[3], (E, D, H)), 'routed_w2': w(ks[4], (E, H, D)), 'shared_w1': w(ks[5], (S_sh, D, H)), 'shared_w3': w(ks[6], (S_sh, D, H)), 'shared_w2': w(ks[7], (S_sh, H, D))}
    _L0_ffn_all = _L0_ffn_setup()
    _L0_ffn_in = {k: v for k, v in _L0_ffn_all.items() if k in ('router_w', 'router_b', 'routed_w1', 'routed_w3', 'routed_w2', 'shared_w1', 'shared_w3', 'shared_w2')}
    del _L0_ffn_all

    def _L1_attn_setup():
        import jax, jax.numpy as jnp
        import numpy as np
        import math
        N_EMBD = 128
        N_HEAD = 16
        HEAD_DIM = N_EMBD // N_HEAD
        BLOCK_SIZE = 256
        ROPE_BASE = 10000.0
        B, T = (4, 256)

        def _rope_cache(n_pos):
            theta = 1.0 / ROPE_BASE ** (jnp.arange(0, HEAD_DIM, 2, dtype=jnp.float32) / HEAD_DIM)
            idx_theta = jnp.arange(n_pos, dtype=jnp.float32)[:, None] * theta[None, :]
            return (jnp.cos(idx_theta), jnp.sin(idx_theta))

        def _apply_rope(x):
            cos, sin = _rope_cache(x.shape[1])
            cos = cos[None, :, None, :]
            sin = sin[None, :, None, :]
            xs = x.reshape(*x.shape[:-1], HEAD_DIM // 2, 2)
            x0, x1 = (xs[..., 0], xs[..., 1])
            out = jnp.stack([x0 * cos - x1 * sin, x1 * cos + x0 * sin], axis=-1)
            return out.reshape(x.shape)
        key = jax.random.key(seed)
        ks = jax.random.split(key, 5)
        x = jax.random.normal(ks[0], (B, T, N_EMBD), dtype=jnp.float32)
        s1 = 1.0 / math.sqrt(N_EMBD)
        W_attn = jax.random.uniform(ks[1], (N_EMBD, 3 * N_EMBD), jnp.float32, -s1, s1)
        b_attn = jax.random.uniform(ks[2], (3 * N_EMBD,), jnp.float32, -s1, s1)
        W_proj = jax.random.uniform(ks[3], (N_EMBD, N_EMBD), jnp.float32, -s1, s1)
        b_proj = jax.random.uniform(ks[4], (N_EMBD,), jnp.float32, -s1, s1)
        return {'x': x, 'W_attn': W_attn, 'b_attn': b_attn, 'W_proj': W_proj, 'b_proj': b_proj}
    _L1_attn_all = _L1_attn_setup()
    _L1_attn_in = {k: v for k, v in _L1_attn_all.items() if k in ('W_attn', 'b_attn', 'W_proj', 'b_proj')}
    del _L1_attn_all

    def _L1_xattn_setup():
        import jax, jax.numpy as jnp
        import numpy as np
        DIM_IN, DIM_LAT, DIM_HEAD = (96, 128, 64)
        INNER = max(DIM_LAT, DIM_IN)
        HEADS = INNER // DIM_HEAD
        SCALE = DIM_HEAD ** (-0.5)
        RMS_EPS = 1e-08
        LN_EPS = 1e-05

        def layernorm(x, g, b):
            mu = jnp.mean(x, axis=-1, keepdims=True)
            var = jnp.mean((x - mu) ** 2, axis=-1, keepdims=True)
            return (x - mu) * jax.lax.rsqrt(var + LN_EPS) * g + b

        def rmsnorm(x, gamma):
            norm = jnp.sqrt(jnp.sum(x * x, axis=-1, keepdims=True)) * x.shape[-1] ** (-0.5)
            return x / jnp.maximum(norm, RMS_EPS) * gamma
        key = jax.random.key(seed)
        ks = jax.random.split(key, 12)
        b, n, m = (4, 512, 64)
        x = jax.random.normal(ks[0], (b, n, DIM_IN), jnp.float32)
        latents = jax.random.normal(ks[1], (b, m, DIM_LAT), jnp.float32)
        mask = jax.random.randint(ks[2], (b, n), 0, 2).astype(bool)
        s = lambda k, sh, fan: jax.random.normal(k, sh, jnp.float32) * fan ** (-0.5)
        return {'x': x, 'latents': latents, 'mask': mask, 'ln_x_g': jnp.ones((DIM_IN,), jnp.float32), 'ln_x_b': jnp.zeros((DIM_IN,), jnp.float32), 'ln_l_g': jnp.ones((DIM_LAT,), jnp.float32), 'ln_l_b': jnp.zeros((DIM_LAT,), jnp.float32), 'qn_g': jnp.ones((DIM_HEAD,), jnp.float32), 'kn_g': jnp.ones((DIM_HEAD,), jnp.float32), 'Wq': s(ks[3], (INNER, DIM_LAT), DIM_LAT), 'Wkv': s(ks[4], (2 * INNER, DIM_IN), DIM_IN), 'Wlkv': s(ks[5], (2 * INNER, DIM_LAT), DIM_LAT), 'Wo': s(ks[6], (DIM_LAT, INNER), INNER), 'bo': jnp.zeros((DIM_LAT,), jnp.float32)}
    _L1_xattn_all = _L1_xattn_setup()
    _L1_xattn_in = {k: v for k, v in _L1_xattn_all.items() if k in ('ln_x_g', 'ln_x_b', 'ln_l_g', 'ln_l_b', 'qn_g', 'kn_g', 'Wq', 'Wkv', 'Wlkv', 'Wo', 'bo')}
    del _L1_xattn_all

    def _L1_ffn_setup():
        import jax, jax.numpy as jnp
        import numpy as np
        H, F, E, TOPK = (128, 512, 8, 2)
        B, S = (4, 128)
        key = jax.random.key(seed)
        ks = jax.random.split(key, 7)
        s_h = 1.0 / np.sqrt(H)
        s_f = 1.0 / np.sqrt(F)
        return {'x': jax.random.normal(ks[0], (B, S, H), dtype=jnp.float32), 'router_w': jax.random.uniform(ks[1], (H, E), jnp.float32, -s_h, s_h), 'router_b': jax.random.uniform(ks[2], (E,), jnp.float32, -s_h, s_h), 'w1': jax.random.uniform(ks[3], (E, H, F), jnp.float32, -s_h, s_h), 'b1': jax.random.uniform(ks[4], (E, F), jnp.float32, -s_h, s_h), 'w2': jax.random.uniform(ks[5], (E, F, H), jnp.float32, -s_f, s_f), 'b2': jax.random.uniform(ks[6], (E, H), jnp.float32, -s_f, s_f)}
    _L1_ffn_all = _L1_ffn_setup()
    _L1_ffn_in = {k: v for k, v in _L1_ffn_all.items() if k in ('router_w', 'router_b', 'w1', 'b1', 'w2', 'b2')}
    del _L1_ffn_all
    return {'x': x, 'ctx_768': ctx_768, 'mask_BxS2_bk0': mask_BxS2_bk0, 'L0_attn_Wq': _L0_attn_in['Wq'], 'L0_attn_bq': _L0_attn_in['bq'], 'L0_attn_Wk': _L0_attn_in['Wk'], 'L0_attn_bk': _L0_attn_in['bk'], 'L0_attn_Wv': _L0_attn_in['Wv'], 'L0_attn_bv': _L0_attn_in['bv'], 'L0_attn_Wo': _L0_attn_in['Wo'], 'L0_attn_bo': _L0_attn_in['bo'], 'L0_xattn_Wq': _L0_xattn_in['Wq'], 'L0_xattn_bq': _L0_xattn_in['bq'], 'L0_xattn_Wk': _L0_xattn_in['Wk'], 'L0_xattn_bk': _L0_xattn_in['bk'], 'L0_xattn_Wv': _L0_xattn_in['Wv'], 'L0_xattn_bv': _L0_xattn_in['bv'], 'L0_xattn_Wo': _L0_xattn_in['Wo'], 'L0_xattn_bo': _L0_xattn_in['bo'], 'L0_ffn_router_w': _L0_ffn_in['router_w'], 'L0_ffn_router_b': _L0_ffn_in['router_b'], 'L0_ffn_routed_w1': _L0_ffn_in['routed_w1'], 'L0_ffn_routed_w3': _L0_ffn_in['routed_w3'], 'L0_ffn_routed_w2': _L0_ffn_in['routed_w2'], 'L0_ffn_shared_w1': _L0_ffn_in['shared_w1'], 'L0_ffn_shared_w3': _L0_ffn_in['shared_w3'], 'L0_ffn_shared_w2': _L0_ffn_in['shared_w2'], 'L1_attn_W_attn': _L1_attn_in['W_attn'], 'L1_attn_b_attn': _L1_attn_in['b_attn'], 'L1_attn_W_proj': _L1_attn_in['W_proj'], 'L1_attn_b_proj': _L1_attn_in['b_proj'], 'L1_xattn_ln_x_g': _L1_xattn_in['ln_x_g'], 'L1_xattn_ln_x_b': _L1_xattn_in['ln_x_b'], 'L1_xattn_ln_l_g': _L1_xattn_in['ln_l_g'], 'L1_xattn_ln_l_b': _L1_xattn_in['ln_l_b'], 'L1_xattn_qn_g': _L1_xattn_in['qn_g'], 'L1_xattn_kn_g': _L1_xattn_in['kn_g'], 'L1_xattn_Wq': _L1_xattn_in['Wq'], 'L1_xattn_Wkv': _L1_xattn_in['Wkv'], 'L1_xattn_Wlkv': _L1_xattn_in['Wlkv'], 'L1_xattn_Wo': _L1_xattn_in['Wo'], 'L1_xattn_bo': _L1_xattn_in['bo'], 'L1_ffn_router_w': _L1_ffn_in['router_w'], 'L1_ffn_router_b': _L1_ffn_in['router_b'], 'L1_ffn_w1': _L1_ffn_in['w1'], 'L1_ffn_b1': _L1_ffn_in['b1'], 'L1_ffn_w2': _L1_ffn_in['w2'], 'L1_ffn_b2': _L1_ffn_in['b2']}

def reference(x, ctx_768, mask_BxS2_bk0, L0_attn_Wq, L0_attn_bq, L0_attn_Wk, L0_attn_bk, L0_attn_Wv, L0_attn_bv, L0_attn_Wo, L0_attn_bo, L0_xattn_Wq, L0_xattn_bq, L0_xattn_Wk, L0_xattn_bk, L0_xattn_Wv, L0_xattn_bv, L0_xattn_Wo, L0_xattn_bo, L0_ffn_router_w, L0_ffn_router_b, L0_ffn_routed_w1, L0_ffn_routed_w3, L0_ffn_routed_w2, L0_ffn_shared_w1, L0_ffn_shared_w3, L0_ffn_shared_w2, L1_attn_W_attn, L1_attn_b_attn, L1_attn_W_proj, L1_attn_b_proj, L1_xattn_ln_x_g, L1_xattn_ln_x_b, L1_xattn_ln_l_g, L1_xattn_ln_l_b, L1_xattn_qn_g, L1_xattn_kn_g, L1_xattn_Wq, L1_xattn_Wkv, L1_xattn_Wlkv, L1_xattn_Wo, L1_xattn_bo, L1_ffn_router_w, L1_ffn_router_b, L1_ffn_w1, L1_ffn_b1, L1_ffn_w2, L1_ffn_b2):
    import jax
    import jax.numpy as jnp

    def _L0_attn_ref(x, Wq, bq, Wk, bk, Wv, bv, Wo, bo):
        import jax, jax.numpy as jnp
        import numpy as np
        D_MODEL = 128
        NHEAD = 16
        HEAD_DIM = D_MODEL // NHEAD

        def _rope(x, sin, cos):
            half = x.shape[-1] // 2
            x1, x2 = (x[..., :half], x[..., half:])
            rotated = jnp.concatenate([-x2, x1], axis=-1)
            return x * cos + rotated * sin
        B, L, D = x.shape
        H, Dh = (NHEAD, HEAD_DIM)
        q = (x @ Wq.T + bq).reshape(B, L, H, Dh)
        k = (x @ Wk.T + bk).reshape(B, L, H, Dh)
        v = (x @ Wv.T + bv).reshape(B, L, H, Dh)
        inv_freq = 1.0 / 10000.0 ** (jnp.arange(0, Dh, 2, dtype=jnp.float32) / Dh)
        t = jnp.arange(L, dtype=jnp.float32)
        freqs = jnp.einsum('i,j->ij', t, inv_freq)
        emb = jnp.concatenate([freqs, freqs], axis=-1)
        cos = jnp.cos(emb)[None, :, None, :]
        sin = jnp.sin(emb)[None, :, None, :]
        q = _rope(q, sin, cos)
        k = _rope(k, sin, cos)
        scores = jnp.einsum('bqhd,bkhd->bhqk', q, k) / jnp.sqrt(jnp.float32(Dh))
        attn = jax.nn.softmax(scores, axis=-1)
        out = jnp.einsum('bhqk,bkhd->bqhd', attn, v).reshape(B, L, D)
        return out @ Wo.T + bo

    def _L0_xattn_ref(query, key_value, Wq, bq, Wk, bk, Wv, bv, Wo, bo):
        import jax, jax.numpy as jnp
        import numpy as np
        NUM_HEADS = 16
        CLAMP = 10000.0
        B, Nq, Cq = query.shape
        Nkv = key_value.shape[1]
        H = NUM_HEADS
        D = Cq // H
        scale = D ** (-0.5)
        q = (query @ Wq + bq).reshape(B, Nq, H, D).transpose(0, 2, 1, 3)
        k = (key_value @ Wk + bk).reshape(B, Nkv, H, D).transpose(0, 2, 1, 3)
        v = (key_value @ Wv + bv).reshape(B, Nkv, H, D).transpose(0, 2, 1, 3)
        attn = jnp.einsum('bhqd,bhkd->bhqk', q, k) * scale
        attn = jnp.clip(attn, -CLAMP, CLAMP)
        attn = jax.nn.softmax(attn, axis=-1)
        attn = jnp.where(jnp.any(jnp.isnan(attn)), jnp.asarray(1.0 / Nkv, attn.dtype), attn)
        x = jnp.einsum('bhqk,bhkd->bqhd', attn, v).reshape(B, Nq, Cq)
        return x @ Wo + bo

    def _L0_ffn_ref(x, router_w, router_b, routed_w1, routed_w3, routed_w2, shared_w1, shared_w3, shared_w2):
        import jax, jax.numpy as jnp
        import numpy as np
        BEST_K = 2

        def _expert(xf, w1, w3, w2):
            return jax.nn.silu(xf @ w1) * (xf @ w3) @ w2
        B, S, D = x.shape
        T = B * S
        xf = x.reshape(T, D)
        logits = xf @ router_w + router_b
        topk_vals, topk_idx = jax.lax.top_k(logits, BEST_K)
        sparse = jnp.full_like(logits, -jnp.inf)
        sparse = sparse.at[jnp.arange(T)[:, None], topk_idx].set(topk_vals)
        gates = jax.nn.softmax(sparse, axis=-1)
        routed = jax.vmap(_expert, in_axes=(None, 0, 0, 0))(xf, routed_w1, routed_w3, routed_w2)
        routed_out = jnp.einsum('etd,te->td', routed, gates)
        shared_out = jax.vmap(_expert, in_axes=(None, 0, 0, 0))(xf, shared_w1, shared_w3, shared_w2).sum(axis=0)
        return (routed_out + shared_out).reshape(B, S, D)

    def _L1_attn_ref(x, W_attn, b_attn, W_proj, b_proj):
        import jax, jax.numpy as jnp
        import numpy as np
        import math
        N_EMBD = 128
        N_HEAD = 16
        HEAD_DIM = N_EMBD // N_HEAD
        BLOCK_SIZE = 256
        ROPE_BASE = 10000.0
        B, T = (4, 256)

        def _rope_cache(n_pos):
            theta = 1.0 / ROPE_BASE ** (jnp.arange(0, HEAD_DIM, 2, dtype=jnp.float32) / HEAD_DIM)
            idx_theta = jnp.arange(n_pos, dtype=jnp.float32)[:, None] * theta[None, :]
            return (jnp.cos(idx_theta), jnp.sin(idx_theta))

        def _apply_rope(x):
            cos, sin = _rope_cache(x.shape[1])
            cos = cos[None, :, None, :]
            sin = sin[None, :, None, :]
            xs = x.reshape(*x.shape[:-1], HEAD_DIM // 2, 2)
            x0, x1 = (xs[..., 0], xs[..., 1])
            out = jnp.stack([x0 * cos - x1 * sin, x1 * cos + x0 * sin], axis=-1)
            return out.reshape(x.shape)
        Bx, Tx, C = x.shape
        qkv = jnp.einsum('btc,cd->btd', x, W_attn) + b_attn
        q, k, v = jnp.split(qkv, 3, axis=2)
        q = q.reshape(Bx, Tx, N_HEAD, HEAD_DIM).transpose(0, 2, 1, 3)
        k = k.reshape(Bx, Tx, N_HEAD, HEAD_DIM).transpose(0, 2, 1, 3)
        v = v.reshape(Bx, Tx, N_HEAD, HEAD_DIM).transpose(0, 2, 1, 3)
        q = _apply_rope(q)
        k = _apply_rope(k)
        scale = 1.0 / math.sqrt(HEAD_DIM)
        att = jnp.einsum('bhqd,bhkd->bhqk', q, k) * scale
        causal = jnp.tril(jnp.ones((Tx, Tx), dtype=bool))
        att = jnp.where(causal[None, None], att, -jnp.inf)
        att = jax.nn.softmax(att, axis=-1)
        y = jnp.einsum('bhqk,bhkd->bhqd', att, v)
        y = y.transpose(0, 2, 1, 3).reshape(Bx, Tx, C)
        return jnp.einsum('btc,cd->btd', y, W_proj) + b_proj

    def _L1_xattn_ref(x, latents, mask, ln_x_g, ln_x_b, ln_l_g, ln_l_b, qn_g, kn_g, Wq, Wkv, Wlkv, Wo, bo):
        import jax, jax.numpy as jnp
        import numpy as np
        DIM_IN, DIM_LAT, DIM_HEAD = (96, 128, 64)
        INNER = max(DIM_LAT, DIM_IN)
        HEADS = INNER // DIM_HEAD
        SCALE = DIM_HEAD ** (-0.5)
        RMS_EPS = 1e-08
        LN_EPS = 1e-05

        def layernorm(x, g, b):
            mu = jnp.mean(x, axis=-1, keepdims=True)
            var = jnp.mean((x - mu) ** 2, axis=-1, keepdims=True)
            return (x - mu) * jax.lax.rsqrt(var + LN_EPS) * g + b

        def rmsnorm(x, gamma):
            norm = jnp.sqrt(jnp.sum(x * x, axis=-1, keepdims=True)) * x.shape[-1] ** (-0.5)
            return x / jnp.maximum(norm, RMS_EPS) * gamma
        b, n, _ = x.shape
        m = latents.shape[1]
        xn = layernorm(x, ln_x_g, ln_x_b)
        ln = layernorm(latents, ln_l_g, ln_l_b)
        q = ln @ Wq.T
        kv = jnp.concatenate([xn @ Wkv.T, ln @ Wlkv.T], axis=1)
        k, v = (kv[..., :INNER], kv[..., INNER:])
        split_heads = lambda t: t.reshape(t.shape[0], t.shape[1], HEADS, DIM_HEAD).transpose(0, 2, 1, 3)
        q, k, v = (split_heads(q), split_heads(k), split_heads(v))
        qn = rmsnorm(q, qn_g) * SCALE
        kn = rmsnorm(k, kn_g)
        attn = jnp.einsum('bhid,bhjd->bhij', qn, kn)
        full_mask = jnp.pad(mask, ((0, 0), (0, m)), constant_values=True)
        attn = jnp.where(full_mask[:, None, None, :], attn, -jnp.finfo(attn.dtype).max)
        attn = jax.nn.softmax(attn, axis=-1)
        out = jnp.einsum('bhij,bhjd->bhid', attn, v)
        out = out.transpose(0, 2, 1, 3).reshape(b, m, INNER)
        return out @ Wo.T + bo

    def _L1_ffn_ref(x, router_w, router_b, w1, b1, w2, b2):
        import jax, jax.numpy as jnp
        import numpy as np
        H, F, E, TOPK = (128, 512, 8, 2)
        B, S = (4, 128)
        bsz, seq, hid = x.shape
        xf = x.reshape(-1, hid)
        T = xf.shape[0]
        logits = xf @ router_w + router_b
        probs = jax.nn.softmax(logits, axis=-1)
        topk_w, topk_i = jax.lax.top_k(probs, TOPK)
        topk_w = topk_w / jnp.sum(topk_w, axis=-1, keepdims=True)
        gates = jnp.zeros((T, E), dtype=x.dtype)
        gates = gates.at[jnp.arange(T)[:, None], topk_i].set(topk_w)
        h = jax.nn.relu(jnp.einsum('th,ehf->tef', xf, w1) + b1)
        y = jnp.einsum('tef,efh->teh', h, w2) + b2
        out = jnp.einsum('te,teh->th', gates, y)
        return out.reshape(bsz, seq, hid)
    x = x + _L0_attn_ref(_layernorm(x, axis=-1), L0_attn_Wq, L0_attn_bq, L0_attn_Wk, L0_attn_bk, L0_attn_Wv, L0_attn_bv, L0_attn_Wo, L0_attn_bo)
    x = x + _L0_xattn_ref(_layernorm(x, axis=-1), ctx_768, L0_xattn_Wq, L0_xattn_bq, L0_xattn_Wk, L0_xattn_bk, L0_xattn_Wv, L0_xattn_bv, L0_xattn_Wo, L0_xattn_bo)
    x = x + _L0_ffn_ref(_layernorm(x, axis=-1), L0_ffn_router_w, L0_ffn_router_b, L0_ffn_routed_w1, L0_ffn_routed_w3, L0_ffn_routed_w2, L0_ffn_shared_w1, L0_ffn_shared_w3, L0_ffn_shared_w2)
    x = x + _L1_attn_ref(_layernorm(x, axis=-1), L1_attn_W_attn, L1_attn_b_attn, L1_attn_W_proj, L1_attn_b_proj)
    x = x + _L1_xattn_ref(ctx_768, _layernorm(x, axis=-1), mask_BxS2_bk0, L1_xattn_ln_x_g, L1_xattn_ln_x_b, L1_xattn_ln_l_g, L1_xattn_ln_l_b, L1_xattn_qn_g, L1_xattn_kn_g, L1_xattn_Wq, L1_xattn_Wkv, L1_xattn_Wlkv, L1_xattn_Wo, L1_xattn_bo)
    x = x + _L1_ffn_ref(_layernorm(x, axis=-1), L1_ffn_router_w, L1_ffn_router_b, L1_ffn_w1, L1_ffn_b1, L1_ffn_w2, L1_ffn_b2)
    return x

_drawn_inputs = setup_inputs


def setup_inputs(seed=0):
    import zlib

    import numpy as np

    out = dict(_drawn_inputs(seed))
    spreads = {'L0_attn_bq': (0.0, 0.8),
     'L0_attn_bk': (0.0, 0.8),
     'L0_attn_bv': (0.0, 0.297),
     'L0_attn_bo': (0.0, 0.1),
     'L0_xattn_bq': (0.0, 0.1),
     'L0_xattn_bk': (0.0, 2.0),
     'L0_xattn_bv': (0.0, 0.1),
     'L0_xattn_bo': (0.0, 0.1),
     'L0_ffn_router_b': (0.0, 0.8),
     'L1_xattn_ln_x_g': (1.0, 0.6),
     'L1_xattn_ln_x_b': (0.0, 1.214),
     'L1_xattn_ln_l_g': (1.0, 0.574),
     'L1_xattn_ln_l_b': (0.0, 0.269),
     'L1_xattn_qn_g': (1.0, 0.6),
     'L1_xattn_kn_g': (1.0, 0.6),
     'L1_xattn_bo': (0.0, 0.1)}
    factors = {'L0_attn_Wq': 8.0,
     'L0_attn_Wk': 8.0,
     'L0_attn_Wv': 7.001,
     'L0_ffn_router_w': 8.0,
     'L0_ffn_routed_w1': 8.0,
     'L0_ffn_routed_w3': 8.0,
     'L0_ffn_routed_w2': 8.0,
     'L0_ffn_shared_w1': 6.167,
     'L0_ffn_shared_w3': 6.475,
     'L0_ffn_shared_w2': 6.785,
     'L1_ffn_b1': 12.74,
     'L1_ffn_b2': 3.836,
     'L1_attn_b_attn': 4.957,
     'L1_attn_b_proj': 3.069,
     'L1_ffn_router_b': 3.775}
    for name, (base, spread) in spreads.items():
        noise = np.random.default_rng([zlib.crc32(name.encode()), seed]).standard_normal(out[name].shape)
        drawn = base * np.exp(spread * noise) if base else spread * noise
        out[name] = jnp.asarray(drawn.astype(out[name].dtype))
    for name, factor in factors.items():
        out[name] = (out[name] * factor).astype(out[name].dtype)
    return out
```

```python
from contextlib import ExitStack

import numpy as np

import concourse.bass as bass
from concourse import mybir

F32, F32R, U8 = mybir.dt.float32, mybir.dt.float32r, mybir.dt.uint8
ACT, ALU, AX = mybir.ActivationFunctionType, mybir.AluOpType, mybir.AxisListType

P = 128
B, D, DC = 32, 128, 96
H, DH = 16, 8
GB = 4
NG = B // GB
GT = GB * P
E0 = 8
W_FFN0 = 3 * (E0 // 2 + 1) * P + E0
U = 4
VW = 64
LN_EPS = 1e-5
RMS_EPS = 1e-8
CLAMP = 1e4
MASKED = -1e30

E1, F1 = 8, 512
C1 = F1 // P
W_LATENT = 6 * P
W_FFN1 = (2 * E1 * C1 + 1) * P + E1

AW = ["q", "q2", "k", "k2", "v", "o"]
ATT = {"self": 0, "cross": 1, "causal": 2}
N_WEIGHTS = 3 * len(AW) * P
COL_LATENT = 3 * 4
N_COLS = COL_LATENT + 6 + E1 * C1
R_ROUTER0 = 3 * 2 * P
R_ROUTER1 = R_ROUTER0 + E0
R_LATENT = R_ROUTER1 + E1
N_ROWS = R_LATENT + P

C_ID, C_ONES, C_MASK = 0, P, 5 * P
C_PAIR = C_MASK + 2 * P
C_ONE_ROW = C_PAIR + (E0 // 2) * P
N_CONST_R = C_ONE_ROW + E1 * P
C_DIAG = N_CONST_R
C_SLOT = C_DIAG + 4
C_ROPE = C_SLOT + 4
C_TURN = C_ROPE + 2 * P
C_TURN_COL = C_TURN + 2 * P
C_EARLIER = C_TURN_COL + 2
C_HEAD = C_EARLIER + E0 * E0
N_CONST = C_HEAD + 2


PHASE_SEMS = 48


def phase_semaphores(nc, ctx, phase, kind):
    numbers = sorted(nc.free_semaphores)[-2 * PHASE_SEMS:]
    own, other = (numbers[i * PHASE_SEMS:(i + 1) * PHASE_SEMS] for i in (phase % 2, 1 - phase % 2))
    free = iter(own)

    def sem(name):
        return ctx.enter_context(nc.semaphore(f"{kind}_{name}", num=next(free)))

    return sem, range(other[0], other[-1] + 1)


def batch_columns(tile, it, n):
    return tile[:, bass.ds(it * (8 * P) + n * P, P)]


def load_setup(nc, x, weights, cols, rows, consts, later, sb, sem, ready):
    with ExitStack() as ctx:
        staged = ctx.enter_context(nc.sbuf_tensor("staged_consts", [P, N_CONST_R], F32))
        staged_w = ctx.enter_context(nc.sbuf_tensor("staged_weights", [P, N_WEIGHTS], F32))
        staged_rows = ctx.enter_context(nc.sbuf_tensor("staged_rows", [P, N_ROWS], F32))
        block = ctx.enter_context(nc.Block())
        consts_in, weights_in, rows_in, x_in = sem("consts_in"), sem("weights_in"), sem("rows_in"), sem("x_in")
        split, values_zero = sem("weights_hi_done"), sem("values_zero")
        turned = sem("weights_turned")

        @block.sync
        def _(sp):
            sp.dma_start(staged[:, :], consts[:, 0:N_CONST_R]).then_inc(consts_in, 16)
            sp.dma_start(staged_w[:, :], weights).then_inc(weights_in, 16)
            sp.dma_start(sb["x"][:, :].rearrange("p (b d) -> p b d", d=D), x.rearrange("b p d -> p b d")).then_inc(x_in, 16)
            for name, tile, src in later:
                sp.dma_start(sb[tile][:, :], src).then_inc(ready[name], 16)
            sp.wait_ge(x_in, 16)

        @block.gpsimd
        def _(pool):
            pool.memset(sb["maxes"][:, :, :], 0.0)
            for z in sb["units"]:
                pool.memset(z[:, :, :].bitcast(F32), 0.0)
            for v in sb["v"]:
                pool.memset(v[:, :, :, :], 0.0).then_inc(values_zero, 1)
            pool.wait_ge(values_zero, 2)
            for v in sb["v"]:
                for j in range(U):
                    pool.memset(v[:, :, j:H:U, 32 + j], 1.0)

        @block.scalar
        def _(act):
            act.dma_start(sb["const"][:, :], consts[:, N_CONST_R:N_CONST]).then_inc(rows_in, 16)
            act.dma_start(sb["cols"][:, :], cols).then_inc(rows_in, 16)
            act.dma_start(staged_rows[:, :], rows).then_inc(rows_in, 16)
            act.dma_start(sb["rows"][:, :], rows).then_inc(rows_in, 16)
            act.wait_ge(consts_in, 16)
            act.activation(sb["const_r"][:, :], staged[:, :], ACT.Copy)
            act.activation(sb["ident"][:, :], staged[:, C_ID:C_ID + P], ACT.Copy)

        @block.vector
        def _(dve):
            dve.wait_ge(weights_in, 16)
            dve.wait_ge(rows_in, 64)
            table = lambda c, n: sb["const"][:, c - N_CONST_R:c - N_CONST_R + n]
            made = 0
            for name in "qk":
                c = (ATT["causal"] * len(AW) + AW.index(name)) * P
                w, partner = staged_w[:, c:c + P], staged_w[:, c + P:c + 2 * P]
                c = ATT["causal"] * 4 + AW.index(name)
                bias, partner_bias = sb["cols"][:, c:c + 1], sb["cols"][:, c + 1:c + 2]
                dve.tensor_tensor(w, w, table(C_TURN, P), ALU.mult).then_inc(turned, 1)
                dve.tensor_tensor(partner, partner, table(C_TURN + P, P), ALU.mult).then_inc(turned, 1)
                dve.tensor_tensor(bias, bias, table(C_TURN_COL, 1), ALU.mult).then_inc(turned, 1)
                dve.tensor_tensor(partner_bias, partner_bias, table(C_TURN_COL + 1, 1), ALU.mult).then_inc(turned, 1)
                made += 4
                dve.wait_ge(turned, made)
                dve.tensor_tensor(w, w, partner, ALU.add).then_inc(turned, 1)
                dve.tensor_tensor(bias, bias, partner_bias, ALU.add).then_inc(turned, 1)
                made += 2
            dve.wait_ge(turned, made)
            dve.tensor_copy(sb["w_hi"][:, :], staged_w[:, :]).then_inc(split, 1)
            dve.tensor_copy(sb["rows_hi"][:, :], staged_rows[:, :]).then_inc(split, 1)
            dve.wait_ge(split, 2)
            dve.tensor_tensor(sb["w_lo"][:, :], staged_w[:, :], sb["w_hi"][:, :].bitcast(F32), ALU.subtract)
            dve.tensor_tensor(sb["rows_lo"][:, :], staged_rows[:, :], sb["rows_hi"][:, :].bitcast(F32), ALU.subtract)


def attention(nc, phase, kind, sb, ps, context=None):
    rope, cross, causal = kind == "self", kind == "cross", kind == "causal"
    clip = cross
    a = ATT[kind]
    kc = DC if kind == "cross" else D
    scale = float(DH) ** -0.5
    pieces = ["q", "q2", "k", "k2", "v"] if rope else ["q", "k", "v"]
    NP = len(pieces)

    def weight(name, rows=P):
        c = (a * len(AW) + AW.index(name)) * P
        return sb["w_hi"][0:rows, c:c + P], sb["w_lo"][0:rows, c:c + P]

    def bias(name):
        c = a * 4 + AW.index(name)
        return sb["cols"][:, c:c + 1]

    cr = sb["const_r"]
    ident_r = cr[:, C_ID:C_ID + P]
    c_rope = C_ROPE - N_CONST_R
    cos, sin = sb["const"][:, c_rope:c_rope + P], sb["const"][:, c_rope + P:c_rope + 2 * P]
    diag, slots = sb["const"][:, 0:U], sb["const"][:, U:2 * U]
    bv = sb["rows"][:, 2 * a * P:(2 * a + 1) * P]
    bo_hi, bo_lo = (sb[r][:, (2 * a + 1) * P:(2 * a + 2) * P] for r in ("rows_hi", "rows_lo"))
    X = sb["x"]
    S, T, OT, PJ, O, TR = ps[0:2], ps[2:4], ps[4], ps[5], ps[6], ps[7]
    V, maxes = sb["v"], sb["maxes"]
    unit_q, unit_k_hi, unit_k_lo = (sb["units"][4 * i:4 * i + 4] for i in range(3))

    tr_turn, pj_turn = {}, {}
    for n in range(-6, B + 2):
        G, b = n // GB, n % GB
        if b == 2 and G + 2 < NG:
            tr_turn["x", G + 2] = len(tr_turn)
        if cross and b == 3 and G + 2 < NG:
            tr_turn["c", G + 2] = len(tr_turn)
        if rope and b == 3 and G + 2 < NG:
            pj_turn["q2", G + 2] = len(pj_turn)
        if rope and b == 0 and 0 <= G + 1 < NG:
            pj_turn["k2", G + 1] = len(pj_turn)
        if n - 2 >= 0:
            pj_turn["y", n - 2] = len(pj_turn)
        if 0 <= n - 1 < B:
            tr_turn["o", n - 1] = len(tr_turn)
        if b == 2 and G + 2 < NG:
            pj_turn["q", G + 2] = len(pj_turn)
        if b == 3 and G + 2 < NG:
            pj_turn["k", G + 2] = len(pj_turn)
        if b == 0 and 0 <= G + 1 < NG:
            pj_turn["v", G + 1] = len(pj_turn)
        if 0 <= n + 1 < B:
            tr_turn["m", n + 1] = len(tr_turn)
    TR8, PJ8 = 16 + (4 if cross else 2), 8 + 2 * NP

    with ExitStack() as ctx:
        def buf(name, shape, dt=F32):
            return ctx.enter_context(nc.sbuf_tensor(f"{kind}_{name}", shape, dt))

        sem, used_before = phase_semaphores(nc, ctx, phase, kind)
        stats, mean_var = buf("stats", [P, GB, 6]), buf("mean_var", [P, GB, 2])
        var_eps, rstd, power = buf("var_eps", [P, GB]), buf("rstd", [P, GB]), buf("power", [P, GB])
        xn = buf("xn", [P, GB, D])
        x_hi, x_lo = buf("x_hi", [P, GT], F32R), buf("x_lo", [P, GT], F32R)
        if cross:
            ctx_in = buf("ctx_in", [P, GB, DC])
            c_hi, c_lo = buf("c_hi", [DC, GT], F32R), buf("c_lo", [DC, GT], F32R)
        else:
            c_hi, c_lo = x_hi, x_lo
        if rope:
            by_cos = [buf(f"by_cos{i}", [P, GB, P]) for i in range(2)]
            by_sin = [buf(f"by_sin{i}", [P, GB, P]) for i in range(2)]
            turned = [buf(f"turned{i}", [P, GT]) for i in range(2)]
        qk_hi = [[buf(f"qk_hi{i}{j}", [P, GT], F32R) for j in range(2)] for i in range(2)]
        qk_lo = [[buf(f"qk_lo{i}{j}", [P, GT], F32R) for j in range(2)] for i in range(2)]
        q_hi_m = [buf(f"q_hi_m{j}", [P, U, P], F32R) for j in range(2)]
        q_lo_m = [buf(f"q_lo_m{j}", [P, U, P], F32R) for j in range(2)]
        k_hi_m = [buf(f"k_hi_m{j}", [P, U, P], F32R) for j in range(2)]
        sums = buf("sums", [P, 2 * P])
        neg_max = [buf(f"neg_max{j}", [P, U, P], F32R) for j in range(2)]
        probs = [buf(f"probs{j}", [P, U, U, P]) for j in range(2)]
        recip = [buf(f"recip{j}", [P, U, U]) for j in range(2)]
        heads = [buf(f"heads{j}", [P, U, U, DH]) for j in range(2)]
        o_hi = [buf(f"o_hi{j}", [P, P], F32R) for j in range(2)]
        o_lo = [buf(f"o_lo{j}", [P, P], F32R) for j in range(2)]

        x_transposed, c_transposed = sem("x_transposed"), sem("c_transposed")
        projected = sem("projected")
        sums_transposed = sem("sums_transposed")
        scored = sem("scored")
        keyed = sem("keyed")
        shifted = sem("shifted")
        max_transposed = sem("max_transposed")
        weighted = sem("weighted")
        o_transposed = sem("o_transposed")
        out_projected = sem("out_projected")
        x_hi_done, c_hi_done = sem("x_hi_done"), sem("c_hi_done")
        qk_hi_done = sem("qk_hi_done")
        sums_done = sem("sums_done")
        exp_done = sem("exp_done")
        o_hi_done = sem("o_hi_done")
        stats_done, mean_done, xn_done = sem("stats_done"), sem("mean_done"), sem("xn_done")
        tr_read, pj_read = sem("tr_read"), sem("pj_read")
        max_done, max_clipped = sem("max_done"), sem("max_clipped")
        clipped = sem("clipped")
        recip_done, heads_done = sem("recip_done"), sem("heads_done")
        power_done, var_done, rstd_done = sem("power_done"), sem("var_done"), sem("rstd_done")
        turned_done, qk_lo_done = sem("turned_done"), sem("qk_lo_done")
        k_masked, q_masked = sem("k_masked"), sem("q_masked")
        spread_done = sem("spread_done")
        ctx_loaded = sem("ctx_loaded")
        passed = sem("passed")

        block = ctx.enter_context(nc.Block())

        def run(engine, slot):
            for n in range(-6, 2):
                slot(0, n)
            with engine.Fori(0, 3) as it:
                for n in range(2, 10):
                    slot(it, n)
            for n in range(26, B + 2):
                slot(0, n)

        def there(it, n):
            return not isinstance(it, int) or 0 <= n < B

        def group(it, G):
            return not isinstance(it, int) or 0 <= G < NG

        @block.tensor
        def _(pe):
            def split_matmul(out, l, r, start=True, stop=True):
                pe.matmul(out, l[0], r[0], start=start, stop=False)
                pe.matmul(out, l[0], r[1], start=False, stop=False)
                return pe.matmul(out, l[1], r[0], start=False, stop=stop)

            def scores(it, n, u):
                if u == 0:
                    pe.wait_ge(k_masked, it * 8 + (n + 1))
                    pe.wait_ge(spread_done, it * 96 + (12 * (n + 1)))
                if 4 * n + u - 1 > 0:
                    pe.wait_ge(max_done, it * 32 + (4 * n + u - 1))
                mm = pe.matmul(S[u % 2][:, :].rearrange("p (j k) -> p j k", j=U), unit_q[n % 4][:, u, :],
                               k_hi_m[n % 2][:, :, :], start=True, stop=not causal)
                if causal:
                    mm = pe.matmul(S[u % 2][:, :].rearrange("p (j k) -> p j k", j=U), ident_r,
                                   cr[:, C_MASK:C_MASK + P].unsqueeze(1).broadcast_to([P, U, P]),
                                   start=False, stop=True)
                mm.then_inc(scored, 1)

            def key_scores(it, n, u):
                if u == 0:
                    pe.wait_ge(q_masked, it * 16 + (2 * n + 2))
                if 4 * n + u - 1 > 0:
                    pe.wait_ge(exp_done, it * 32 + (4 * n + u - 1))
                k_hi, k_lo = unit_k_hi[n % 4][:, u, :], unit_k_lo[n % 4][:, u, :]
                out = T[u % 2][:, :].rearrange("p (j q) -> p j q", j=U)
                pe.matmul(out, k_hi, q_hi_m[n % 2][:, :, :], start=True, stop=False)
                pe.matmul(out, k_hi, q_lo_m[n % 2][:, :, :], start=False, stop=False)
                mm = pe.matmul(out, k_lo, q_hi_m[n % 2][:, :, :], start=False, stop=clip)
                if causal:
                    mm = pe.matmul(out, ident_r, cr[:, C_MASK + P:C_MASK + 2 * P].unsqueeze(1).broadcast_to([P, U, P]),
                                   start=False, stop=False)
                if clip:
                    mm.then_inc(keyed, 1)

            def shift(it, n, u):
                if u == 0:
                    pe.wait_ge(tr_read, it * TR8 + (tr_turn['m', n] + 1))
                if clip:
                    pe.wait_ge(clipped, it * 32 + (4 * n + u + 1))
                pe.matmul(T[u % 2][:, :], cr[:, C_ONES + u * P:C_ONES + (u + 1) * P],
                          neg_max[n % 2][:, :, :].rearrange("p j q -> p (j q)"),
                          start=False, stop=True, skip_group_check=clip).then_inc(shifted, 1)

            def weigh(it, n):
                pe.wait_ge(exp_done, it * 32 + (4 * n + 4))
                if n > 0:
                    pe.wait_ge(sums_done, it * 8 + n)
                pe.wait_ge(pj_read, it * PJ8 + (pj_turn['v', n // GB] + 1))
                for u in range(U):
                    out = O[VW * (u % 2):VW * (u % 2) + VW, (u // 2) * P:(u // 2 + 1) * P]
                    for j in range(U):
                        mm = pe.matmul(out, V[(n // GB) % 2][:, n % GB, U * u + j, :], probs[n % 2][:, u, j, :],
                                       start=j == 0, stop=j == U - 1)
                mm.then_inc(weighted, 1)

            def transpose_sums(it, n):
                pe.wait_ge(sums_done, it * 8 + (n + 1))
                if n > 0:
                    pe.wait_ge(heads_done, it * 8 + n)
                for c in range(2):
                    mm = pe.transpose(OT[:, c * P:(c + 1) * P], sums[:, c * P:(c + 1) * P], sb["ident"][:, :])
                mm.then_inc(sums_transposed, 1)

            def out_project(it, n):
                pe.wait_ge(pj_read, it * PJ8 + pj_turn['y', n])
                pe.wait_ge(tr_read, it * TR8 + (tr_turn['o', n] + 1))
                pe.matmul(PJ[:, 0:P], ident_r, bo_hi, start=True, stop=False)
                pe.matmul(PJ[:, 0:P], ident_r, bo_lo, start=False, stop=False)
                split_matmul(PJ[:, 0:P], (o_hi[n % 2][:, :], o_lo[n % 2][:, :]), weight("o"), start=False)\
                    .then_inc(out_projected, 1)

            def transpose_x(it, G):
                pe.wait_ge(xn_done, it * 8 + (4 * G + 4))
                if tr_turn['x', G] > 0:
                    pe.wait_ge(tr_read, it * TR8 + tr_turn['x', G])
                for b in range(GB):
                    mm = pe.transpose(TR[:, b * P:(b + 1) * P], xn[:, b, :], sb["ident"][:, :])
                mm.then_inc(x_transposed, 1)

            def transpose_c(it, G):
                pe.wait_ge(ctx_loaded, it * 32 + (16 * (G + 1)))
                pe.wait_ge(tr_read, it * TR8 + tr_turn['c', G])
                for b in range(GB):
                    mm = pe.transpose(TR[0:DC, b * P:(b + 1) * P], ctx_in[:, b, :], sb["ident"][:, :])
                mm.then_inc(c_transposed, 1)

            def project(it, G, name):
                if pj_turn[name, G] > 0:
                    pe.wait_ge(pj_read, it * PJ8 + pj_turn[name, G])
                src = "c" if cross and name != "q" else "x"
                pe.wait_ge(tr_read, it * TR8 + (tr_turn[src, G] + 1))
                hi, lo = (x_hi, x_lo) if src == "x" else (c_hi, c_lo)
                w = weight(name, P if src == "x" else DC)
                if name == "v":
                    for b in range(GB):
                        cols = slice(b * P, (b + 1) * P)
                        mm = split_matmul(PJ[:, cols], (hi[:, cols], lo[:, cols]), w)
                else:
                    mm = split_matmul(PJ[:, :], w, (hi[:, :], lo[:, :]))
                mm.then_inc(projected, 1)

            def slot(it, n):
                G, b = n // GB, n % GB
                now, nxt, old = there(it, n), there(it, n + 1), there(it, n - 1)
                if clip:
                    order = "k0 s0 k1 s1 f0 s2 f1 k2 s3 f2 w mid k3 t y f3"
                else:
                    order = "s0 s1 k0 f0 s2 k1 f1 s3 k2 f2 w mid t y k3 f3"
                for step in order.split():
                    if step[0] == "s" and nxt:
                        scores(it, n + 1, int(step[1]))
                    elif step[0] == "k" and now:
                        key_scores(it, n, int(step[1]))
                    elif step[0] == "f" and now:
                        shift(it, n, int(step[1]))
                    elif step == "w" and old:
                        weigh(it, n - 1)
                    elif step == "mid":
                        if b == 2 and group(it, G + 2):
                            transpose_x(it, G + 2)
                        if cross and b == 3 and group(it, G + 2):
                            transpose_c(it, G + 2)
                        if rope and b == 3 and group(it, G + 2):
                            project(it, G + 2, "q2")
                        if rope and b == 0 and group(it, G + 1):
                            project(it, G + 1, "k2")
                    elif step == "t" and old:
                        transpose_sums(it, n - 1)
                    elif step == "y" and there(it, n - 2):
                        out_project(it, n - 2)
                if old:
                    pe.wait_ge(heads_done, it * 8 + n)
                    pe.wait_ge(tr_read, it * TR8 + tr_turn['o', n - 1])
                    pe.transpose(TR[:, 0:P], heads[(n - 1) % 2][:, :, :, :].rearrange("p u j d -> p (u j d)"),
                                 sb["ident"][:, :]).then_inc(o_transposed, 1)
                if b == 2 and group(it, G + 2):
                    project(it, G + 2, "q")
                if b == 3 and group(it, G + 2):
                    project(it, G + 2, "k")
                if b == 0 and group(it, G + 1):
                    project(it, G + 1, "v")
                if nxt:
                    pe.wait_ge(max_clipped if clip else max_done, it * (8 if clip else 32) + ((1 if clip else 4) * (n + 2)))
                    pe.wait_ge(tr_read, it * TR8 + tr_turn['m', n + 1])
                    pe.transpose(TR[:, 0:P], maxes[:, :, :].rearrange("p u c -> p (u c)"),
                                 sb["ident"][:, :]).then_inc(max_transposed, 1)

            run(pe, slot)

        @block.scalar
        def _(act):
            def exps(it, n, u):
                act.wait_ge(shifted, it * 32 + (4 * n + u + 1))
                if u == 0:
                    if n - 1 > 0:
                        act.wait_ge(weighted, it * 8 + (n - 1))
                act.activation(probs[n % 2][:, u, :, :].rearrange("p g q -> p (g q)"), T[u % 2][:, :],
                               ACT.Exp, scale=scale).then_inc(exp_done, 1)

            def spread(it, n):
                G = n // GB
                cols = slice((n % GB) * P, (n % GB + 1) * P)
                if not rope:
                    act.wait_ge(pj_read, it * PJ8 + (pj_turn['k', G] + 1))
                else:
                    act.wait_ge(qk_lo_done, it * 4 + (2 * G + 2))
                act.wait_ge(qk_hi_done, it * 4 + (2 * G + 2))
                for src, out in ((qk_hi[0], unit_q), (qk_hi[1], unit_k_hi), (qk_lo[1], unit_k_lo)):
                    for u in range(U):
                        rows = slice(32 * u, 32 * u + 32)
                        act.activation(out[n % 4][rows, u, :], src[G % 2][rows, cols].bitcast(F32), ACT.Copy)\
                            .then_inc(spread_done, 1)

            def copy_sums(it, n):
                act.wait_ge(weighted, it * 8 + (n + 1))
                if n > 0:
                    act.wait_ge(sums_transposed, it * 8 + n)
                act.activation(sums[:, :], O[:, 0:2 * P], ACT.Copy).then_inc(sums_done, 1)

            def hi_of(it, G, i):
                if rope:
                    act.wait_ge(turned_done, it * 4 + (2 * G + i + 1))
                    act.activation(qk_hi[i][G % 2][:, :], turned[i][:, :], ACT.Copy).then_inc(qk_hi_done, 1)
                else:
                    act.wait_ge(projected, it * (2 * NP) + (NP * G + i + 1))
                    act.activation(qk_hi[i][G % 2][:, :], PJ[:, :], ACT.Identity,
                                   bias=bias("qk"[i])).then_inc(qk_hi_done, 1)

            def slot(it, n):
                G, b = n // GB, n % GB
                if there(it, n):
                    for u in range(3):
                        exps(it, n, u)
                if there(it, n - 1):
                    copy_sums(it, n - 1)
                if b == 2 and group(it, G + 2):
                    act.wait_ge(x_transposed, it * 2 + (G + 3))
                    act.activation(x_hi[:, :], TR[:, :], ACT.Copy).then_inc(x_hi_done, 1)
                if cross and b == 3 and group(it, G + 2):
                    act.wait_ge(c_transposed, it * 2 + (G + 3))
                    act.activation(c_hi[:, :], TR[0:DC, :], ACT.Copy).then_inc(c_hi_done, 1)
                if there(it, n + 2):
                    spread(it, n + 2)
                if there(it, n):
                    exps(it, n, 3)
                if there(it, n - 1):
                    act.wait_ge(o_transposed, it * 8 + n)
                    act.activation(o_hi[(n - 1) % 2][:, :], TR[:, 0:P], ACT.Copy).then_inc(o_hi_done, 1)
                if b == (3 if rope else 2) and group(it, G + 2):
                    hi_of(it, G + 2, 0)
                if rope and b == 0 and group(it, G + 1):
                    hi_of(it, G + 1, 1)
                if not rope and b == 3 and group(it, G + 2):
                    hi_of(it, G + 2, 1)

            run(act, slot)

        @block.vector
        def _(dve):
            def head_max(it, n, u):
                dve.wait_ge(scored, it * 32 + (4 * n + u + 1))
                if n - 1 >= 0 and u == 0:
                    dve.wait_ge(tr_read, it * TR8 + (tr_turn['m', n - 1] + 1))
                dve.tensor_reduce(maxes[:, u, 0:U], S[u % 2][:, :].rearrange("p (j k) -> p j k", k=P),
                                  AX.X, ALU.max, negate=True).then_inc(max_done, 1)

            def clip_scores(it, n, u):
                dve.wait_ge(keyed, it * 32 + (4 * n + u + 1))
                dve.tensor_scalar(T[u % 2][:, :], T[u % 2][:, :], CLAMP / scale, -CLAMP / scale,
                                  ALU.min, ALU.max).then_inc(clipped, 1)

            def normalise(it, n):
                dve.wait_ge(sums_transposed, it * 8 + (n + 1))
                if n > 0:
                    dve.wait_ge(heads_done, it * 8 + n)
                o = OT[:, 0:U * VW].rearrange("p (u c) -> p u c", c=VW)
                dve.reciprocal(recip[n % 2][:, :, :], o[:, :, 32:32 + U]).then_inc(recip_done, 1)
                dve.wait_ge(recip_done, it * 8 + (n + 1))
                dve.tensor_tensor(heads[n % 2][:, :, :, :],
                                  o[:, :, 0:32].rearrange("p u (j d) -> p u j d", j=U),
                                  recip[n % 2][:, :, :].unsqueeze(3).broadcast_to([P, U, U, DH]),
                                  ALU.mult).then_inc(heads_done, 1)

            def rotate(it, G, name):
                i, second = ("q", "k").index(name[0]), name.endswith("2")
                dve.wait_ge(projected, it * (2 * NP) + (NP * G + pieces.index(name) + 1))
                if 2 * (G - 1) + i + 1 > 0:
                    dve.wait_ge(turned_done, it * 4 + (2 * (G - 1) + i + 1))
                dst = (by_sin if second else by_cos)[i]
                dve.scalar_tensor_tensor(dst[:, :, :], PJ[:, :].rearrange("p (b t) -> p b t", t=P), bias(name),
                                         (sin if second else cos).unsqueeze(1).broadcast_to([P, GB, P]),
                                         ALU.add, ALU.mult).then_inc(pj_read, 1)

            def values(it, G):
                dve.wait_ge(projected, it * (2 * NP) + (NP * G + NP))
                for j in range(U):
                    at = lambda x: x.rearrange("p (u j d) -> p u j d", u=U, j=U)[:, :, j, :]
                    op = dve.tensor_tensor(V[G % 2][:, :, j:H:U, DH * j:DH * (j + 1)],
                                           PJ[:, :].rearrange("p (b u j d) -> p b u j d", b=GB, u=U, j=U)[:, :, :, j, :],
                                           at(bv).unsqueeze(1).broadcast_to([P, GB, U, DH]), ALU.add)
                op.then_inc(pj_read, 1)

            def lo_of(it, G, i):
                dve.wait_ge(qk_hi_done, it * 4 + (2 * G + i + 1))
                dve.scalar_tensor_tensor(qk_lo[i][G % 2][:, :], PJ[:, :], bias("qk"[i]),
                                         qk_hi[i][G % 2][:, :].bitcast(F32), ALU.add, ALU.subtract)\
                    .then_inc(pj_read, 1)

            def moments(it, G):
                if 4 * G > 0:
                    dve.wait_ge(xn_done, it * 8 + (4 * G))
                if 4 * G > 0:
                    dve.wait_ge(mean_done, it * 8 + (4 * G))
                if G > 0:
                    dve.wait_ge(rstd_done, it * 2 + G)
                for b in range(GB):
                    dve.bn_stats(stats[:, b, :], batch_columns(X, it, 4 * G + b)).then_inc(stats_done, 1)
                dve.wait_ge(stats_done, it * 8 + (4 * G + 4))
                dve.sem_inc(passed, 1)
                for b in range(GB):
                    dve.bn_aggr(mean_var[:, b, :], stats[:, b, :]).then_inc(mean_done, 1)

            def layernorm(it, G):
                dve.wait_ge(rstd_done, it * 2 + (G + 1))
                dve.wait_ge(mean_done, it * 8 + (4 * G + 4))
                if G > 0:
                    dve.wait_ge(x_hi_done, it * 2 + G)
                for b in range(GB):
                    dve.tensor_scalar(xn[:, b, :], batch_columns(X, it, 4 * G + b), mean_var[:, b, 0:1],
                                      rstd[:, b:b + 1], ALU.subtract, ALU.mult).then_inc(xn_done, 1)

            def slot(it, n):
                G, b = n // GB, n % GB
                now, nxt = there(it, n), there(it, n + 1)
                if b == 2 and group(it, G + 2):
                    moments(it, G + 2)
                for step in "c0 m0 ln c1 m1 m2 c2 m3".split():
                    if step[0] == "c" and clip and now:
                        clip_scores(it, n, int(step[1]))
                    elif step[0] == "m" and nxt:
                        head_max(it, n + 1, int(step[1]))
                    elif step == "ln" and b == 2 and group(it, G + 2):
                        layernorm(it, G + 2)
                if clip and nxt:
                    dve.wait_ge(max_done, it * 32 + (4 * (n + 2)))
                    dve.tensor_scalar(maxes[:, :, 0:U], maxes[:, :, 0:U], CLAMP / scale, -CLAMP / scale,
                                      ALU.min, ALU.max).then_inc(max_clipped, 1)
                if b == 2 and group(it, G + 2):
                    dve.wait_ge(x_hi_done, it * 2 + (G + 3))
                    dve.tensor_tensor(x_lo[:, :], TR[:, :], x_hi[:, :].bitcast(F32), ALU.subtract)\
                        .then_inc(tr_read, 1)
                if cross and b == 3 and group(it, G + 2):
                    dve.wait_ge(c_hi_done, it * 2 + (G + 3))
                    dve.tensor_tensor(c_lo[:, :], TR[0:DC, :], c_hi[:, :].bitcast(F32), ALU.subtract)\
                        .then_inc(tr_read, 1)
                if rope and b == 3 and group(it, G + 2):
                    rotate(it, G + 2, "q2")
                if rope and b == 0 and group(it, G + 1):
                    rotate(it, G + 1, "k2")
                if there(it, n - 1):
                    normalise(it, n - 1)
                if clip and now:
                    clip_scores(it, n, 3)
                if there(it, n - 2):
                    dve.wait_ge(out_projected, it * 8 + (n - 1))
                    dve.wait_ge(xn_done, it * 8 + (4 * ((n - 2) // GB) + 4))
                    x = batch_columns(X, it, n - 2)
                    dve.tensor_tensor(x, PJ[:, 0:P], x, ALU.add).then_inc(pj_read, 1)
                if there(it, n - 1):
                    dve.wait_ge(o_hi_done, it * 8 + n)
                    dve.tensor_tensor(o_lo[(n - 1) % 2][:, :], TR[:, 0:P], o_hi[(n - 1) % 2][:, :].bitcast(F32),
                                      ALU.subtract).then_inc(tr_read, 1)
                if b == 2 and group(it, G + 2):
                    rotate(it, G + 2, "q") if rope else lo_of(it, G + 2, 0)
                if b == 3 and group(it, G + 2):
                    rotate(it, G + 2, "k") if rope else lo_of(it, G + 2, 1)
                if b == 0 and group(it, G + 1):
                    values(it, G + 1)
                if nxt:
                    dve.wait_ge(max_transposed, it * 8 + (n + 2))
                    if 4 * (n + 1) - 4 > 0:
                        dve.wait_ge(shifted, it * 32 + (4 * (n + 1) - 4))
                    dve.tensor_tensor(neg_max[(n + 1) % 2][:, :, :],
                                      TR[:, 0:P].unsqueeze(1).broadcast_to([P, U, P]),
                                      diag.unsqueeze(2).broadcast_to([P, U, P]), ALU.mult).then_inc(tr_read, 1)

            run(dve, slot)

        @block.gpsimd
        def _(pool):
            def reciprocal_deviation(it, G):
                pool.wait_ge(mean_done, it * 8 + (4 * G + 4))
                if 4 * G > 0:
                    pool.wait_ge(xn_done, it * 8 + (4 * G))
                if G > 0:
                    pool.wait_ge(rstd_done, it * 2 + G)
                pool.sem_inc(passed, 1)
                pool.tensor_scalar(var_eps[:, :], mean_var[:, :, 1], LN_EPS, 1.0, ALU.add, ALU.mult)\
                    .then_inc(var_done, 1)
                pool.wait_ge(var_done, it * 2 + (G + 1))
                pool.tensor_tensor(rstd[:, :], var_eps[:, :], power[:, :], ALU.pow).then_inc(rstd_done, 1)

            def turn(it, G, i):
                name = ("q2", "k2")[i]
                pool.wait_ge(pj_read, it * PJ8 + (pj_turn[name, G] + 1))
                if 2 * (G - 1) + i + 1 > 0:
                    pool.wait_ge(qk_hi_done, it * 4 + (2 * (G - 1) + i + 1))
                if 2 * (G - 1) + i + 1 > 0:
                    pool.wait_ge(qk_lo_done, it * 4 + (2 * (G - 1) + i + 1))
                pool.tensor_tensor(turned[i][:, :], by_cos[i][:, :, :].rearrange("p b t -> p (b t)"),
                                   by_sin[i][:, :, :].rearrange("p b t -> p (b t)"), ALU.add)\
                    .then_inc(turned_done, 1)
                pool.wait_ge(qk_hi_done, it * 4 + (2 * G + i + 1))
                if 4 * (4 * G - 4) > 0:
                    pool.wait_ge(shifted, it * 32 + (4 * (4 * G - 4)))
                pool.tensor_tensor(qk_lo[i][G % 2][:, :], turned[i][:, :], qk_hi[i][G % 2][:, :].bitcast(F32),
                                   ALU.subtract).then_inc(qk_lo_done, 1)

            def mask(it, n, out, src, done):
                cols = slice((n % GB) * P, (n % GB + 1) * P)
                pool.tensor_tensor(out[n % 2][:, :, :],
                                   src[(n // GB) % 2][:, cols].bitcast(F32).unsqueeze(1).broadcast_to([P, U, P]),
                                   slots.unsqueeze(2).broadcast_to([P, U, P]), ALU.mult).then_inc(done, 1)

            def mask_all(it, n):
                G = n // GB
                pool.wait_ge(qk_hi_done, it * 4 + (2 * G + 2))
                if 4 * (n - 1) > 0:
                    pool.wait_ge(scored, it * 32 + (4 * (n - 1)))
                mask(it, n, k_hi_m, qk_hi[1], k_masked)
                if 4 * (n - 1) > 0:
                    pool.wait_ge(shifted, it * 32 + (4 * (n - 1)))
                mask(it, n, q_hi_m, qk_hi[0], q_masked)
                if rope:
                    pool.wait_ge(qk_lo_done, it * 4 + (2 * G + 2))
                else:
                    pool.wait_ge(pj_read, it * PJ8 + (pj_turn['k', G] + 1))
                mask(it, n, q_lo_m, qk_lo[0], q_masked)

            def slot(it, n):
                G, b = n // GB, n % GB
                if b == 2 and group(it, G + 2):
                    reciprocal_deviation(it, G + 2)
                if there(it, n + 2):
                    mask_all(it, n + 2)
                if rope and b == 3 and group(it, G + 2):
                    turn(it, G + 2, 0)
                if rope and b == 0 and group(it, G + 1):
                    turn(it, G + 1, 1)

            pool.sem_clear(used_before)
            pool.memset(power[:, :], -0.5).then_inc(power_done, 1)
            pool.wait_ge(power_done, 1)
            run(pool, slot)

        if cross:
            @block.sync
            def _(sp):
                sp.dma_start(ctx_in[:, :, :], context[0:GB, :, :].rearrange("b p d -> p b d")).then_inc(ctx_loaded, 16)
                with sp.Fori(1, NG) as G:
                    sp.wait_ge(c_transposed, G)
                    sp.dma_start(ctx_in[:, :, :],
                                 context[bass.ds(G * GB, GB), :, :].rearrange("b p d -> p b d"))\
                        .then_inc(ctx_loaded, 16)


def gated_experts(nc, phase, sb, ps, ready):
    NB = E0 // 2 + 1
    X = sb["x"]
    H1, H3, GATE, YT, TR, LG = ps[0:2], ps[2:4], ps[4], ps[5], ps[6], ps[7]
    cr = sb["const_r"]
    earlier = sb["const"][:, C_EARLIER - N_CONST_R:C_EARLIER - N_CONST_R + E0 * E0].rearrange("p (a b) -> p a b", b=E0)
    router_b = sb["rows"][:, R_ROUTER0:R_ROUTER0 + E0]

    with ExitStack() as ctx:
        def buf(name, shape, dt=F32):
            return ctx.enter_context(nc.sbuf_tensor(f"ffn0_{name}", shape, dt))

        sem, used_before = phase_semaphores(nc, ctx, phase, "ffn0")
        raw = sb["raw_ffn0"]
        w_hi, w_lo = buf("w_hi", [P, W_FFN0], F32R), buf("w_lo", [P, W_FFN0], F32R)
        stats, mean_var = buf("stats", [P, GB, 6]), buf("mean_var", [P, GB, 2])
        var_eps, rstd, power = buf("var_eps", [P, GB]), buf("rstd", [P, GB]), buf("power", [P, GB])
        xn = buf("xn", [P, GB, D])
        x_hi = [buf(f"x_hi{i}", [P, GT], F32R) for i in range(2)]
        x_lo = [buf(f"x_lo{i}", [P, GT], F32R) for i in range(2)]
        logits, shifted = buf("logits", [P, GB, E0]), buf("shifted", [P, GB, E0])
        top, exps = buf("top", [P, GB]), buf("exps", [P, GB, E0])
        above, equal = buf("above", [P, GB, E0, E0]), buf("equal", [P, GB, E0, E0])
        rank, chosen = buf("rank", [P, GB, E0]), buf("chosen", [P, GB, E0])
        total, recip, gates = buf("total", [P, GB]), buf("recip", [P, GB]), buf("gates", [P, GB, E0])
        g_hi = [buf(f"g_hi{i}", [E0, GT], F32R) for i in range(2)]
        g_lo = [buf(f"g_lo{i}", [E0, GT], F32R) for i in range(2)]
        silu = [buf(f"silu{i}", [P, GT]) for i in range(2)]
        product = [buf(f"product{i}", [P, GT]) for i in range(2)]
        hidden = [buf(f"hidden{i}", [P, GT]) for i in range(2)]
        h_hi = [buf(f"h_hi{i}", [P, GT], F32R) for i in range(2)]
        h_lo = [buf(f"h_lo{i}", [P, GT], F32R) for i in range(2)]
        y = buf("y", [P, GT])

        split, split_lo = sem("weights_hi_done"), sem("weights_lo_done")
        x_transposed, logits_made, g_transposed = sem("x_transposed"), sem("logits_made"), sem("g_transposed")
        h1_made, h3_made, gate_spread = sem("h1_made"), sem("h3_made"), sem("gate_spread")
        y_summed, y_back = sem("y_summed"), sem("y_back")
        x_hi_done, g_hi_done, exps_done = sem("x_hi_done"), sem("g_hi_done"), sem("exps_done")
        silu_done, h_hi_done, y_copied = sem("silu_done"), sem("h_hi_done"), sem("y_copied")
        stats_done, mean_done, xn_done = sem("stats_done"), sem("mean_done"), sem("xn_done")
        tr_read = sem("tr_read")
        routed = sem("routed")
        product_done, hidden_done = sem("product_done"), sem("hidden_done")
        power_done, var_done, rstd_done = sem("power_done"), sem("var_done"), sem("rstd_done")
        h_lo_done, passed = sem("h_lo_done"), sem("passed")
        product_summed = sem("product_summed")
        RS = 11

        turn = {}
        for n in range(-2, NG + 1):
            for name, G in (("x", n + 1), ("o", n - 1), ("g", n + 1)):
                if 0 <= G < NG:
                    turn[name, G] = len(turn)

        block = ctx.enter_context(nc.Block())

        def run(engine, slot):
            for n in range(-2, 2):
                slot(0, n)
            with engine.Fori(0, 2) as it:
                for n in range(2, 4):
                    slot(it, n)
            for n in range(6, NG + 1):
                slot(0, n)

        def there(it, G):
            return not isinstance(it, int) or 0 <= G < NG

        def group_columns(it, G):
            return X[:, bass.ds(it * (2 * GT) + G * GT, GT)]

        @block.tensor
        def _(pe):
            def split_matmul(out, l, r, start=True, stop=True):
                pe.matmul(out, l[0], r[0], start=start, stop=False)
                pe.matmul(out, l[0], r[1], start=False, stop=False)
                return pe.matmul(out, l[1], r[0], start=False, stop=stop)

            def weight(block, width=P):
                return w_hi[:, block * P:block * P + width], w_lo[:, block * P:block * P + width]

            def xs(n, cols=slice(0, GT)):
                return x_hi[n % 2][:, cols], x_lo[n % 2][:, cols]

            def hidden_rows(it, n, k):
                i = NB * n + k
                if k == 0:
                    pe.wait_ge(tr_read, it * 6 + (turn['x', n] + 1))
                if i - 1 > 0:
                    pe.wait_ge(silu_done, it * (2 * NB) + (i - 1))
                split_matmul(H1[i % 2][:, :], weight(k), xs(n)).then_inc(h1_made, 1)
                if i - 1 > 0:
                    pe.wait_ge(hidden_done, it * (2 * NB) + (i - 1))
                split_matmul(H3[i % 2][:, :], weight(NB + k), xs(n)).then_inc(h3_made, 1)

            def spread_gate(it, n, k):
                if k == 0:
                    pe.wait_ge(tr_read, it * 6 + (turn['g', n] + 1))
                if NB * n + k > 0:
                    pe.wait_ge(hidden_done, it * (2 * NB) + (NB * n + k))
                sel = cr[0:E0, C_PAIR + k * P:C_PAIR + (k + 1) * P]
                pe.matmul(GATE[:, :], sel, g_hi[n % 2][:, :], start=True, stop=False)
                pe.matmul(GATE[:, :], sel, g_lo[n % 2][:, :], start=False, stop=True).then_inc(gate_spread, 1)

            def down(it, n, k):
                i = NB * n + k
                pe.wait_ge(h_lo_done, it * (2 * NB) + (i + 1))
                if k == 0:
                    if n > 0:
                        pe.wait_ge(y_copied, it * 2 + n)
                split_matmul(YT[:, :], weight(2 * NB + k), (h_hi[i % 2][:, :], h_lo[i % 2][:, :]),
                             start=k == 0, stop=k == NB - 1).then_inc(y_summed, 1)

            def transpose_x(it, n):
                pe.wait_ge(xn_done, it * (2 * GB) + (GB * (n + 1)))
                if turn['x', n] > 0:
                    pe.wait_ge(tr_read, it * 6 + turn['x', n])
                for b in range(GB):
                    mm = pe.transpose(TR[:, b * P:(b + 1) * P], xn[:, b, :], sb["ident"][:, :])
                mm.then_inc(x_transposed, 1)

            def make_logits(it, n):
                pe.wait_ge(tr_read, it * 6 + (turn['x', n] + 1))
                if RS * (n - 1) + 1 > 0:
                    pe.wait_ge(routed, it * (2 * RS) + (RS * (n - 1) + 1))
                for b in range(GB):
                    mm = split_matmul(LG[:, b * E0:(b + 1) * E0], xs(n, slice(b * P, (b + 1) * P)), weight(3 * NB, E0))
                mm.then_inc(logits_made, 1)

            def transpose_gates(it, n):
                pe.wait_ge(routed, it * (2 * RS) + (RS * (n + 1)))
                pe.wait_ge(tr_read, it * 6 + turn['g', n])
                for b in range(GB):
                    mm = pe.transpose(TR[0:E0, b * P:(b + 1) * P], gates[:, b, :], sb["ident"][:, :])
                mm.then_inc(g_transposed, 1)

            def transpose_back(it, n):
                pe.wait_ge(y_copied, it * 2 + (n + 1))
                pe.wait_ge(tr_read, it * 6 + turn['o', n])
                for b in range(GB):
                    mm = pe.transpose(TR[:, b * P:(b + 1) * P], y[:, b * P:(b + 1) * P], sb["ident"][:, :])
                mm.then_inc(y_back, 1)

            def slot(it, n):
                for k in range(NB):
                    if there(it, n):
                        hidden_rows(it, n, k)
                    if k == 0 and there(it, n + 1):
                        transpose_x(it, n + 1)
                    if k >= 2 and there(it, n):
                        down(it, n, k - 2)
                    elif k < 2 and there(it, n - 1):
                        down(it, n - 1, NB + k - 2)
                    if k < NB - 1 and there(it, n):
                        spread_gate(it, n, k)
                    if k == 1 and there(it, n + 1):
                        make_logits(it, n + 1)
                    if k == 2 and there(it, n - 1):
                        transpose_back(it, n - 1)
                    if k == NB - 1 and there(it, n + 1):
                        transpose_gates(it, n + 1)

            pe.wait_ge(split_lo, 1)
            run(pe, slot)

        @block.scalar
        def _(act):
            def copy(out, src, done):
                act.activation(out, src, ACT.Copy).then_inc(done, 1)

            def make_silu(it, n, k):
                i = NB * n + k
                act.wait_ge(h1_made, it * (2 * NB) + (i + 1))
                if i - 1 > 0:
                    act.wait_ge(hidden_done, it * (2 * NB) + (i - 1))
                act.activation(silu[i % 2][:, :], H1[i % 2][:, :], ACT.Silu).then_inc(silu_done, 1)

            def hidden_hi(it, n, k):
                i = NB * n + k
                act.wait_ge(hidden_done, it * (2 * NB) + (i + 1))
                if i - 1 > 0:
                    act.wait_ge(y_summed, it * (2 * NB) + (i - 1))
                copy(h_hi[i % 2][:, :], hidden[i % 2][:, :], h_hi_done)

            def slot(it, n):
                for k in range(NB):
                    if there(it, n):
                        make_silu(it, n, k)
                    if k >= 1 and there(it, n):
                        hidden_hi(it, n, k - 1)
                    elif k == 0 and there(it, n - 1):
                        hidden_hi(it, n - 1, NB - 1)
                    if k == 0 and there(it, n + 1):
                        act.wait_ge(x_transposed, it * 2 + (n + 2))
                        if NB * n > 0:
                            act.wait_ge(h3_made, it * (2 * NB) + (NB * n))
                        copy(x_hi[(n + 1) % 2][:, :], TR[:, :], x_hi_done)
                    if k == 1 and there(it, n - 1):
                        act.wait_ge(y_summed, it * (2 * NB) + (NB * n))
                        if n - 1 > 0:
                            act.wait_ge(y_back, it * 2 + (n - 1))
                        copy(y[:, :], YT[:, :], y_copied)
                    if k == 2 and there(it, n + 1):
                        act.wait_ge(routed, it * (2 * RS) + (RS * (n + 1) + 3))
                        act.activation(exps[:, :, :], shifted[:, :, :], ACT.Exp).then_inc(exps_done, 1)
                    if k == NB - 1 and there(it, n + 1):
                        act.wait_ge(g_transposed, it * 2 + (n + 2))
                        if 4 * n > 0:
                            act.wait_ge(gate_spread, it * 8 + (4 * n))
                        copy(g_hi[(n + 1) % 2][:, :], TR[0:E0, :], g_hi_done)

            run(act, slot)

        @block.vector
        def _(dve):
            def hidden_products(it, n, k):
                i = NB * n + k
                dve.wait_ge(silu_done, it * (2 * NB) + (i + 1))
                dve.wait_ge(h3_made, it * (2 * NB) + (i + 1))
                if k == NB - 1:
                    dve.wait_ge(h_lo_done, it * (2 * NB) + (i - 1))
                    dve.tensor_tensor(hidden[i % 2][:, :], silu[i % 2][:, :], H3[i % 2][:, :], ALU.mult)\
                        .then_inc(hidden_done, 1)
                    return
                if i > 0:
                    dve.wait_ge(hidden_done, it * (2 * NB) + i)
                dve.tensor_tensor(product[i % 2][:, :], silu[i % 2][:, :], H3[i % 2][:, :], ALU.mult)\
                    .then_inc(product_done, 1)
                dve.wait_ge(product_done, it * 8 + (4 * n + k + 1))
                dve.wait_ge(gate_spread, it * 8 + (4 * n + k + 1))
                if i - 1 > 0:
                    dve.wait_ge(h_lo_done, it * (2 * NB) + (i - 1))
                dve.tensor_tensor(hidden[i % 2][:, :], product[i % 2][:, :], GATE[:, :], ALU.mult)\
                    .then_inc(hidden_done, 1)

            def by_expert(x):
                return x.unsqueeze(2).broadcast_to([P, GB, E0])

            def route(it, n, steps):
                base = RS * n
                l = logits[:, :, :]
                mine = l.unsqueeze(3).broadcast_to([P, GB, E0, E0])
                other = l.unsqueeze(2).broadcast_to([P, GB, E0, E0])
                for s in steps:
                    if s == 0:
                        dve.wait_ge(logits_made, it * 2 + (n + 1))
                    if s == 7:
                        dve.wait_ge(exps_done, it * 2 + (n + 1))
                    if s == 10:
                        if n > 0:
                            dve.wait_ge(g_transposed, it * 2 + n)
                    if base + s > 0:
                        dve.wait_ge(routed, it * (2 * RS) + (base + s))
                    if s == 0:
                        op = dve.tensor_tensor(l, LG[:, 0:GB * E0].rearrange("p (b e) -> p b e", e=E0),
                                               router_b.unsqueeze(1).broadcast_to([P, GB, E0]), ALU.add)
                    elif s == 1:
                        op = dve.tensor_reduce(top[:, :], l, AX.X, ALU.max)
                    elif s == 2:
                        op = dve.tensor_tensor(shifted[:, :, :], l, by_expert(top[:, :]), ALU.subtract)
                    elif s == 3:
                        op = dve.tensor_tensor(equal[:, :, :, :], other, mine, ALU.is_equal)
                    elif s == 4:
                        op = dve.tensor_tensor(equal[:, :, :, :], equal[:, :, :, :],
                                               earlier.unsqueeze(1).broadcast_to([P, GB, E0, E0]), ALU.mult)
                    elif s == 5:
                        op = dve.tensor_tensor(above[:, :, :, :], other, mine, ALU.is_gt)
                    elif s == 6:
                        dve.tensor_tensor(above[:, :, :, :], above[:, :, :, :], equal[:, :, :, :], ALU.add)\
                            .then_inc(product_summed, 1)
                        dve.wait_ge(product_summed, it * 2 + (n + 1))
                        op = dve.tensor_reduce(rank[:, :, :], above[:, :, :, :], AX.X, ALU.add)
                    elif s == 7:
                        op = dve.scalar_tensor_tensor(chosen[:, :, :], rank[:, :, :], 2.0, exps[:, :, :],
                                                      ALU.is_lt, ALU.mult)
                    elif s == 8:
                        op = dve.tensor_reduce(total[:, :], chosen[:, :, :], AX.X, ALU.add)
                    elif s == 9:
                        op = dve.reciprocal(recip[:, :], total[:, :])
                    else:
                        op = dve.tensor_tensor(gates[:, :, :], chosen[:, :, :], by_expert(recip[:, :]), ALU.mult)
                    op.then_inc(routed, 1)

            def moments(it, G):
                if GB * G > 0:
                    dve.wait_ge(xn_done, it * (2 * GB) + (GB * G))
                if GB * G > 0:
                    dve.wait_ge(mean_done, it * (2 * GB) + (GB * G))
                if G > 0:
                    dve.wait_ge(rstd_done, it * 2 + G)
                for b in range(GB):
                    dve.bn_stats(stats[:, b, :], X[:, bass.ds(it * (2 * GT) + G * GT + b * P, P)])\
                        .then_inc(stats_done, 1)
                dve.wait_ge(stats_done, it * (2 * GB) + (GB * (G + 1)))
                dve.sem_inc(passed, 1)
                for b in range(GB):
                    dve.bn_aggr(mean_var[:, b, :], stats[:, b, :]).then_inc(mean_done, 1)

            def layernorm(it, G):
                dve.wait_ge(rstd_done, it * 2 + (G + 1))
                dve.wait_ge(mean_done, it * (2 * GB) + (GB * (G + 1)))
                if G > 0:
                    dve.wait_ge(x_transposed, it * 2 + G)
                for b in range(GB):
                    dve.tensor_scalar(xn[:, b, :], X[:, bass.ds(it * (2 * GT) + G * GT + b * P, P)],
                                      mean_var[:, b, 0:1], rstd[:, b:b + 1], ALU.subtract, ALU.mult)\
                        .then_inc(xn_done, 1)

            def slot(it, n):
                for k in range(NB):
                    if there(it, n):
                        hidden_products(it, n, k)
                    if k == 0 and there(it, n + 1):
                        dve.wait_ge(x_hi_done, it * 2 + (n + 2))
                        dve.tensor_tensor(x_lo[(n + 1) % 2][:, :], TR[:, :], x_hi[(n + 1) % 2][:, :].bitcast(F32),
                                          ALU.subtract).then_inc(tr_read, 1)
                    if k == 1 and there(it, n + 1):
                        route(it, n + 1, range(0, 5))
                    if k == 2 and there(it, n + 1):
                        route(it, n + 1, range(5, 7))
                    if k == 2 and there(it, n - 1):
                        dve.wait_ge(y_back, it * 2 + n)
                        dve.wait_ge(xn_done, it * (2 * GB) + (GB * n))
                        x = group_columns(it, n - 1)
                        dve.tensor_tensor(x, TR[:, :], x, ALU.add).then_inc(tr_read, 1)
                    if k == 2 and there(it, n + 2):
                        moments(it, n + 2)
                    if k == 3 and there(it, n + 1):
                        route(it, n + 1, range(7, RS))
                    if k == 3 and there(it, n + 2):
                        layernorm(it, n + 2)
                    if k == NB - 1 and there(it, n + 1):
                        dve.wait_ge(g_hi_done, it * 2 + (n + 2))
                        dve.tensor_tensor(g_lo[(n + 1) % 2][:, :], TR[0:E0, :], g_hi[(n + 1) % 2][:, :].bitcast(F32),
                                          ALU.subtract).then_inc(tr_read, 1)

            dve.wait_ge(ready["ffn0"], 16)
            dve.tensor_copy(w_hi[:, :], raw[:, :]).then_inc(split, 1)
            dve.wait_ge(split, 1)
            dve.tensor_tensor(w_lo[:, :], raw[:, :], w_hi[:, :].bitcast(F32), ALU.subtract).then_inc(split_lo, 1)
            run(dve, slot)

        @block.gpsimd
        def _(pool):
            def hidden_lo(it, n, k):
                i = NB * n + k
                pool.wait_ge(h_hi_done, it * (2 * NB) + (i + 1))
                if i - 1 > 0:
                    pool.wait_ge(y_summed, it * (2 * NB) + (i - 1))
                pool.tensor_tensor(h_lo[i % 2][:, :], hidden[i % 2][:, :], h_hi[i % 2][:, :].bitcast(F32),
                                   ALU.subtract).then_inc(h_lo_done, 1)

            def reciprocal_deviation(it, G):
                pool.wait_ge(mean_done, it * (2 * GB) + (GB * (G + 1)))
                if GB * G > 0:
                    pool.wait_ge(xn_done, it * (2 * GB) + (GB * G))
                if G > 0:
                    pool.wait_ge(rstd_done, it * 2 + G)
                pool.sem_inc(passed, 1)
                pool.tensor_scalar(var_eps[:, :], mean_var[:, :, 1], LN_EPS, 1.0, ALU.add, ALU.mult)\
                    .then_inc(var_done, 1)
                pool.wait_ge(var_done, it * 2 + (G + 1))
                pool.tensor_tensor(rstd[:, :], var_eps[:, :], power[:, :], ALU.pow).then_inc(rstd_done, 1)

            def slot(it, n):
                for k in range(NB):
                    if k >= 1 and there(it, n):
                        hidden_lo(it, n, k - 1)
                    elif k == 0 and there(it, n - 1):
                        hidden_lo(it, n - 1, NB - 1)
                    if k == 2 and there(it, n + 2):
                        reciprocal_deviation(it, n + 2)

            pool.sem_clear(used_before)
            pool.memset(power[:, :], -0.5).then_inc(power_done, 1)
            pool.wait_ge(power_done, 1)
            run(pool, slot)


def relu_experts(nc, phase, sb, ps, ready):
    NB = E1 * C1
    X = sb["x"]
    HT, YT, GATE, TR, LG, BT = ps[0:2], ps[2:4], ps[4], ps[5], ps[6], ps[7]
    cr = sb["const_r"]
    earlier = sb["const"][:, C_EARLIER - N_CONST_R:C_EARLIER - N_CONST_R + E1 * E1].rearrange("p (a b) -> p a b", b=E1)
    router_b = sb["rows"][:, R_ROUTER1:R_ROUTER1 + E1]

    with ExitStack() as ctx:
        def buf(name, shape, dt=F32):
            return ctx.enter_context(nc.sbuf_tensor(f"ffn1_{name}", shape, dt))

        sem, used_before = phase_semaphores(nc, ctx, phase, "ffn1")
        raw = sb["raw_ffn1"]
        w_hi, w_lo = buf("w_hi", [P, W_FFN1], F32R), buf("w_lo", [P, W_FFN1], F32R)
        stats, mean_var = buf("stats", [P, GB, 6]), buf("mean_var", [P, GB, 2])
        var_eps, rstd, power = buf("var_eps", [P, GB]), buf("rstd", [P, GB]), buf("power", [P, GB])
        xn = buf("xn", [P, GB, D])
        x_hi = [buf(f"x_hi{i}", [P, GT], F32R) for i in range(2)]
        x_lo = [buf(f"x_lo{i}", [P, GT], F32R) for i in range(2)]
        logits, shifted = buf("logits", [P, GB, E1]), buf("shifted", [P, GB, E1])
        top, exps = buf("top", [P, GB]), buf("exps", [P, GB, E1])
        above, equal = buf("above", [P, GB, E1, E1]), buf("equal", [P, GB, E1, E1])
        rank, chosen = buf("rank", [P, GB, E1]), buf("chosen", [P, GB, E1])
        total, recip, gates = buf("total", [P, GB]), buf("recip", [P, GB]), buf("gates", [P, GB, E1])
        g_hi = [buf(f"g_hi{i}", [E1, GT], F32R) for i in range(2)]
        g_lo = [buf(f"g_lo{i}", [E1, GT], F32R) for i in range(2)]
        scaled = [buf(f"scaled{i}", [P, GT]) for i in range(2)]
        hidden = [buf(f"hidden{i}", [P, GT]) for i in range(2)]
        h_hi = [buf(f"h_hi{i}", [P, GT], F32R) for i in range(2)]
        h_lo = [buf(f"h_lo{i}", [P, GT], F32R) for i in range(2)]
        gate = buf("gate", [P, GT])
        probs = buf("probs", [P, GB, E1])
        y = [buf(f"y{i}", [P, GT]) for i in range(2)]

        split, split_lo = sem("weights_hi_done"), sem("weights_lo_done")
        x_transposed, logits_made, g_transposed = sem("x_transposed"), sem("logits_made"), sem("g_transposed")
        hidden_made, gate_spread, bias_made = sem("hidden_made"), sem("gate_spread"), sem("bias_made")
        y_summed, y_back = sem("y_summed"), sem("y_back")
        x_hi_done, g_hi_done, exps_done = sem("x_hi_done"), sem("g_hi_done"), sem("exps_done")
        h_hi_done, y_started = sem("h_hi_done"), sem("y_started")
        stats_done, mean_done, xn_done = sem("stats_done"), sem("mean_done"), sem("xn_done")
        tr_read = sem("tr_read")
        routed = sem("routed")
        scaled_done, y_added, hidden_done = sem("scaled_done"), sem("y_added"), sem("hidden_done")
        power_done, var_done, rstd_done = sem("power_done"), sem("var_done"), sem("rstd_done")
        h_lo_done, passed = sem("h_lo_done"), sem("passed")
        gate_copied = sem("gate_copied")
        product_summed = sem("product_summed")
        RS = 13

        turn = {}
        for n in range(-2, NG + 1):
            for name, G in (("o", n - 1), ("x", n + 1), ("g", n + 1)):
                if 0 <= G < NG:
                    turn[name, G] = len(turn)

        def weight_parts(e):
            if e == 0:
                return [slice(2 * NB * P, W_FFN1)]
            return [slice((e - 1) * C1 * P, e * C1 * P), slice((NB + (e - 1) * C1) * P, (NB + e * C1) * P)]

        block = ctx.enter_context(nc.Block())

        def run(engine, slot):
            for n in range(-2, 2):
                slot(0, n)
            with engine.Fori(0, 2) as it:
                for n in range(2, 4):
                    slot(it, n)
            for n in range(6, NG + 1):
                slot(0, n)

        def there(it, G):
            return not isinstance(it, int) or 0 <= G < NG

        def group_columns(it, G):
            return X[:, bass.ds(it * (2 * GT) + G * GT, GT)]

        @block.tensor
        def _(pe):
            def split_matmul(out, l, r, start=True, stop=True):
                pe.matmul(out, l[0], r[0], start=start, stop=False)
                pe.matmul(out, l[0], r[1], start=False, stop=False)
                return pe.matmul(out, l[1], r[0], start=False, stop=stop)

            def weight(block, width=P):
                return w_hi[:, block * P:block * P + width], w_lo[:, block * P:block * P + width]

            def xs(n, cols=slice(0, GT)):
                return x_hi[n % 2][:, cols], x_lo[n % 2][:, cols]

            def hidden_rows(it, n, k):
                i = NB * n + k
                if k == 0:
                    pe.wait_ge(tr_read, it * 6 + (turn['x', n] + 1))
                if n == 0 and isinstance(it, int) and k % C1 == 0:
                    pe.wait_ge(split_lo, k // C1 + 2)
                if i - 1 > 0:
                    pe.wait_ge(hidden_done, it * (2 * NB) + (i - 1))
                split_matmul(HT[i % 2][:, :], weight(k), xs(n)).then_inc(hidden_made, 1)

            def spread_gate(it, n, e):
                if e == 0:
                    pe.wait_ge(tr_read, it * 6 + (turn['g', n] + 1))
                if E1 * n + e > 0:
                    pe.wait_ge(gate_copied, it * (2 * E1) + (E1 * n + e))
                sel = cr[0:E1, C_ONE_ROW + e * P:C_ONE_ROW + (e + 1) * P]
                pe.matmul(GATE[:, :], sel, g_hi[n % 2][:, :], start=True, stop=False)
                pe.matmul(GATE[:, :], sel, g_lo[n % 2][:, :], start=False, stop=True).then_inc(gate_spread, 1)

            def mixed_bias(it, n):
                if n > 0:
                    pe.wait_ge(y_started, it * 2 + n)
                c = (2 * NB) * P
                split_matmul(BT[:, :], (w_hi[0:E1, c:c + P], w_lo[0:E1, c:c + P]), (g_hi[n % 2][:, :], g_lo[n % 2][:, :]))\
                    .then_inc(bias_made, 1)

            def down(it, n, k):
                i, e = NB * n + k, k // C1
                pe.wait_ge(h_lo_done, it * (2 * NB) + (i + 1))
                if k % C1 == 0:
                    if E1 * n + e - 1 > 0:
                        pe.wait_ge(scaled_done, it * (2 * E1) + (E1 * n + e - 1))
                mm = split_matmul(YT[e % 2][:, :], weight(NB + k), (h_hi[i % 2][:, :], h_lo[i % 2][:, :]),
                                  start=k % C1 == 0, stop=k % C1 == C1 - 1)
                mm.then_inc(y_summed, 1)

            def transpose_x(it, n):
                pe.wait_ge(xn_done, it * (2 * GB) + (GB * (n + 1)))
                if turn['x', n] > 0:
                    pe.wait_ge(tr_read, it * 6 + turn['x', n])
                for b in range(GB):
                    mm = pe.transpose(TR[:, b * P:(b + 1) * P], xn[:, b, :], sb["ident"][:, :])
                mm.then_inc(x_transposed, 1)

            def make_logits(it, n):
                pe.wait_ge(tr_read, it * 6 + (turn['x', n] + 1))
                if RS * (n - 1) + 1 > 0:
                    pe.wait_ge(routed, it * (2 * RS) + (RS * (n - 1) + 1))
                for b in range(GB):
                    mm = split_matmul(LG[:, b * E1:(b + 1) * E1], xs(n, slice(b * P, (b + 1) * P)), weight(2 * NB + 1, E1))
                mm.then_inc(logits_made, 1)

            def transpose_gates(it, n):
                pe.wait_ge(routed, it * (2 * RS) + (RS * (n + 1)))
                pe.wait_ge(tr_read, it * 6 + turn['g', n])
                for b in range(GB):
                    mm = pe.transpose(TR[0:E1, b * P:(b + 1) * P], gates[:, b, :], sb["ident"][:, :])
                mm.then_inc(g_transposed, 1)

            def transpose_back(it, n):
                pe.wait_ge(y_added, it * (2 * E1) + (E1 * (n + 1)))
                pe.wait_ge(tr_read, it * 6 + turn['o', n])
                for b in range(GB):
                    mm = pe.transpose(TR[:, b * P:(b + 1) * P], y[n % 2][:, b * P:(b + 1) * P], sb["ident"][:, :])
                mm.then_inc(y_back, 1)

            def slot(it, n):
                for k in range(NB):
                    e, c = k // C1, k % C1
                    if there(it, n):
                        hidden_rows(it, n, k)
                    if k >= 2 and there(it, n):
                        down(it, n, k - 2)
                    elif k < 2 and there(it, n - 1):
                        down(it, n - 1, NB + k - 2)
                    if c == 3 and there(it, n):
                        spread_gate(it, n, e)
                    if k == 2 and there(it, n):
                        mixed_bias(it, n)
                    if (e, c) == (2, 0) and there(it, n - 1):
                        transpose_back(it, n - 1)
                    if (e, c) == (2, 2) and there(it, n + 1):
                        transpose_x(it, n + 1)
                    if (e, c) == (3, 2) and there(it, n + 1):
                        make_logits(it, n + 1)
                    if (e, c) == (7, 0) and there(it, n + 1):
                        transpose_gates(it, n + 1)

            pe.wait_ge(split_lo, 1)
            run(pe, slot)

        @block.scalar
        def _(act):
            def copy(out, src, done):
                act.activation(out, src, ACT.Copy).then_inc(done, 1)

            def copy_gate(it, n, e):
                act.wait_ge(gate_spread, it * (2 * E1) + (E1 * n + e + 1))
                if E1 * n + e > 0:
                    act.wait_ge(scaled_done, it * (2 * E1) + (E1 * n + e))
                copy(gate[:, :], GATE[:, :], gate_copied)

            def rectify(it, n, k):
                i = NB * n + k
                act.wait_ge(hidden_made, it * (2 * NB) + (i + 1))
                if i - 1 > 0:
                    act.wait_ge(h_lo_done, it * (2 * NB) + (i - 1))
                act.activation(hidden[i % 2][:, :], HT[i % 2][:, :], ACT.Relu,
                               bias=sb["cols"][:, N_COLS - NB + k:N_COLS - NB + k + 1]).then_inc(hidden_done, 1)
                if i - 1 > 0:
                    act.wait_ge(y_summed, it * (2 * NB) + (i - 1))
                act.wait_ge(hidden_done, it * (2 * NB) + (i + 1))
                copy(h_hi[i % 2][:, :], hidden[i % 2][:, :], h_hi_done)

            def slot(it, n):
                for k in range(NB):
                    e, c = k // C1, k % C1
                    if there(it, n):
                        rectify(it, n, k)
                    if c == 0 and e >= 1 and there(it, n):
                        copy_gate(it, n, e - 1)
                    if k == 0 and there(it, n - 1):
                        copy_gate(it, n - 1, E1 - 1)
                    if k == 3 and there(it, n):
                        act.wait_ge(bias_made, it * 2 + (n + 1))
                        if n - 1 > 0:
                            act.wait_ge(y_back, it * 2 + (n - 1))
                        copy(y[n % 2][:, :], BT[:, :], y_started)
                    if (e, c) == (2, 2) and there(it, n + 1):
                        act.wait_ge(x_transposed, it * 2 + (n + 2))
                        if NB * n > 0:
                            act.wait_ge(hidden_made, it * (2 * NB) + (NB * n))
                        copy(x_hi[(n + 1) % 2][:, :], TR[:, :], x_hi_done)
                    if (e, c) == (4, 1) and there(it, n + 1):
                        act.wait_ge(routed, it * (2 * RS) + (RS * (n + 1) + 3))
                        act.activation(exps[:, :, :], shifted[:, :, :], ACT.Exp).then_inc(exps_done, 1)
                    if (e, c) == (7, 0) and there(it, n + 1):
                        act.wait_ge(g_transposed, it * 2 + (n + 2))
                        if E1 * n > 0:
                            act.wait_ge(gate_spread, it * (2 * E1) + (E1 * n))
                        copy(g_hi[(n + 1) % 2][:, :], TR[0:E1, :], g_hi_done)

            act.wait_ge(ready["ffn1"], 16)
            for e in range(E1 + 1):
                for part in weight_parts(e):
                    op = act.activation(w_hi[:, part], raw[:, part], ACT.Copy)
                    op.then_inc(split, 1)
            run(act, slot)

        @block.vector
        def _(dve):
            def hidden_lo(it, n, k):
                i = NB * n + k
                dve.wait_ge(h_hi_done, it * (2 * NB) + (i + 1))
                if i - 1 > 0:
                    dve.wait_ge(y_summed, it * (2 * NB) + (i - 1))
                dve.tensor_tensor(h_lo[i % 2][:, :], hidden[i % 2][:, :], h_hi[i % 2][:, :].bitcast(F32),
                                  ALU.subtract).then_inc(h_lo_done, 1)

            def scale_expert(it, n, e):
                i = E1 * n + e
                dve.wait_ge(gate_copied, it * (2 * E1) + (i + 1))
                dve.wait_ge(y_summed, it * (2 * NB) + (NB * n + C1 * (e + 1)))
                if i - 1 > 0:
                    dve.wait_ge(y_added, it * (2 * E1) + (i - 1))
                dve.tensor_tensor(scaled[i % 2][:, :], gate[:, :], YT[e % 2][:, :], ALU.mult)\
                    .then_inc(scaled_done, 1)

            def by_expert(x):
                return x.unsqueeze(2).broadcast_to([P, GB, E1])

            def route(it, n, steps):
                base = RS * n
                l = logits[:, :, :]
                mine = probs[:, :, :].unsqueeze(3).broadcast_to([P, GB, E1, E1])
                other = probs[:, :, :].unsqueeze(2).broadcast_to([P, GB, E1, E1])
                for s in steps:
                    if s == 0:
                        dve.wait_ge(logits_made, it * 2 + (n + 1))
                    if s == 3:
                        dve.wait_ge(exps_done, it * 2 + (n + 1))
                    if s == 12:
                        if n > 0:
                            dve.wait_ge(g_transposed, it * 2 + n)
                    if base + s > 0:
                        dve.wait_ge(routed, it * (2 * RS) + (base + s))
                    if s == 0:
                        op = dve.tensor_tensor(l, LG[:, 0:GB * E1].rearrange("p (b e) -> p b e", e=E1),
                                               router_b.unsqueeze(1).broadcast_to([P, GB, E1]), ALU.add)
                    elif s == 1:
                        op = dve.tensor_reduce(top[:, :], l, AX.X, ALU.max)
                    elif s == 2:
                        op = dve.tensor_tensor(shifted[:, :, :], l, by_expert(top[:, :]), ALU.subtract)
                    elif s in (3, 10):
                        op = dve.tensor_reduce(total[:, :], exps[:, :, :] if s == 3 else chosen[:, :, :], AX.X, ALU.add)
                    elif s in (4, 11):
                        op = dve.reciprocal(recip[:, :], total[:, :])
                    elif s == 5:
                        op = dve.tensor_tensor(probs[:, :, :], exps[:, :, :], by_expert(recip[:, :]), ALU.mult)
                    elif s == 6:
                        op = dve.tensor_tensor(equal[:, :, :, :], other, mine, ALU.is_equal)
                    elif s == 7:
                        dve.tensor_tensor(equal[:, :, :, :], equal[:, :, :, :],
                                          earlier.unsqueeze(1).broadcast_to([P, GB, E1, E1]), ALU.mult)\
                            .then_inc(product_summed, 1)
                        op = dve.tensor_tensor(above[:, :, :, :], other, mine, ALU.is_gt)
                    elif s == 8:
                        dve.tensor_tensor(above[:, :, :, :], above[:, :, :, :], equal[:, :, :, :], ALU.add)\
                            .then_inc(product_summed, 1)
                        dve.wait_ge(product_summed, it * 4 + (2 * n + 2))
                        op = dve.tensor_reduce(rank[:, :, :], above[:, :, :, :], AX.X, ALU.add)
                    elif s == 9:
                        op = dve.scalar_tensor_tensor(chosen[:, :, :], rank[:, :, :], 2.0, probs[:, :, :],
                                                      ALU.is_lt, ALU.mult)
                    else:
                        op = dve.tensor_tensor(gates[:, :, :], chosen[:, :, :], by_expert(recip[:, :]), ALU.mult)
                    op.then_inc(routed, 1)

            def moments(it, G):
                if GB * G > 0:
                    dve.wait_ge(xn_done, it * (2 * GB) + (GB * G))
                if GB * G > 0:
                    dve.wait_ge(mean_done, it * (2 * GB) + (GB * G))
                if G > 0:
                    dve.wait_ge(rstd_done, it * 2 + G)
                for b in range(GB):
                    dve.bn_stats(stats[:, b, :], X[:, bass.ds(it * (2 * GT) + G * GT + b * P, P)])\
                        .then_inc(stats_done, 1)
                dve.wait_ge(stats_done, it * (2 * GB) + (GB * (G + 1)))
                dve.sem_inc(passed, 1)
                for b in range(GB):
                    dve.bn_aggr(mean_var[:, b, :], stats[:, b, :]).then_inc(mean_done, 1)

            def layernorm(it, G):
                dve.wait_ge(rstd_done, it * 2 + (G + 1))
                dve.wait_ge(mean_done, it * (2 * GB) + (GB * (G + 1)))
                if G > 0:
                    dve.wait_ge(x_transposed, it * 2 + G)
                for b in range(GB):
                    dve.tensor_scalar(xn[:, b, :], X[:, bass.ds(it * (2 * GT) + G * GT + b * P, P)],
                                      mean_var[:, b, 0:1], rstd[:, b:b + 1], ALU.subtract, ALU.mult)\
                        .then_inc(xn_done, 1)

            def slot(it, n):
                for k in range(NB):
                    e, c = k // C1, k % C1
                    if there(it, n):
                        hidden_lo(it, n, k)
                    if c == 2 and e >= 1 and there(it, n):
                        scale_expert(it, n, e - 1)
                    if k == 2 and there(it, n - 1):
                        scale_expert(it, n - 1, E1 - 1)
                    if (e, c) == (2, 0) and there(it, n - 1):
                        dve.wait_ge(y_back, it * 2 + n)
                        dve.wait_ge(xn_done, it * (2 * GB) + (GB * n))
                        x = group_columns(it, n - 1)
                        dve.tensor_tensor(x, TR[:, :], x, ALU.add).then_inc(tr_read, 1)
                    if (e, c) == (2, 3) and there(it, n + 1):
                        dve.wait_ge(x_hi_done, it * 2 + (n + 2))
                        dve.tensor_tensor(x_lo[(n + 1) % 2][:, :], TR[:, :], x_hi[(n + 1) % 2][:, :].bitcast(F32),
                                          ALU.subtract).then_inc(tr_read, 1)
                    if (e, c) == (4, 0) and there(it, n + 1):
                        route(it, n + 1, range(0, 3))
                    if (e, c) == (4, 3) and there(it, n + 1):
                        route(it, n + 1, range(3, 5))
                    if (e, c) == (5, 0) and there(it, n + 1):
                        route(it, n + 1, range(5, 7))
                    if (e, c) == (5, 1) and there(it, n + 1):
                        route(it, n + 1, range(7, 8))
                    if (e, c) == (5, 3) and there(it, n + 1):
                        route(it, n + 1, range(8, 10))
                    if (e, c) == (6, 1) and there(it, n + 1):
                        route(it, n + 1, range(10, RS))
                    if (e, c) == (3, 0) and there(it, n + 2):
                        moments(it, n + 2)
                    if (e, c) == (6, 3) and there(it, n + 2):
                        layernorm(it, n + 2)
                    if (e, c) == (7, 1) and there(it, n + 1):
                        dve.wait_ge(g_hi_done, it * 2 + (n + 2))
                        dve.tensor_tensor(g_lo[(n + 1) % 2][:, :], TR[0:E1, :], g_hi[(n + 1) % 2][:, :].bitcast(F32),
                                          ALU.subtract).then_inc(tr_read, 1)

            made = 0
            for e in range(E1 + 1):
                for part in weight_parts(e):
                    made += 1
                    dve.wait_ge(split, made)
                    op = dve.tensor_tensor(w_lo[:, part], raw[:, part], w_hi[:, part].bitcast(F32), ALU.subtract)
                op.then_inc(split_lo, 1)
            run(dve, slot)

        @block.gpsimd
        def _(pool):
            def add_expert(it, n, e):
                i = E1 * n + e
                pool.wait_ge(scaled_done, it * (2 * E1) + (i + 1))
                pool.wait_ge(y_started, it * 2 + (n + 1))
                if i > 0:
                    pool.wait_ge(y_added, it * (2 * E1) + i)
                pool.tensor_tensor(y[n % 2][:, :], y[n % 2][:, :], scaled[i % 2][:, :], ALU.add).then_inc(y_added, 1)

            def reciprocal_deviation(it, G):
                pool.wait_ge(mean_done, it * (2 * GB) + (GB * (G + 1)))
                if GB * G > 0:
                    pool.wait_ge(xn_done, it * (2 * GB) + (GB * G))
                if G > 0:
                    pool.wait_ge(rstd_done, it * 2 + G)
                pool.sem_inc(passed, 1)
                pool.tensor_scalar(var_eps[:, :], mean_var[:, :, 1], LN_EPS, 1.0, ALU.add, ALU.mult)\
                    .then_inc(var_done, 1)
                pool.wait_ge(var_done, it * 2 + (G + 1))
                pool.tensor_tensor(rstd[:, :], var_eps[:, :], power[:, :], ALU.pow).then_inc(rstd_done, 1)

            def slot(it, n):
                for e in range(E1):
                    if e >= 1 and there(it, n):
                        add_expert(it, n, e - 1)
                    elif e == 0 and there(it, n - 1):
                        add_expert(it, n - 1, E1 - 1)
                    if e == 3 and there(it, n + 2):
                        reciprocal_deviation(it, n + 2)

            pool.sem_clear(used_before)
            pool.memset(power[:, :], -0.5).then_inc(power_done, 1)
            pool.wait_ge(power_done, 1)
            run(pool, slot)


def latent_attention(nc, phase, sb, ps, t, ready):
    kc, HL, DL = DC, 2, D // 2
    X = sb["x"]
    TR, PL, PC, KT, S, T, O, M = ps
    cr, cols = sb["const_r"], sb["cols"]
    ident, ident_r = sb["ident"][:, :], cr[:, C_ID:C_ID + P]
    diag = sb["const"][0:32, 0:HL]
    c = C_HEAD - N_CONST_R
    head_rows = sb["const"][:, c:c + HL]
    ctx_g, ctx_b, lat_g, lat_b, q_gamma, k_gamma = (cols[:, COL_LATENT + n:COL_LATENT + n + 1] for n in range(6))
    bo_hi, bo_lo = (sb[r][:, R_LATENT:R_LATENT + P] for r in ("rows_hi", "rows_lo"))

    turn = {}
    for n in range(-6, B + 2):
        for name, m in (("y", n - 2), ("m", n), ("o", n - 1)):
            if 0 <= m < B:
                turn[name, m] = len(turn)

    with ExitStack() as ctx:
        def buf(name, shape, dt=F32):
            return ctx.enter_context(nc.sbuf_tensor(f"latent_{name}", shape, dt))

        sem, used_before = phase_semaphores(nc, ctx, phase, "latent")
        raw = sb["raw_xattn1"]
        w_hi, w_lo = buf("w_hi", [P, W_LATENT], F32R), buf("w_lo", [P, W_LATENT], F32R)
        mask_rows = buf("mask_rows", [P, B * P], F32R)
        mask_cols = buf("mask_cols", [P, B])
        gamma, head_gamma = buf("gamma", [P, 1]), buf("head_gamma", [P, HL])
        ctx_in = buf("ctx_in", [P, GB, DC])
        stats, mean_var = buf("stats", [P, 2 * GB, 6]), buf("mean_var", [P, 2 * GB, 2])
        var_eps, rstd, once = buf("var_eps", [P, 2 * GB]), buf("rstd", [P, 2 * GB]), buf("once", [P, 2 * GB])
        twice, twice_eps, again = buf("twice", [P, GB]), buf("twice_eps", [P, GB]), buf("again", [P, GB])
        power = buf("power", [P, 2 * GB])
        xn, cn = buf("xn", [P, GB, D]), buf("cn", [P, GB, DC])
        xf, cf = buf("xf", [P, GT]), buf("cf", [kc, GT])
        x_hi, x_lo = ([buf(f"x_{w}{i}", [P, GT], F32R) for i in range(2)] for w in ("hi", "lo"))
        c_hi, c_lo = ([buf(f"c_{w}{i}", [kc, GT], F32R) for i in range(2)] for w in ("hi", "lo"))
        squares = buf("squares", [P, 3 * P])
        norms, norms_kept, inverse = buf("norms", [P, 3 * HL]), buf("norms_kept", [P, 3 * HL]), buf("inverse", [P, 3 * HL])
        unit = [buf(f"unit{i}", [P, 3, P]) for i in range(2)]
        v = [buf(f"v{i}", [P, 2, HL, DL + 1]) for i in range(4)]
        q_heads = buf("q_heads", [P, HL, P])
        q_hi, q_lo, k_hi, k_lo = ([buf(f"{w}{i}", [P, 2 * P], F32R) for i in range(2)]
                                  for w in ("q_hi", "q_lo", "k_hi", "k_lo"))
        maxes = buf("maxes", [P, 32])
        neg_max = buf("neg_max", [32, HL, P], F32R)
        probs = [buf(f"probs{i}", [P, 2, HL * P]) for i in range(2)]
        recip, heads = buf("recip", [P, HL]), buf("heads", [P, HL, DL])
        o_hi, o_lo = buf("o_hi", [P, P], F32R), buf("o_lo", [P, P], F32R)

        x_transposed, c_transposed = sem("x_transposed"), sem("c_transposed")
        projected, keys_transposed = sem("projected"), sem("keys_transposed")
        scored, max_transposed, shifted = sem("scored"), sem("max_transposed"), sem("shifted")
        weighted, o_transposed, out_projected = sem("weighted"), sem("o_transposed"), sem("out_projected")
        affine_done, squares_done, v_done = sem("affine_done"), sem("squares_done"), sem("v_done")
        exp_done, k_hi_done, q_hi_done, o_hi_done = sem("exp_done"), sem("k_hi_done"), sem("q_hi_done"), sem("o_hi_done")
        setup_steps = sem("setup_steps")
        stats_done, mean_done, normal_done, hi_done = sem("stats_done"), sem("mean_done"), sem("normal_done"), sem("hi_done")
        norms_done, norms_bounded, unit_done = sem("norms_done"), sem("norms_bounded"), sem("unit_done")
        q_heads_done, k_lo_done = sem("q_heads_done"), sem("k_lo_done")
        max_done, m_read, recip_done, heads_done = sem("max_done"), sem("m_read"), sem("recip_done"), sem("heads_done")
        filled, rstd_steps, rstd_done = sem("filled"), sem("rstd_steps"), sem("rstd_done")
        lo_done, inverse_done, q_lo_done = sem("lo_done"), sem("inverse_done"), sem("q_lo_done")
        again_done = sem("again_done")
        ctx_loaded, passed = sem("ctx_loaded"), sem("passed")
        SETUP = 6

        block = ctx.enter_context(nc.Block())

        def run(engine, slot):
            for n in range(-6, 2):
                slot(0, n)
            with engine.Fori(0, 3) as it:
                for n in range(2, 10):
                    slot(it, n)
            for n in range(26, B + 2):
                slot(0, n)

        def there(it, n):
            return not isinstance(it, int) or 0 <= n < B

        def group(it, G):
            return not isinstance(it, int) or 0 <= G < NG

        def split_parts(tiles, n):
            cols = slice((n % GB) * P, (n % GB + 1) * P)
            return tuple(x[(n // GB) % 2][:, cols] for x in tiles)

        @block.tensor
        def _(pe):
            def split_matmul(out, l, r, start=True, stop=True):
                pe.matmul(out, l[0], r[0], start=start, stop=False)
                pe.matmul(out, l[0], r[1], start=False, stop=False)
                return pe.matmul(out, l[1], r[0], start=False, stop=stop)

            def transpose_inputs(it, G):
                pe.wait_ge(normal_done, it * (4 * GB) + (2 * GB * (G + 1)))
                if 2 * G > 0:
                    pe.wait_ge(affine_done, it * 4 + (2 * G))
                for b in range(GB):
                    mm = pe.transpose(TR[:, b * P:(b + 1) * P], xn[:, b, :], ident)
                mm.then_inc(x_transposed, 1)

            def transpose_context(it, G):
                pe.wait_ge(affine_done, it * 4 + (2 * G + 1))
                for b in range(GB):
                    mm = pe.transpose(TR[0:kc, b * P:(b + 1) * P], cn[:, b, :], ident)
                mm.then_inc(c_transposed, 1)

            def project(it, n):
                pe.wait_ge(lo_done, it * 4 + (2 * (n // GB) + 2))
                if 2 * n > 0:
                    pe.wait_ge(unit_done, it * 16 + (2 * n))
                if 2 * n > 0:
                    pe.wait_ge(v_done, it * 16 + (2 * n))
                split_matmul(PL[:, 0:3 * P], split_parts((x_hi, x_lo), n), (w_hi[:, 0:3 * P], w_lo[:, 0:3 * P]))
                split_matmul(PC[:, 0:2 * P], split_parts((c_hi, c_lo), n),
                             (w_hi[0:kc, 3 * P:5 * P], w_lo[0:kc, 3 * P:5 * P])).then_inc(projected, 1)

            def transpose_keys(it, n):
                pe.wait_ge(unit_done, it * 16 + (2 * n + 2))
                if n > 0:
                    pe.wait_ge(k_lo_done, it * 8 + n)
                for i in range(3):
                    mm = pe.transpose(KT[:, i * P:(i + 1) * P], unit[n % 2][:, i, :], ident)
                mm.then_inc(keys_transposed, 1)

            def scores(it, n):
                pe.wait_ge(q_lo_done, it * 8 + (n + 1))
                pe.wait_ge(k_lo_done, it * 8 + (n + 1))
                if n > 0:
                    pe.wait_ge(max_done, it * 8 + n)
                for h in range(HL):
                    pe.matmul(S[:, h * 2 * P:(h + 1) * 2 * P], q_hi[n % 2][:, h * P:(h + 1) * P], k_hi[n % 2][:, :],
                              start=True, stop=False)
                    mm = pe.matmul(S[:, h * 2 * P + P:(h + 1) * 2 * P], ident_r,
                                   mask_rows[:, bass.ds(it * (8 * P) + n * P, P)], start=False, stop=True)
                mm.then_inc(scored, 1)

            def key_scores(it, n):
                if 2 * n > 0:
                    pe.wait_ge(exp_done, it * 16 + (2 * n))
                q = (q_hi[n % 2][:, :], q_lo[n % 2][:, :])
                for i in range(2):
                    keys = slice(i * P, (i + 1) * P)
                    split_matmul(T[:, i * 2 * P:(i + 1) * 2 * P], (k_hi[n % 2][:, keys], k_lo[n % 2][:, keys]), q,
                                 start=i == 0, stop=False)

            def transpose_max(it, n):
                pe.wait_ge(max_done, it * 8 + (n + 1))
                if turn['m', n] > 0:
                    pe.wait_ge(m_read, it * 24 + turn['m', n])
                pe.transpose(M[0:32, 0:P], maxes[:, :], ident).then_inc(max_transposed, 1)

            def shift(it, n):
                pe.wait_ge(m_read, it * 24 + (turn['m', n] + 1))
                for i in range(2):
                    mm = pe.matmul(T[:, i * 2 * P:(i + 1) * 2 * P], cr[0:32, C_ONES:C_ONES + P],
                                   neg_max[:, :, :].rearrange("p h q -> p (h q)"), start=False, stop=i == 1)
                mm.then_inc(shifted, 1)

            def weigh(it, n):
                pe.wait_ge(exp_done, it * 16 + (2 * n + 2))
                pe.wait_ge(v_done, it * 16 + (2 * n + 2))
                if n > 0:
                    pe.wait_ge(heads_done, it * 8 + n)
                for h in range(HL):
                    for i in range(2):
                        mm = pe.matmul(O[:, h * (DL + 1):(h + 1) * (DL + 1)], probs[n % 2][:, i, h * P:(h + 1) * P],
                                       v[n % 4][:, i, h, :], start=i == 0, stop=i == 1)
                mm.then_inc(weighted, 1)

            def transpose_heads(it, n):
                pe.wait_ge(heads_done, it * 8 + (n + 1))
                pe.wait_ge(m_read, it * 24 + turn['o', n])
                pe.transpose(M[:, 0:P], heads[:, :, :].rearrange("p h d -> p (h d)"), ident).then_inc(o_transposed, 1)

            def out_project(it, n):
                pe.wait_ge(m_read, it * 24 + (turn['o', n] + 1))
                pe.wait_ge(m_read, it * 24 + turn['y', n])
                pe.matmul(M[:, 0:P], ident_r, bo_hi, start=True, stop=False)
                pe.matmul(M[:, 0:P], ident_r, bo_lo, start=False, stop=False)
                split_matmul(M[:, 0:P], (o_hi[:, :], o_lo[:, :]), (w_hi[:, 5 * P:6 * P], w_lo[:, 5 * P:6 * P]),
                             start=False).then_inc(out_projected, 1)

            def slot(it, n):
                G, b = n // GB, n % GB
                if there(it, n):
                    scores(it, n)
                    key_scores(it, n)
                if there(it, n + 2):
                    project(it, n + 2)
                if there(it, n - 2):
                    out_project(it, n - 2)
                if there(it, n - 1):
                    weigh(it, n - 1)
                if there(it, n):
                    transpose_max(it, n)
                if b == 0 and group(it, G + 1):
                    transpose_context(it, G + 1)
                if there(it, n + 1):
                    transpose_keys(it, n + 1)
                if there(it, n):
                    shift(it, n)
                if there(it, n - 1):
                    transpose_heads(it, n - 1)
                if b == 3 and group(it, G + 2):
                    transpose_inputs(it, G + 2)

            pe.wait_ge(setup_steps, SETUP)
            pe.wait_ge(filled, 10)
            run(pe, slot)

        @block.scalar
        def _(act):
            def square(it, n):
                act.wait_ge(projected, it * 8 + (n + 1))
                if n > 0:
                    act.wait_ge(norms_done, it * 8 + n)
                act.activation(squares[:, 0:2 * P], PL[:, 0:2 * P], ACT.Square).then_inc(squares_done, 1)
                act.activation(squares[:, 2 * P:3 * P], PC[:, 0:P], ACT.Square).then_inc(squares_done, 1)

            def copy_values(it, n):
                if n - 3 > 0:
                    act.wait_ge(weighted, it * 8 + (n - 3))
                for i, src in ((1, PC[:, P:2 * P]), (0, PL[:, 2 * P:3 * P])):
                    act.activation(v[n % 4][:, i, :, 0:DL], src.rearrange("p (h d) -> p h d", h=HL), ACT.Copy)\
                        .then_inc(v_done, 1)

            def exps(it, n):
                act.wait_ge(shifted, it * 8 + (n + 1))
                if n - 1 > 0:
                    act.wait_ge(weighted, it * 8 + (n - 1))
                act.activation(probs[n % 2][:, 0, :], T[:, 0:2 * P], ACT.Exp, scale=DL ** -0.5).then_inc(exp_done, 1)
                act.activation(probs[n % 2][:, 1, :], T[:, 2 * P:4 * P], ACT.Exp, scale=DL ** -0.5,
                               bias=mask_cols[:, bass.ds(it * 8 + n, 1)]).then_inc(exp_done, 1)

            def key_hi(it, n):
                act.wait_ge(q_heads_done, it * 8 + (n + 1))
                if n - 1 > 0:
                    act.wait_ge(shifted, it * 8 + (n - 1))
                act.activation(k_hi[n % 2][:, :], KT[:, P:3 * P], ACT.Copy).then_inc(k_hi_done, 1)
                act.activation(q_hi[n % 2][:, :], q_heads[:, :, :].rearrange("p h q -> p (h q)"), ACT.Copy)\
                    .then_inc(q_hi_done, 1)

            def affine(it, G, i):
                act.wait_ge((x_transposed, c_transposed)[i], it * 2 + (G + 1))
                if 2 * G + i - 1 > 0:
                    act.wait_ge(hi_done, it * 4 + (2 * G + i - 1))
                if 2 * G + i - 1 > 0:
                    act.wait_ge(lo_done, it * 4 + (2 * G + i - 1))
                if i == 0:
                    act.activation(xf[:, :], TR[:, :], ACT.Identity, bias=lat_b, scale=lat_g).then_inc(affine_done, 1)
                else:
                    act.activation(cf[:, :], TR[0:kc, :], ACT.Identity, bias=ctx_b[0:kc, :], scale=ctx_g[0:kc, :])\
                        .then_inc(affine_done, 1)

            def slot(it, n):
                G, b = n // GB, n % GB
                if there(it, n + 2):
                    square(it, n + 2)
                    copy_values(it, n + 2)
                if b == 0 and group(it, G + 1):
                    affine(it, G + 1, 1)
                if there(it, n):
                    exps(it, n)
                if there(it, n + 1):
                    key_hi(it, n + 1)
                if there(it, n - 1):
                    act.wait_ge(o_transposed, it * 8 + n)
                    if n - 1 > 0:
                        act.wait_ge(out_projected, it * 8 + (n - 1))
                    act.activation(o_hi[:, :], M[:, 0:P], ACT.Copy).then_inc(o_hi_done, 1)
                if b == 3 and group(it, G + 2):
                    affine(it, G + 2, 0)

            act.wait_ge(filled, 10)
            run(act, slot)

        @block.vector
        def _(dve):
            def moments(it, G):
                if 2 * GB * G > 0:
                    dve.wait_ge(normal_done, it * (4 * GB) + (2 * GB * G))
                if 2 * GB * G > 0:
                    dve.wait_ge(mean_done, it * (4 * GB) + (2 * GB * G))
                if G > 0:
                    dve.wait_ge(rstd_done, it * 2 + G)
                dve.wait_ge(ctx_loaded, it * 32 + (16 * (G + 1)))
                for b in range(GB):
                    dve.bn_stats(stats[:, b, :], ctx_in[:, b, :]).then_inc(stats_done, 1)
                    dve.bn_stats(stats[:, GB + b, :], batch_columns(X, it, GB * G + b)).then_inc(stats_done, 1)
                dve.wait_ge(stats_done, it * (4 * GB) + (2 * GB * (G + 1)))
                dve.sem_inc(passed, 1)
                for b in range(2 * GB):
                    dve.bn_aggr(mean_var[:, b, :], stats[:, b, :]).then_inc(mean_done, 1)

            def normal(it, G):
                dve.wait_ge(rstd_done, it * 2 + (G + 1))
                dve.wait_ge(mean_done, it * (4 * GB) + (2 * GB * (G + 1)))
                if G > 0:
                    dve.wait_ge(c_transposed, it * 2 + G)
                for b in range(GB):
                    dve.tensor_scalar(xn[:, b, :], batch_columns(X, it, GB * G + b), mean_var[:, GB + b, 0:1],
                                      rstd[:, GB + b:GB + b + 1], ALU.subtract, ALU.mult).then_inc(normal_done, 1)
                    dve.tensor_scalar(cn[:, b, :], ctx_in[:, b, :], mean_var[:, b, 0:1],
                                      rstd[:, b:b + 1], ALU.subtract, ALU.mult).then_inc(normal_done, 1)

            def input_hi(it, G, i):
                dve.wait_ge(affine_done, it * 4 + (2 * G + i + 1))
                if GB * (G - 1) > 0:
                    dve.wait_ge(projected, it * 8 + (GB * (G - 1)))
                out, src = ((x_hi, xf), (c_hi, cf))[i]
                dve.tensor_copy(out[G % 2][:, :], src[:, :]).then_inc(hi_done, 1)

            def sum_squares(it, n):
                dve.wait_ge(squares_done, it * 16 + (2 * n + 2))
                if n > 0:
                    dve.wait_ge(norms_bounded, it * 8 + n)
                dve.tensor_reduce(norms[:, :], squares[:, :].rearrange("p (h d) -> p h d", d=DL), AX.X, ALU.add)\
                    .then_inc(norms_done, 1)
                dve.wait_ge(norms_done, it * 8 + (n + 1))
                if n > 0:
                    dve.wait_ge(inverse_done, it * 8 + n)
                dve.tensor_scalar(norms_kept[:, :], norms[:, :], 1.0 / DL, RMS_EPS ** 2, ALU.mult, ALU.max)\
                    .then_inc(norms_bounded, 1)

            def normalise(it, n):
                dve.wait_ge(inverse_done, it * 8 + (n + 1))
                dve.wait_ge(v_done, it * 16 + (2 * n + 2))
                if n - 1 > 0:
                    dve.wait_ge(keys_transposed, it * 8 + (n - 1))
                for lo, hi, src in ((0, 2, PL[:, 0:2 * P]), (2, 3, PC[:, 0:P])):
                    dve.tensor_tensor(unit[n % 2][:, lo:hi, :].rearrange("p a (h d) -> p (a h) d", d=DL),
                                      src.rearrange("p (h d) -> p h d", d=DL),
                                      inverse[:, HL * lo:HL * hi].unsqueeze(2).broadcast_to([P, HL * (hi - lo), DL]),
                                      ALU.mult).then_inc(unit_done, 1)

            def split_heads(it, n):
                dve.wait_ge(keys_transposed, it * 8 + (n + 1))
                if n > 0:
                    dve.wait_ge(q_lo_done, it * 8 + n)
                dve.tensor_tensor(q_heads[:, :, :], KT[:, 0:P].unsqueeze(1).broadcast_to([P, HL, P]),
                                  head_gamma[:, :].unsqueeze(2).broadcast_to([P, HL, P]), ALU.mult)\
                    .then_inc(q_heads_done, 1)

            def slot(it, n):
                G, b = n // GB, n % GB
                now, old = there(it, n), there(it, n - 1)
                if now:
                    dve.wait_ge(scored, it * 8 + (n + 1))
                    if n > 0:
                        dve.wait_ge(max_transposed, it * 8 + n)
                    dve.tensor_reduce(maxes[:, 0:HL], S[:, :].rearrange("p (h k) -> p h k", h=HL), AX.X, ALU.max,
                                      negate=True).then_inc(max_done, 1)
                if there(it, n - 2):
                    dve.wait_ge(out_projected, it * 8 + (n - 1))
                    dve.wait_ge(normal_done, it * (4 * GB) + (2 * GB * ((n - 2) // GB + 1)))
                    x = batch_columns(X, it, n - 2)
                    dve.tensor_tensor(x, M[:, 0:P], x, ALU.add).then_inc(m_read, 1)
                if there(it, n + 2):
                    sum_squares(it, n + 2)
                if now:
                    dve.wait_ge(max_transposed, it * 8 + (n + 1))
                    if n > 0:
                        dve.wait_ge(shifted, it * 8 + n)
                    dve.tensor_tensor(neg_max[:, :, :], M[0:32, 0:P].unsqueeze(1).broadcast_to([32, HL, P]),
                                      diag.unsqueeze(2).broadcast_to([32, HL, P]), ALU.mult).then_inc(m_read, 1)
                if there(it, n + 1):
                    split_heads(it, n + 1)
                if old:
                    dve.wait_ge(weighted, it * 8 + n)
                    if n - 1 > 0:
                        dve.wait_ge(heads_done, it * 8 + (n - 1))
                    if n - 1 > 0:
                        dve.wait_ge(o_transposed, it * 8 + (n - 1))
                    o = O[:, 0:HL * (DL + 1)].rearrange("p (h c) -> p h c", h=HL)
                    dve.reciprocal(recip[:, :], o[:, :, DL]).then_inc(recip_done, 1)
                    dve.wait_ge(recip_done, it * 8 + n)
                    dve.tensor_tensor(heads[:, :, :], o[:, :, 0:DL], recip[:, :].unsqueeze(2).broadcast_to([P, HL, DL]),
                                      ALU.mult).then_inc(heads_done, 1)
                if there(it, n + 2):
                    normalise(it, n + 2)
                if there(it, n + 1):
                    dve.wait_ge(k_hi_done, it * 8 + (n + 2))
                    if n > 0:
                        dve.wait_ge(shifted, it * 8 + n)
                    dve.tensor_tensor(k_lo[(n + 1) % 2][:, :], KT[:, P:3 * P], k_hi[(n + 1) % 2][:, :].bitcast(F32),
                                      ALU.subtract).then_inc(k_lo_done, 1)
                if old:
                    dve.wait_ge(o_hi_done, it * 8 + n)
                    dve.tensor_tensor(o_lo[:, :], M[:, 0:P], o_hi[:, :].bitcast(F32), ALU.subtract).then_inc(m_read, 1)
                if b == 3 and group(it, G + 2):
                    normal(it, G + 2)
                if b == 1 and group(it, G + 1):
                    input_hi(it, G + 1, 0)
                    input_hi(it, G + 1, 1)
                if b == 2 and group(it, G + 2):
                    moments(it, G + 2)

            dve.wait_ge(ready["xattn1"], 48)
            dve.tensor_copy(w_hi[:, :], raw[:, :]).then_inc(setup_steps, 1)
            dve.tensor_tensor(gamma[:, :], q_gamma, k_gamma, ALU.mult).then_inc(setup_steps, 1)
            for out, src in ((mask_rows, sb["mask_by_row"]), (mask_cols, sb["mask_by_col"])):
                dve.tensor_scalar(out[:, :], src[:, :], -1.0, -MASKED, ALU.add, ALU.mult).then_inc(setup_steps, 1)
            dve.wait_ge(setup_steps, 4)
            dve.tensor_tensor(w_lo[:, :], raw[:, :], w_hi[:, :].bitcast(F32), ALU.subtract).then_inc(setup_steps, 1)
            dve.tensor_scalar(head_gamma[:, :], head_rows, gamma[:, :], None, ALU.mult).then_inc(setup_steps, 1)
            run(dve, slot)

        @block.gpsimd
        def _(pool):
            def reciprocal_deviations(it, G):
                base = 5 * G
                pool.wait_ge(mean_done, it * (4 * GB) + (2 * GB * (G + 1)))
                if 2 * GB * G > 0:
                    pool.wait_ge(normal_done, it * (4 * GB) + (2 * GB * G))
                if G > 0:
                    pool.wait_ge(rstd_done, it * 2 + G)
                pool.sem_inc(passed, 1)
                pool.tensor_scalar(var_eps[:, :], mean_var[:, :, 1], LN_EPS, 1.0, ALU.add, ALU.mult)\
                    .then_inc(rstd_steps, 1)
                pool.wait_ge(rstd_steps, it * 10 + (base + 1))
                pool.tensor_tensor(rstd[:, :], var_eps[:, :], power[:, :], ALU.pow).then_inc(rstd_steps, 1)
                pool.wait_ge(rstd_steps, it * 10 + (base + 2))
                pool.tensor_tensor(once[:, 0:GB], mean_var[:, GB:, 1], rstd[:, GB:], ALU.mult).then_inc(rstd_steps, 1)
                pool.wait_ge(rstd_steps, it * 10 + (base + 3))
                pool.tensor_tensor(twice[:, :], once[:, 0:GB], rstd[:, GB:], ALU.mult).then_inc(rstd_steps, 1)
                pool.wait_ge(rstd_steps, it * 10 + (base + 4))
                pool.sem_inc(passed, 1)
                pool.tensor_scalar(twice_eps[:, :], twice[:, :], LN_EPS, 1.0, ALU.add, ALU.mult).then_inc(rstd_steps, 1)
                pool.wait_ge(rstd_steps, it * 10 + (base + 5))
                if G > 0:
                    pool.wait_ge(rstd_done, it * 2 + G)
                pool.tensor_tensor(again[:, :], twice_eps[:, :], power[:, 0:GB], ALU.pow).then_inc(again_done, 1)
                pool.wait_ge(again_done, it * 2 + (G + 1))
                pool.tensor_tensor(rstd[:, GB:], rstd[:, GB:], again[:, :], ALU.mult).then_inc(rstd_done, 1)

            def input_lo(it, G, i):
                pool.wait_ge(hi_done, it * 4 + (2 * G + i + 1))
                if GB * (G - 1) > 0:
                    pool.wait_ge(projected, it * 8 + (GB * (G - 1)))
                out, src, hi = ((x_lo, xf, x_hi), (c_lo, cf, c_hi))[i]
                pool.tensor_tensor(out[G % 2][:, :], src[:, :], hi[G % 2][:, :].bitcast(F32), ALU.subtract)\
                    .then_inc(lo_done, 1)

            def slot(it, n):
                G, b = n // GB, n % GB
                if there(it, n + 2):
                    pool.wait_ge(norms_bounded, it * 8 + (n + 3))
                    if 2 * (n + 2) > 0:
                        pool.wait_ge(unit_done, it * 16 + (2 * (n + 2)))
                    pool.tensor_tensor(inverse[:, :], norms_kept[:, :], power[:, 0:3 * HL], ALU.pow)\
                        .then_inc(inverse_done, 1)
                if there(it, n + 1):
                    pool.wait_ge(q_hi_done, it * 8 + (n + 2))
                    if n > 0:
                        pool.wait_ge(shifted, it * 8 + n)
                    pool.tensor_tensor(q_lo[(n + 1) % 2][:, :], q_heads[:, :, :].rearrange("p h q -> p (h q)"),
                                       q_hi[(n + 1) % 2][:, :].bitcast(F32), ALU.subtract).then_inc(q_lo_done, 1)
                if b == 1 and group(it, G + 1):
                    input_lo(it, G + 1, 0)
                    input_lo(it, G + 1, 1)
                if b == 2 and group(it, G + 2):
                    reciprocal_deviations(it, G + 2)

            pool.sem_clear(used_before)
            pool.memset(power[:, :], -0.5).then_inc(filled, 1)
            pool.memset(maxes[:, :], 0.0).then_inc(filled, 1)
            for x in v:
                pool.memset(x[:, :, :, DL:DL + 1], 1.0).then_inc(filled, 2)
            pool.wait_ge(filled, 10)
            run(pool, slot)

        @block.sync
        def _(sp):
            sp.wait_ge(ready["ffn0"], 16)
            sp.dma_start(sb["raw_ffn1"][:, :], t["w_ffn1"]).then_inc(ready["ffn1"], 16)
            sp.dma_start(ctx_in[:, :, :], t["ctx_768"][0:GB, :, :].rearrange("b p d -> p b d")).then_inc(ctx_loaded, 16)
            with sp.Fori(1, NG) as G:
                sp.wait_ge(normal_done, G * (2 * GB))
                sp.dma_start(ctx_in[:, :, :], t["ctx_768"][bass.ds(G * GB, GB), :, :].rearrange("b p d -> p b d"))\
                    .then_inc(ctx_loaded, 16)


def store(nc, sb, out, sem):
    stored = sem("stored")
    with nc.Block() as block:
        @block.sync
        def _(sp):
            sp.dma_start(out.rearrange("b p d -> p b d"), sb["x"][:, :].rearrange("p (b d) -> p b d", d=D))\
                .then_inc(stored, 16)
            sp.wait_ge(stored, 16)


def decoder(nc, t, out):
    with ExitStack() as ctx:
        def buf(name, shape, dt=F32):
            return ctx.enter_context(nc.sbuf_tensor(name, shape, dt))

        def sem(name):
            return ctx.enter_context(nc.semaphore(name))

        sb = {
            "x": buf("x_all", [P, B * D]),
            "const_r": buf("const_r", [P, N_CONST_R], F32R),
            "ident": buf("ident", [P, P]),
            "const": buf("const", [P, N_CONST - N_CONST_R]),
            "cols": buf("cols", [P, N_COLS]),
            "rows": buf("rows", [P, N_ROWS]),
            "rows_hi": buf("rows_hi", [P, N_ROWS], F32R),
            "rows_lo": buf("rows_lo", [P, N_ROWS], F32R),
        }
        sb["raw_xattn1"] = buf("raw_xattn1", [P, W_LATENT])
        sb["mask_by_row"] = buf("mask_by_row", [P, B * P], U8)
        sb["mask_by_col"] = buf("mask_by_col", [P, B], U8)
        ps = [ctx.enter_context(nc.psum_tensor(f"bank{i}", [P, 512], F32)) for i in range(8)]
        ready = {name: sem(f"{name}_weights_in") for name in ("ffn0", "xattn1", "ffn1")}
        with ExitStack() as early:
            def buf(name, shape, dt=F32):
                return early.enter_context(nc.sbuf_tensor(name, shape, dt))

            sb.update({
                "w_hi": buf("w_hi", [P, N_WEIGHTS], F32R),
                "w_lo": buf("w_lo", [P, N_WEIGHTS], F32R),
                "raw_ffn0": buf("raw_ffn0", [P, W_FFN0]),
                "v": [buf(f"values{i}", [P, GB, H, VW]) for i in range(2)],
                "units": [buf(f"unit{i}", [P, U, P], F32R) for i in range(12)],
                "maxes": buf("maxes", [P, U, 32]),
            })
            load_setup(nc, t["x"], t["weights"], t["cols"], t["rows"], t["consts"],
                       [("ffn0", "raw_ffn0", t["w_ffn0"]), ("xattn1", "raw_xattn1", t["w_xattn1"]),
                        ("xattn1", "mask_by_row", t["mask_by_row"]), ("xattn1", "mask_by_col", t["mask_by_col"])],
                       sb, sem, ready)
            attention(nc, 0, "self", sb, ps)
            attention(nc, 1, "cross", sb, ps, t["ctx_768"])
            gated_experts(nc, 2, sb, ps, ready)
            attention(nc, 3, "causal", sb, ps)
        sb["raw_ffn1"] = ctx.enter_context(nc.sbuf_tensor("raw_ffn1", [P, W_FFN1], F32))
        latent_attention(nc, 4, sb, ps, t, ready)
        relu_experts(nc, 5, sb, ps, ready)
        store(nc, sb, out, sem)


def shape_constants():
    c = np.zeros((P, N_CONST), np.float32)
    eye = np.eye(P, dtype=np.float32)
    c[:, C_ID:C_ID + P] = eye
    for u in range(U):
        c[32 * u:32 * u + 32, C_ONES + u * P:C_ONES + (u + 1) * P] = 1.0
        for g in range(U):
            c[32 * u + g, C_DIAG + g] = 1.0
            c[32 * u + DH * g:32 * u + DH * (g + 1), C_SLOT + g] = 1.0
    e = np.arange(E0)
    c[:, C_EARLIER:C_EARLIER + E0 * E0] = (e[None, :] < e[:, None]).astype(np.float32).reshape(1, -1)
    for h in range(2):
        c[h * P // 2:(h + 1) * P // 2, C_HEAD + h] = 1.0
    for e in range(E1):
        c[e, C_ONE_ROW + e * P:C_ONE_ROW + (e + 1) * P] = 1.0
    for k in range(E0 // 2):
        c[2 * k, C_PAIR + k * P:C_PAIR + k * P + P // 2] = 1.0
        c[2 * k + 1, C_PAIR + k * P + P // 2:C_PAIR + (k + 1) * P] = 1.0
    hidden = np.triu(np.ones((P, P), np.float32), 1) * np.float32(MASKED)
    c[:, C_MASK:C_MASK + P] = hidden
    c[:, C_MASK + P:C_MASK + 2 * P] = hidden.T
    rate = (np.float32(1.0) / np.float32(10000.0) ** (np.arange(0, DH, 2, dtype=np.float32) / np.float32(DH)))
    ch = np.arange(D)
    angle = (rate[ch % (DH // 2)][:, None] * np.arange(P, dtype=np.float32)[None, :]).astype(np.float32)
    sign = np.where(ch % DH < DH // 2, -1, 1).astype(np.float32)[:, None]
    c[:, C_ROPE:C_ROPE + P] = np.cos(angle)
    c[:, C_ROPE + P:C_ROPE + 2 * P] = sign * np.sin(angle)
    angle = (rate[ch % DH // 2] * (ch // DH).astype(np.float32)).astype(np.float32)
    sign = np.where(ch % 2 == 0, -1, 1).astype(np.float32)
    for n, table in enumerate((np.cos(angle), sign * np.sin(angle))):
        c[:, C_TURN + n * P:C_TURN + (n + 1) * P] = table[None, :]
        c[:, C_TURN_COL + n] = table
    return c


def packed(i):
    ch = np.arange(D)
    half = ch // DH * DH + (ch % DH + DH // 2) % DH
    pair = ch ^ 1
    rows_of = lambda v: np.broadcast_to(v, (P, len(v)))
    pad = lambda w: np.concatenate([w, np.zeros((P - len(w),) + w.shape[1:], w.dtype)])
    wq, wk, wv, wo = (i["L0_attn_" + n].T for n in ("Wq", "Wk", "Wv", "Wo"))
    bq, bk = i["L0_attn_bq"], i["L0_attn_bk"]
    w = [wq, wq[:, half], wk, wk[:, half], wv, wo]
    cols = [bq, bq[half], bk, bk[half]]
    rows = [i["L0_attn_bv"], i["L0_attn_bo"]]
    xq, xk, xv, xo = (i["L0_xattn_" + n] for n in ("Wq", "Wk", "Wv", "Wo"))
    w += [xq, xq, pad(xk), pad(xk), pad(xv), xo]
    cols += [i["L0_xattn_bq"]] * 2 + [i["L0_xattn_bk"]] * 2
    rows += [i["L0_xattn_bv"], i["L0_xattn_bo"]]
    q, k, v = (i["L1_attn_W_attn"][:, n * D:(n + 1) * D] for n in range(3))
    bq, bk, bv = (i["L1_attn_b_attn"][n * D:(n + 1) * D] for n in range(3))
    w += [q, q[:, pair], k, k[:, pair], v, i["L1_attn_W_proj"]]
    cols += [bq, bq[pair], bk, bk[pair]]
    rows += [bv, i["L1_attn_b_proj"]]
    rows += [i["L0_ffn_router_b"], i["L1_ffn_router_b"]]
    twice = lambda v: np.concatenate([v, v])
    xa = {n: i["L1_xattn_" + n] for n in ("ln_x_g", "ln_x_b", "ln_l_g", "ln_l_b", "qn_g", "kn_g", "Wq", "Wkv", "Wlkv", "Wo", "bo")}
    cols += [pad(xa["ln_x_g"]), pad(xa["ln_x_b"]), xa["ln_l_g"], xa["ln_l_b"], twice(xa["qn_g"]), twice(xa["kn_g"])]
    rows += [xa["bo"]]
    w_xattn1 = np.concatenate([xa["Wq"].T, xa["Wlkv"].T, pad(xa["Wkv"].T), xa["Wo"].T], 1)
    mask = i["mask_BxS2_bk0"]
    cols += list(i["L1_ffn_b1"].reshape(E1 * C1, P))
    w_ffn1 = np.concatenate([i["L1_ffn_w1"].transpose(1, 0, 2).reshape(D, E1 * F1),
                             i["L1_ffn_w2"].reshape(E1 * C1, P, D).transpose(1, 0, 2).reshape(P, -1),
                             pad(i["L1_ffn_b2"]), i["L1_ffn_router_w"]], 1)

    def experts(routed, shared):
        both = np.concatenate([i["L0_ffn_routed_" + routed], i["L0_ffn_shared_" + shared]])
        return both.transpose(1, 0, 2).reshape(D, -1)

    w2 = np.concatenate([i["L0_ffn_routed_w2"], i["L0_ffn_shared_w2"]]).reshape(-1, P, D)
    w_ffn0 = np.concatenate([experts("w1", "w1"), experts("w3", "w3"), w2.transpose(1, 0, 2).reshape(P, -1),
                             i["L0_ffn_router_w"]], 1)
    return {
        "w_xattn1": w_xattn1,
        "mask_by_row": rows_of(mask.reshape(-1)), "mask_by_col": mask.T,
        "w_ffn0": w_ffn0, "w_ffn1": w_ffn1,
        "x": i["x"], "ctx_768": i["ctx_768"],
        "weights": np.concatenate(w, 1),
        "cols": np.stack(cols, 1),
        "rows": np.concatenate([rows_of(r) for r in rows], 1),
        "consts": shape_constants(),
    }


def kernel(**inputs):
    import concourse.bacc as bacc
    from concourse.bass_utils import run_bass_kernel_spmd

    nc = bacc.Bacc("TRN2", target_bir_lowering=False, num_devices=1)
    arrays, drams = {}, {}
    for name, a in packed({k: np.asarray(v) for k, v in inputs.items()}).items():
        a = np.ascontiguousarray(a)
        arrays[f"in_{name}"] = a
        drams[name] = nc.dram_tensor(f"in_{name}", a.shape, mybir.dt.from_np(a.dtype), kind="ExternalInput").ap()
    out = nc.dram_tensor("out_x", (B, P, D), F32, kind="ExternalOutput").ap()
    decoder(nc, drams, out)
    result = run_bass_kernel_spmd(nc, [arrays], core_ids=[0])
    return result.results[0]["out_x"]
```

```python
from contextlib import ExitStack

import numpy as np

import concourse.bass as bass
from concourse import mybir

F32, F32R, U8, I32 = mybir.dt.float32, mybir.dt.float32r, mybir.dt.uint8, mybir.dt.int32
ACT, ALU, AX = mybir.ActivationFunctionType, mybir.AluOpType, mybir.AxisListType

P = 128
B, D, DC = 32, 128, 96
H, DH = 16, 8
GB = 4
NG = B // GB
GT = GB * P
E0 = 8
W_FFN0 = 3 * (E0 // 2 + 1) * P + E0
U = 4
VW = 64
LN_EPS = 1e-5
RMS_EPS = 1e-8
CLAMP = 1e4
MASKED = -1e30

E1, F1 = 8, 512
C1 = F1 // P
W_LATENT = 6 * P
W_FFN1 = (2 * E1 * C1 + 1) * P + E1

AW = ["q", "q2", "k", "k2", "v", "o"]
ATT = {"self": 0, "cross": 1, "causal": 2}
N_WEIGHTS = 3 * len(AW) * P
COL_LATENT = 3 * 4
COL_V0 = COL_LATENT + 6
N_COLS = COL_V0 + 1 + E1 * C1
N_ROWS_R = 4 * P
R_LATENT = 3 * P
R_VALUES = N_ROWS_R
R_ROUTER0 = R_VALUES + 3 * P
R_ROUTER1 = R_ROUTER0 + E0
N_ROWS = R_ROUTER1 + E1

C_ID, C_ONES, C_MASK = 0, P, 5 * P
C_PAIR = C_MASK + 2 * P
C_ONE_ROW = C_PAIR + (E0 // 2) * P
N_CONST_R = C_ONE_ROW + E1 * P
C_DIAG = N_CONST_R
C_SLOT = C_DIAG + 4
C_ROPE = C_SLOT + 4
C_TURN = C_ROPE + 2 * P
C_TURN_COL = C_TURN + 2 * P
C_EARLIER = C_TURN_COL + 2
C_HEAD = C_EARLIER + E0 * E0
N_CONST = C_HEAD + 2


PHASE_SEMS = 48


def phase_semaphores(nc, ctx, phase, kind):
    numbers = sorted(nc.free_semaphores)[-2 * PHASE_SEMS:]
    own, other = (numbers[i * PHASE_SEMS:(i + 1) * PHASE_SEMS] for i in (phase % 2, 1 - phase % 2))
    free = iter(own)

    def sem(name):
        return ctx.enter_context(nc.semaphore(f"{kind}_{name}", num=next(free)))

    return sem, range(other[0], other[-1] + 1)


def batch_columns(tile, it, n):
    return tile[:, bass.ds(it * (8 * P) + n * P, P)]


def load_setup(nc, x, weights, cols, rows, consts, later, sb, sem, ready):
    with ExitStack() as ctx:
        staged = ctx.enter_context(nc.sbuf_tensor("staged_consts", [P, N_CONST_R], F32))
        staged_w = ctx.enter_context(nc.sbuf_tensor("staged_weights", [P, N_WEIGHTS], F32))
        block = ctx.enter_context(nc.Block())
        consts_in, weights_in, rows_in, x_in = sem("consts_in"), sem("weights_in"), sem("rows_in"), sem("x_in")
        split, values_zero = sem("weights_hi_done"), sem("values_zero")
        turned = sem("weights_turned")

        @block.sync
        def _(sp):
            def load_group(sp, G, done):
                sp.dma_start(sb["x"][:, G * GT:(G + 1) * GT].rearrange("p (b d) -> p b d", d=D),
                             x[G * GB:(G + 1) * GB].rearrange("b p d -> p b d")).then_inc(done, 16)

            sp.dma_start(staged[:, :], consts[:, 0:N_CONST_R]).then_inc(consts_in, 16)
            load_group(sp, 0, x_in)
            sp.dma_start(staged_w[:, :], weights).then_inc(weights_in, 16)
            load_group(sp, 1, x_in)
            for G in range(2, NG):
                load_group(sp, G, ready["x"])
            for name, tile, src in later:
                sp.dma_start(sb[tile][:, :], src).then_inc(ready[name], 16)
            sp.wait_ge(x_in, 32)

        @block.gpsimd
        def _(pool):
            pool.memset(sb["maxes"][:, :, :], 0.0)
            for z in sb["units"]:
                pool.memset(z[:, :, :].bitcast(F32), 0.0)
            for v in sb["v"]:
                pool.memset(v[:, :, :, :], 0.0).then_inc(values_zero, 1)
            pool.wait_ge(values_zero, 2)
            for v in sb["v"]:
                for j in range(U):
                    pool.memset(v[:, :, j:H:U, 32 + j], 1.0)

        @block.scalar
        def _(act):
            act.dma_start(sb["const"][:, :], consts[:, N_CONST_R:N_CONST]).then_inc(rows_in, 16)
            act.dma_start(sb["cols"][:, :], cols).then_inc(rows_in, 16)
            act.dma_start(sb["rows"][:, :], rows).then_inc(rows_in, 16)
            act.wait_ge(consts_in, 16)
            act.activation(sb["const_r"][:, :], staged[:, :], ACT.Copy)
            act.activation(sb["ident"][:, :], staged[:, C_ID:C_ID + P], ACT.Copy)

        @block.vector
        def _(dve):
            dve.wait_ge(weights_in, 16)
            dve.wait_ge(rows_in, 48)
            table = lambda c, n: sb["const"][:, c - N_CONST_R:c - N_CONST_R + n]
            made = 0
            for name in "qk":
                c = (ATT["causal"] * len(AW) + AW.index(name)) * P
                w, partner = staged_w[:, c:c + P], staged_w[:, c + P:c + 2 * P]
                c = ATT["causal"] * 4 + AW.index(name)
                bias, partner_bias = sb["cols"][:, c:c + 1], sb["cols"][:, c + 1:c + 2]
                dve.tensor_tensor(w, w, table(C_TURN, P), ALU.mult).then_inc(turned, 1)
                dve.tensor_tensor(partner, partner, table(C_TURN + P, P), ALU.mult).then_inc(turned, 1)
                dve.tensor_tensor(bias, bias, table(C_TURN_COL, 1), ALU.mult).then_inc(turned, 1)
                dve.tensor_tensor(partner_bias, partner_bias, table(C_TURN_COL + 1, 1), ALU.mult).then_inc(turned, 1)
                made += 4
                dve.wait_ge(turned, made)
                dve.tensor_tensor(w, w, partner, ALU.add).then_inc(turned, 1)
                dve.tensor_tensor(bias, bias, partner_bias, ALU.add).then_inc(turned, 1)
                made += 2
            dve.wait_ge(turned, made)
            dve.tensor_copy(sb["w_hi"][:, :], staged_w[:, :]).then_inc(split, 1)
            dve.tensor_copy(sb["rows_hi"][:, :], sb["rows"][:, 0:N_ROWS_R]).then_inc(split, 1)
            dve.wait_ge(split, 2)
            dve.tensor_tensor(sb["w_lo"][:, :], staged_w[:, :], sb["w_hi"][:, :].bitcast(F32), ALU.subtract)
            dve.tensor_tensor(sb["rows_lo"][:, :], sb["rows"][:, 0:N_ROWS_R], sb["rows_hi"][:, :].bitcast(F32), ALU.subtract)


def attention(nc, phase, kind, sb, ps, context=None, x_ready=None):
    rope, cross, causal = kind == "self", kind == "cross", kind == "causal"
    clip = cross
    a = ATT[kind]
    kc = DC if kind == "cross" else D
    scale = float(DH) ** -0.5
    pieces = ["q", "q2", "k", "k2", "v"] if rope else ["q", "k", "v"]
    NP = len(pieces)

    def weight(name, rows=P):
        c = (a * len(AW) + AW.index(name)) * P
        return sb["w_hi"][0:rows, c:c + P], sb["w_lo"][0:rows, c:c + P]

    def bias(name):
        c = a * 4 + AW.index(name)
        return sb["cols"][:, c:c + 1]

    cr = sb["const_r"]
    ident_r = cr[:, C_ID:C_ID + P]
    c_rope = C_ROPE - N_CONST_R
    cos, sin = sb["const"][:, c_rope:c_rope + P], sb["const"][:, c_rope + P:c_rope + 2 * P]
    diag, slots = sb["const"][:, 0:U], sb["const"][:, U:2 * U]
    bv = sb["rows"][:, R_VALUES + a * P:R_VALUES + (a + 1) * P]
    bo_hi, bo_lo = (sb[r][:, a * P:(a + 1) * P] for r in ("rows_hi", "rows_lo"))
    X = sb["x"]
    S, T, OT, PJ, O, TR = ps[0:2], ps[2:4], ps[4], ps[5], ps[6], ps[7]
    V, maxes = sb["v"], sb["maxes"]
    unit_q, unit_k_hi, unit_k_lo = (sb["units"][4 * i:4 * i + 4] for i in range(3))

    tr_turn, pj_turn = {}, {}
    for n in range(-6, B + 2):
        G, b = n // GB, n % GB
        if clip and n - 2 >= 0:
            tr_turn["y", n - 2] = len(tr_turn)
        if b == 2 and G + 2 < NG:
            tr_turn["x", G + 2] = len(tr_turn)
        if cross and b == 3 and G + 2 < NG:
            tr_turn["c", G + 2] = len(tr_turn)
        if rope and b == 3 and G + 2 < NG:
            pj_turn["q2", G + 2] = len(pj_turn)
        if rope and b == 0 and 0 <= G + 1 < NG:
            pj_turn["k2", G + 1] = len(pj_turn)
        if not clip and n - 2 >= 0:
            tr_turn["y", n - 2] = len(tr_turn)
        if 0 <= n - 1 < B:
            tr_turn["o", n - 1] = len(tr_turn)
        if b == 2 and G + 2 < NG:
            pj_turn["q", G + 2] = len(pj_turn)
        if b == 3 and G + 2 < NG:
            pj_turn["k", G + 2] = len(pj_turn)
        if b == 0 and 0 <= G + 1 < NG:
            pj_turn["v", G + 1] = len(pj_turn)
    TR8, PJ8 = 16 + (4 if cross else 2), 2 * NP

    with ExitStack() as ctx:
        def buf(name, shape, dt=F32):
            return ctx.enter_context(nc.sbuf_tensor(f"{kind}_{name}", shape, dt))

        sem, used_before = phase_semaphores(nc, ctx, phase, kind)
        stats, mean_var = buf("stats", [P, GB, 6]), buf("mean_var", [P, GB, 2])
        var_eps, rstd, power = buf("var_eps", [P, GB]), buf("rstd", [P, GB]), buf("power", [P, GB])
        xn = buf("xn", [P, GB, D])
        x_hi, x_lo = buf("x_hi", [P, GT], F32R), buf("x_lo", [P, GT], F32R)
        if cross:
            ctx_in = buf("ctx_in", [P, GB, DC])
            c_hi, c_lo = buf("c_hi", [DC, GT], F32R), buf("c_lo", [DC, GT], F32R)
        else:
            c_hi, c_lo = x_hi, x_lo
        if rope:
            by_cos = [buf(f"by_cos{i}", [P, GB, P]) for i in range(2)]
            by_sin = [buf(f"by_sin{i}", [P, GB, P]) for i in range(2)]
            turned = [buf(f"turned{i}", [P, GT]) for i in range(2)]
        qk_hi = [[buf(f"qk_hi{i}{j}", [P, GT], F32R) for j in range(2)] for i in range(2)]
        qk_lo = [[buf(f"qk_lo{i}{j}", [P, GT], F32R) for j in range(2)] for i in range(2)]
        q_hi_m = [buf(f"q_hi_m{j}", [P, U, P], F32R) for j in range(2)]
        q_lo_m = [buf(f"q_lo_m{j}", [P, U, P], F32R) for j in range(2)]
        k_hi_m = [buf(f"k_hi_m{j}", [P, U, P], F32R) for j in range(2)]
        sums = buf("sums", [P, 2 * P])
        neg_max = [buf(f"neg_max{j}", [P, U, P], F32R) for j in range(2)]
        probs = [buf(f"probs{j}", [P, U, U, P]) for j in range(2)]
        recip = [buf(f"recip{j}", [P, U, U]) for j in range(2)]
        heads = [buf(f"heads{j}", [P, U, U, DH]) for j in range(2)]
        o_hi = [buf(f"o_hi{j}", [P, P], F32R) for j in range(2)]
        o_lo = [buf(f"o_lo{j}", [P, P], F32R) for j in range(2)]

        x_transposed, c_transposed = sem("x_transposed"), sem("c_transposed")
        projected = sem("projected")
        sums_transposed = sem("sums_transposed")
        scored = sem("scored")
        keyed = sem("keyed")
        shifted = sem("shifted")
        max_transposed = sem("max_transposed")
        weighted = sem("weighted")
        o_transposed = sem("o_transposed")
        out_projected = sem("out_projected")
        x_hi_done, c_hi_done = sem("x_hi_done"), sem("c_hi_done")
        qk_hi_done = sem("qk_hi_done")
        sums_done = sem("sums_done")
        exp_done = sem("exp_done")
        o_hi_done = sem("o_hi_done")
        stats_done, mean_done, xn_done = sem("stats_done"), sem("mean_done"), sem("xn_done")
        tr_read, pj_read = sem("tr_read"), sem("pj_read")
        max_done, max_clipped = sem("max_done"), sem("max_clipped")
        clipped = sem("clipped")
        neg_max_done, lo_summed, x_kept = sem("neg_max_done"), sem("lo_summed"), sem("x_kept")
        recip_done, heads_done = sem("recip_done"), sem("heads_done")
        power_done, var_done, rstd_done = sem("power_done"), sem("var_done"), sem("rstd_done")
        turned_done, qk_lo_done = sem("turned_done"), sem("qk_lo_done")
        k_masked, q_masked = sem("k_masked"), sem("q_masked")
        spread_done = sem("spread_done")
        ctx_loaded = sem("ctx_loaded")
        passed = sem("passed")

        block = ctx.enter_context(nc.Block())

        def run(engine, slot):
            for n in range(-6, 2):
                slot(0, n)
            with engine.Fori(0, 3) as it:
                for n in range(2, 10):
                    slot(it, n)
            for n in range(26, B + 2):
                slot(0, n)

        def there(it, n):
            return not isinstance(it, int) or 0 <= n < B

        def group(it, G):
            return not isinstance(it, int) or 0 <= G < NG

        @block.tensor
        def _(pe):
            def split_matmul(out, l, r, start=True, stop=True):
                pe.matmul(out, l[0], r[0], start=start, stop=False)
                pe.matmul(out, l[0], r[1], start=False, stop=False)
                return pe.matmul(out, l[1], r[0], start=False, stop=stop)

            def scores(it, n, u):
                if u == 0:
                    pe.wait_ge(k_masked, it * 8 + (n + 1))
                    pe.wait_ge(spread_done, it * 96 + (12 * (n + 1)))
                if 4 * n + u - 1 > 0:
                    pe.wait_ge(max_done, it * 32 + (4 * n + u - 1))
                mm = pe.matmul(S[u % 2][:, :].rearrange("p (j k) -> p j k", j=U), unit_q[n % 4][:, u, :],
                               k_hi_m[n % 2][:, :, :], start=True, stop=not causal)
                if causal:
                    mm = pe.matmul(S[u % 2][:, :].rearrange("p (j k) -> p j k", j=U), ident_r,
                                   cr[:, C_MASK:C_MASK + P].unsqueeze(1).broadcast_to([P, U, P]),
                                   start=False, stop=True)
                mm.then_inc(scored, 1)

            def key_scores(it, n, u):
                if u == 0:
                    pe.wait_ge(q_masked, it * 16 + (2 * n + 2))
                if 4 * n + u - 1 > 0:
                    pe.wait_ge(exp_done, it * 32 + (4 * n + u - 1))
                k_hi, k_lo = unit_k_hi[n % 4][:, u, :], unit_k_lo[n % 4][:, u, :]
                out = T[u % 2][:, :].rearrange("p (j q) -> p j q", j=U)
                pe.matmul(out, k_hi, q_hi_m[n % 2][:, :, :], start=True, stop=False)
                pe.matmul(out, k_hi, q_lo_m[n % 2][:, :, :], start=False, stop=False)
                mm = pe.matmul(out, k_lo, q_hi_m[n % 2][:, :, :], start=False, stop=clip)
                if causal:
                    mm = pe.matmul(out, ident_r, cr[:, C_MASK + P:C_MASK + 2 * P].unsqueeze(1).broadcast_to([P, U, P]),
                                   start=False, stop=False)
                if clip:
                    mm.then_inc(keyed, 1)

            def shift(it, n, u):
                if u == 0:
                    pe.wait_ge(neg_max_done, it * 8 + (n + 1))
                if clip:
                    pe.wait_ge(clipped, it * 32 + (4 * n + u + 1))
                pe.matmul(T[u % 2][:, :], cr[:, C_ONES + u * P:C_ONES + (u + 1) * P],
                          neg_max[n % 2][:, :, :].rearrange("p j q -> p (j q)"),
                          start=False, stop=True, skip_group_check=clip).then_inc(shifted, 1)

            def weigh(it, n):
                pe.wait_ge(exp_done, it * 32 + (4 * n + 4))
                if n > 0:
                    pe.wait_ge(sums_done, it * 8 + n)
                pe.wait_ge(pj_read, it * PJ8 + (pj_turn['v', n // GB] + 1))
                for u in range(U):
                    out = O[VW * (u % 2):VW * (u % 2) + VW, (u // 2) * P:(u // 2 + 1) * P]
                    for j in range(U):
                        mm = pe.matmul(out, V[(n // GB) % 2][:, n % GB, U * u + j, :], probs[n % 2][:, u, j, :],
                                       start=j == 0, stop=j == U - 1)
                mm.then_inc(weighted, 1)

            def transpose_sums(it, n):
                pe.wait_ge(sums_done, it * 8 + (n + 1))
                if n > 0:
                    pe.wait_ge(heads_done, it * 8 + n)
                pe.wait_ge(neg_max_done, it * 8 + min(n + (2 if clip else 3), B))
                for c in range(2):
                    mm = pe.transpose(OT[:, c * P:(c + 1) * P], sums[:, c * P:(c + 1) * P], sb["ident"][:, :])
                mm.then_inc(sums_transposed, 1)

            def transpose_heads(it, n):
                pe.wait_ge(heads_done, it * 8 + (n + 1))
                pe.wait_ge(tr_read, it * TR8 + tr_turn["o", n])
                pe.transpose(TR[:, 0:P], heads[n % 2][:, :, :, :].rearrange("p u j d -> p (u j d)"),
                             sb["ident"][:, :]).then_inc(o_transposed, 1)

            def transpose_max(it, n):
                pe.wait_ge(max_clipped if clip else max_done, it * (8 if clip else 32) + ((1 if clip else 4) * (n + 1)))
                before = n - 1 if clip else n - 2
                if before > 0:
                    pe.wait_ge(heads_done, it * 8 + before)
                pe.transpose(OT[:, 0:P], maxes[:, :, :].rearrange("p u c -> p (u c)"),
                             sb["ident"][:, :]).then_inc(max_transposed, 1)

            def out_project(it, n):
                pe.wait_ge(tr_read, it * TR8 + tr_turn["y", n])
                pe.matmul(TR[:, 0:P], ident_r, bo_hi, start=True, stop=False)
                pe.matmul(TR[:, 0:P], ident_r, bo_lo, start=False, stop=False)
                split_matmul(TR[:, 0:P], (o_hi[n % 2][:, :], o_lo[n % 2][:, :]), weight("o"), start=False)\
                    .then_inc(out_projected, 1)

            def transpose_x(it, G):
                pe.wait_ge(xn_done, it * 8 + (4 * G + 4))
                if tr_turn['x', G] > 0:
                    pe.wait_ge(tr_read, it * TR8 + tr_turn['x', G])
                for b in range(GB):
                    mm = pe.transpose(TR[:, b * P:(b + 1) * P], xn[:, b, :], sb["ident"][:, :])
                mm.then_inc(x_transposed, 1)

            def transpose_c(it, G):
                pe.wait_ge(ctx_loaded, it * 32 + (16 * (G + 1)))
                pe.wait_ge(tr_read, it * TR8 + tr_turn['c', G])
                for b in range(GB):
                    mm = pe.transpose(TR[0:DC, b * P:(b + 1) * P], ctx_in[:, b, :], sb["ident"][:, :])
                mm.then_inc(c_transposed, 1)

            def project(it, G, name):
                if pj_turn[name, G] > 0:
                    pe.wait_ge(pj_read, it * PJ8 + pj_turn[name, G])
                src = "c" if cross and name != "q" else "x"
                pe.wait_ge(tr_read, it * TR8 + (tr_turn[src, G] + 1))
                hi, lo = (x_hi, x_lo) if src == "x" else (c_hi, c_lo)
                w = weight(name, P if src == "x" else DC)
                if name == "v":
                    for b in range(GB):
                        cols = slice(b * P, (b + 1) * P)
                        mm = split_matmul(PJ[:, cols], (hi[:, cols], lo[:, cols]), w)
                else:
                    mm = split_matmul(PJ[:, :], w, (hi[:, :], lo[:, :]))
                mm.then_inc(projected, 1)

            def slot(it, n):
                G, b = n // GB, n % GB
                now, nxt, old = there(it, n), there(it, n + 1), there(it, n - 1)
                if clip:
                    order = "k0 s0 k1 s1 w f0 s2 f1 t y k2 s3 mid x k3 f2 p h m f3"
                else:
                    order = "s0 s1 k0 f0 s2 k1 f1 s3 k2 f2 mid m w x k3 t f3 y p h"
                for step in order.split():
                    if step == "m" and nxt:
                        transpose_max(it, n + 1)
                    elif step == "h" and old:
                        transpose_heads(it, n - 1)
                    elif step == "x":
                        if b == 2 and group(it, G + 2):
                            transpose_x(it, G + 2)
                    elif step == "p":
                        if b == 2 and group(it, G + 2):
                            project(it, G + 2, "q")
                        if b == 3 and group(it, G + 2):
                            project(it, G + 2, "k")
                        if b == 0 and group(it, G + 1):
                            project(it, G + 1, "v")
                    elif step[0] == "s" and nxt:
                        scores(it, n + 1, int(step[1]))
                    elif step[0] == "k" and now:
                        key_scores(it, n, int(step[1]))
                    elif step[0] == "f" and now:
                        shift(it, n, int(step[1]))
                    elif step == "w" and old:
                        weigh(it, n - 1)
                    elif step == "mid":
                        if cross and b == 3 and group(it, G + 2):
                            transpose_c(it, G + 2)
                        if rope and b == 3 and group(it, G + 2):
                            project(it, G + 2, "q2")
                        if rope and b == 0 and group(it, G + 1):
                            project(it, G + 1, "k2")
                    elif step == "t" and old:
                        transpose_sums(it, n - 1)
                    elif step == "y" and there(it, n - 2):
                        out_project(it, n - 2)

            run(pe, slot)

        @block.scalar
        def _(act):
            def exps(it, n, u):
                act.wait_ge(shifted, it * 32 + (4 * n + u + 1))
                if u == 0:
                    if n - 1 > 0:
                        act.wait_ge(weighted, it * 8 + (n - 1))
                act.activation(probs[n % 2][:, u, :, :].rearrange("p g q -> p (g q)"), T[u % 2][:, :],
                               ACT.Exp, scale=scale).then_inc(exp_done, 1)

            def spread(it, n, i):
                G = n // GB
                cols = slice((n % GB) * P, (n % GB + 1) * P)
                if not rope:
                    act.wait_ge(pj_read, it * PJ8 + (pj_turn['k', G] + 1))
                else:
                    act.wait_ge(qk_lo_done, it * 4 + (2 * G + 2))
                act.wait_ge(qk_hi_done, it * 4 + (2 * G + 2))
                src, out = ((qk_hi[0], unit_q), (qk_hi[1], unit_k_hi), (qk_lo[1], unit_k_lo))[i]
                for u in range(U):
                    rows = slice(32 * u, 32 * u + 32)
                    act.activation(out[n % 4][rows, u, :], src[G % 2][rows, cols].bitcast(F32), ACT.Copy)\
                        .then_inc(spread_done, 1)

            def copy_sums(it, n):
                act.wait_ge(weighted, it * 8 + (n + 1))
                if n > 0:
                    act.wait_ge(sums_transposed, it * 8 + n)
                act.activation(sums[:, :], O[:, 0:2 * P], ACT.Copy).then_inc(sums_done, 1)

            def hi_of(it, G, i):
                if rope:
                    act.wait_ge(turned_done, it * 4 + (2 * G + i + 1))
                    act.activation(qk_hi[i][G % 2][:, :], turned[i][:, :], ACT.Copy).then_inc(qk_hi_done, 1)
                else:
                    act.wait_ge(projected, it * (2 * NP) + (NP * G + i + 1))
                    act.activation(qk_hi[i][G % 2][:, :], PJ[:, :], ACT.Identity,
                                   bias=bias("qk"[i])).then_inc(qk_hi_done, 1)

            def slot(it, n):
                G, b = n // GB, n % GB
                if clip:
                    order = "w e0 s0 e1 s1 x c e2 s2 p h e3"
                else:
                    order = "e0 s0 e1 s1 e2 s2 w x e3 h p"
                for step in order.split():
                    if step[0] == "e" and there(it, n):
                        exps(it, n, int(step[1]))
                    elif step[0] == "s" and there(it, n + 2):
                        spread(it, n + 2, int(step[1]))
                    elif step == "w" and there(it, n - 1):
                        copy_sums(it, n - 1)
                    elif step == "x" and b == 2 and group(it, G + 2):
                        act.wait_ge(x_transposed, it * 2 + (G + 3))
                        act.activation(x_hi[:, :], TR[:, :], ACT.Copy).then_inc(x_hi_done, 1)
                    elif step == "c" and b == 3 and group(it, G + 2):
                        act.wait_ge(c_transposed, it * 2 + (G + 3))
                        act.activation(c_hi[:, :], TR[0:DC, :], ACT.Copy).then_inc(c_hi_done, 1)
                    elif step == "h" and there(it, n - 1):
                        act.wait_ge(o_transposed, it * 8 + n)
                        act.activation(o_hi[(n - 1) % 2][:, :], TR[:, 0:P], ACT.Copy).then_inc(o_hi_done, 1)
                    elif step == "p":
                        if b == (3 if rope else 2) and group(it, G + 2):
                            hi_of(it, G + 2, 0)
                        if rope and b == 0 and group(it, G + 1):
                            hi_of(it, G + 1, 1)
                        if not rope and b == 3 and group(it, G + 2):
                            hi_of(it, G + 2, 1)

            run(act, slot)

        @block.vector
        def _(dve):
            def head_max(it, n, u):
                dve.wait_ge(scored, it * 32 + (4 * n + u + 1))
                if n - 1 >= 0 and u == 0:
                    dve.wait_ge(max_transposed, it * 8 + n)
                dve.tensor_reduce(maxes[:, u, 0:U], S[u % 2][:, :].rearrange("p (j k) -> p j k", k=P),
                                  AX.X, ALU.max, negate=True).then_inc(max_done, 1)

            def clip_scores(it, n, u):
                dve.wait_ge(keyed, it * 32 + (4 * n + u + 1))
                dve.tensor_scalar(T[u % 2][:, :], T[u % 2][:, :], CLAMP / scale, -CLAMP / scale,
                                  ALU.min, ALU.max).then_inc(clipped, 1)

            def normalise(it, n):
                dve.wait_ge(sums_transposed, it * 8 + (n + 1))
                if n > 0:
                    dve.wait_ge(heads_done, it * 8 + n)
                o = OT[:, 0:U * VW].rearrange("p (u c) -> p u c", c=VW)
                dve.reciprocal(recip[n % 2][:, :, :], o[:, :, 32:32 + U]).then_inc(recip_done, 1)
                dve.wait_ge(recip_done, it * 8 + (n + 1))
                dve.tensor_tensor(heads[n % 2][:, :, :, :],
                                  o[:, :, 0:32].rearrange("p u (j d) -> p u j d", j=U),
                                  recip[n % 2][:, :, :].unsqueeze(3).broadcast_to([P, U, U, DH]),
                                  ALU.mult).then_inc(heads_done, 1)

            def rotate(it, G, name):
                i, second = ("q", "k").index(name[0]), name.endswith("2")
                dve.wait_ge(projected, it * (2 * NP) + (NP * G + pieces.index(name) + 1))
                if 2 * (G - 1) + i + 1 > 0:
                    dve.wait_ge(turned_done, it * 4 + (2 * (G - 1) + i + 1))
                dst = (by_sin if second else by_cos)[i]
                dve.scalar_tensor_tensor(dst[:, :, :], PJ[:, :].rearrange("p (b t) -> p b t", t=P), bias(name),
                                         (sin if second else cos).unsqueeze(1).broadcast_to([P, GB, P]),
                                         ALU.add, ALU.mult).then_inc(pj_read, 1)

            def values(it, G):
                dve.wait_ge(projected, it * (2 * NP) + (NP * G + NP))
                for j in range(U):
                    at = lambda x: x.rearrange("p (u j d) -> p u j d", u=U, j=U)[:, :, j, :]
                    op = dve.tensor_tensor(V[G % 2][:, :, j:H:U, DH * j:DH * (j + 1)],
                                           PJ[:, :].rearrange("p (b u j d) -> p b u j d", b=GB, u=U, j=U)[:, :, :, j, :],
                                           at(bv).unsqueeze(1).broadcast_to([P, GB, U, DH]), ALU.add)
                op.then_inc(pj_read, 1)

            def lo_of(it, G, i):
                if cross and G > 1:
                    dve.wait_ge(lo_summed, it * 4 + (2 * G + i - 3))
                dve.wait_ge(qk_hi_done, it * 4 + (2 * G + i + 1))
                dve.scalar_tensor_tensor(qk_lo[i][G % 2][:, :], PJ[:, :], bias("qk"[i]),
                                         qk_hi[i][G % 2][:, :].bitcast(F32), ALU.add, ALU.subtract)\
                    .then_inc(pj_read, 1)
                if cross:
                    dve.wait_ge(pj_read, it * PJ8 + (pj_turn["qk"[i], G] + 1))
                    dve.tensor_reduce(sb["lo_sums"][:, bass.ds(it * 4 + (2 * G + i), 1)], qk_lo[i][G % 2][:, :],
                                      AX.X, ALU.add).then_inc(lo_summed, 1)

            def moments(it, G):
                if kind == "self" and G >= 2:
                    dve.wait_ge(x_ready, 16 * (NG - 2))
                if 4 * G > 0:
                    dve.wait_ge(xn_done, it * 8 + (4 * G))
                if 4 * G > 0:
                    dve.wait_ge(mean_done, it * 8 + (4 * G))
                if G > 0:
                    dve.wait_ge(rstd_done, it * 2 + G)
                for b in range(GB):
                    dve.bn_stats(stats[:, b, :], batch_columns(X, it, 4 * G + b)).then_inc(stats_done, 1)
                dve.wait_ge(stats_done, it * 8 + (4 * G + 4))
                dve.sem_inc(passed, 1)
                for b in range(GB):
                    dve.bn_aggr(mean_var[:, b, :], stats[:, b, :]).then_inc(mean_done, 1)

            def layernorm(it, G):
                dve.wait_ge(rstd_done, it * 2 + (G + 1))
                dve.wait_ge(mean_done, it * 8 + (4 * G + 4))
                if G > 0:
                    dve.wait_ge(x_hi_done, it * 2 + G)
                for b in range(GB):
                    dve.tensor_scalar(xn[:, b, :], batch_columns(X, it, 4 * G + b), mean_var[:, b, 0:1],
                                      rstd[:, b:b + 1], ALU.subtract, ALU.mult).then_inc(xn_done, 1)

            def read_projection(it, n):
                G, b = n // GB, n % GB
                if b == 2 and group(it, G + 2):
                    rotate(it, G + 2, "q") if rope else lo_of(it, G + 2, 0)
                if b == 3 and group(it, G + 2):
                    rotate(it, G + 2, "k") if rope else lo_of(it, G + 2, 1)
                if b == 0 and group(it, G + 1):
                    values(it, G + 1)

            def heads_lo(it, n):
                dve.wait_ge(o_hi_done, it * 8 + (n + 1))
                dve.tensor_tensor(o_lo[n % 2][:, :], TR[:, 0:P], o_hi[n % 2][:, :].bitcast(F32),
                                  ALU.subtract).then_inc(tr_read, 1)

            def spread_max(it, n):
                dve.wait_ge(max_transposed, it * 8 + (n + 1))
                if 4 * n - 4 > 0:
                    dve.wait_ge(shifted, it * 32 + (4 * n - 4))
                dve.tensor_tensor(neg_max[n % 2][:, :, :], OT[:, 0:P].unsqueeze(1).broadcast_to([P, U, P]),
                                  diag.unsqueeze(2).broadcast_to([P, U, P]), ALU.mult).then_inc(neg_max_done, 1)

            def input_lo(it, G):
                dve.wait_ge(x_hi_done, it * 2 + (G + 1))
                dve.tensor_tensor(x_lo[:, :], TR[:, :], x_hi[:, :].bitcast(F32), ALU.subtract).then_inc(tr_read, 1)

            def add_output(it, n):
                if cross:
                    dve.wait_ge(x_kept, 16)
                dve.wait_ge(out_projected, it * 8 + (n + 1))
                dve.wait_ge(xn_done, it * 8 + (4 * (n // GB) + 4))
                x = batch_columns(X, it, n)
                dve.tensor_tensor(x, TR[:, 0:P], x, ALU.add).then_inc(tr_read, 1)

            def slot(it, n):
                G, b = n // GB, n % GB
                if clip:
                    order = "c0 m0 c1 m1 mo m2 n y c2 ln m3 mc x c c3 p h m"
                else:
                    order = "m0 m1 mo m2 m3 ln m x p2 n y p h"
                for step in order.split():
                    if step in ("c0", "c1", "c2", "c3") and there(it, n):
                        clip_scores(it, n, int(step[1]))
                    elif step in ("m0", "m1", "m2", "m3") and there(it, n + 1):
                        head_max(it, n + 1, int(step[1]))
                    elif step == "mo" and b == 2 and group(it, G + 2):
                        moments(it, G + 2)
                    elif step == "ln" and b == 2 and group(it, G + 2):
                        layernorm(it, G + 2)
                    elif step == "mc" and there(it, n + 1):
                        dve.wait_ge(max_done, it * 32 + (4 * (n + 2)))
                        dve.tensor_scalar(maxes[:, :, 0:U], maxes[:, :, 0:U], CLAMP / scale, -CLAMP / scale,
                                          ALU.min, ALU.max).then_inc(max_clipped, 1)
                    elif step == "m" and there(it, n + 1):
                        spread_max(it, n + 1)
                    elif step == "x" and b == 2 and group(it, G + 2):
                        input_lo(it, G + 2)
                    elif step == "c" and b == 3 and group(it, G + 2):
                        dve.wait_ge(c_hi_done, it * 2 + (G + 3))
                        dve.tensor_reduce(sb["key_sums"][:, bass.ds(it * 8 + GB * (G + 2), GB)],
                                          TR[0:DC, :].rearrange("p (b k) -> p b k", k=P), AX.X, ALU.add)
                        dve.tensor_tensor(c_lo[:, :], TR[0:DC, :], c_hi[:, :].bitcast(F32), ALU.subtract)\
                            .then_inc(tr_read, 1)
                    elif step == "p2" and rope and b == 3 and group(it, G + 2):
                        rotate(it, G + 2, "q2")
                    elif step == "p2" and rope and b == 0 and group(it, G + 1):
                        rotate(it, G + 1, "k2")
                    elif step == "n" and there(it, n - 1):
                        normalise(it, n - 1)
                    elif step == "y" and there(it, n - 2):
                        add_output(it, n - 2)
                    elif step == "p":
                        read_projection(it, n)
                    elif step == "h" and there(it, n - 1):
                        heads_lo(it, n - 1)

            run(dve, slot)

        @block.gpsimd
        def _(pool):
            def reciprocal_deviation(it, G):
                pool.wait_ge(mean_done, it * 8 + (4 * G + 4))
                if 4 * G > 0:
                    pool.wait_ge(xn_done, it * 8 + (4 * G))
                if G > 0:
                    pool.wait_ge(rstd_done, it * 2 + G)
                pool.sem_inc(passed, 1)
                pool.tensor_scalar(var_eps[:, :], mean_var[:, :, 1], LN_EPS, 1.0, ALU.add, ALU.mult)\
                    .then_inc(var_done, 1)
                pool.wait_ge(var_done, it * 2 + (G + 1))
                pool.tensor_tensor(rstd[:, :], var_eps[:, :], power[:, :], ALU.pow).then_inc(rstd_done, 1)

            def turn(it, G, i):
                name = ("q2", "k2")[i]
                pool.wait_ge(pj_read, it * PJ8 + (pj_turn[name, G] + 1))
                if 2 * (G - 1) + i + 1 > 0:
                    pool.wait_ge(qk_hi_done, it * 4 + (2 * (G - 1) + i + 1))
                if 2 * (G - 1) + i + 1 > 0:
                    pool.wait_ge(qk_lo_done, it * 4 + (2 * (G - 1) + i + 1))
                pool.tensor_tensor(turned[i][:, :], by_cos[i][:, :, :].rearrange("p b t -> p (b t)"),
                                   by_sin[i][:, :, :].rearrange("p b t -> p (b t)"), ALU.add)\
                    .then_inc(turned_done, 1)
                pool.wait_ge(qk_hi_done, it * 4 + (2 * G + i + 1))
                if 4 * (4 * G - 4) > 0:
                    pool.wait_ge(shifted, it * 32 + (4 * (4 * G - 4)))
                pool.tensor_tensor(qk_lo[i][G % 2][:, :], turned[i][:, :], qk_hi[i][G % 2][:, :].bitcast(F32),
                                   ALU.subtract).then_inc(qk_lo_done, 1)

            def mask(it, n, out, src, done):
                cols = slice((n % GB) * P, (n % GB + 1) * P)
                pool.tensor_tensor(out[n % 2][:, :, :],
                                   src[(n // GB) % 2][:, cols].bitcast(F32).unsqueeze(1).broadcast_to([P, U, P]),
                                   slots.unsqueeze(2).broadcast_to([P, U, P]), ALU.mult).then_inc(done, 1)

            def mask_all(it, n):
                G = n // GB
                pool.wait_ge(qk_hi_done, it * 4 + (2 * G + 2))
                if 4 * (n - 1) > 0:
                    pool.wait_ge(scored, it * 32 + (4 * (n - 1)))
                mask(it, n, k_hi_m, qk_hi[1], k_masked)
                if 4 * (n - 1) > 0:
                    pool.wait_ge(shifted, it * 32 + (4 * (n - 1)))
                mask(it, n, q_hi_m, qk_hi[0], q_masked)
                if rope:
                    pool.wait_ge(qk_lo_done, it * 4 + (2 * G + 2))
                else:
                    pool.wait_ge(pj_read, it * PJ8 + (pj_turn['k', G] + 1))
                mask(it, n, q_lo_m, qk_lo[0], q_masked)

            def slot(it, n):
                G, b = n // GB, n % GB
                if b == 2 and group(it, G + 2):
                    reciprocal_deviation(it, G + 2)
                if there(it, n + 2):
                    mask_all(it, n + 2)
                if rope and b == 3 and group(it, G + 2):
                    turn(it, G + 2, 0)
                if rope and b == 0 and group(it, G + 1):
                    turn(it, G + 1, 1)

            pool.sem_clear(used_before)
            pool.memset(power[:, :], -0.5).then_inc(power_done, 1)
            pool.wait_ge(power_done, 1)
            run(pool, slot)

        if cross:
            @block.sync
            def _(sp):
                sp.dma_start(sb["x_before"][:, :], X[:, :]).then_inc(x_kept, 16)
                sp.dma_start(ctx_in[:, :, :], context[0:GB, :, :].rearrange("b p d -> p b d")).then_inc(ctx_loaded, 16)
                with sp.Fori(1, NG) as G:
                    sp.wait_ge(c_transposed, G)
                    sp.dma_start(ctx_in[:, :, :],
                                 context[bass.ds(G * GB, GB), :, :].rearrange("b p d -> p b d"))\
                        .then_inc(ctx_loaded, 16)


def uniform_guard(nc, phase, sb, ps):
    a = ATT["cross"]
    wv, wo = (slice((a * len(AW) + AW.index(n)) * P, (a * len(AW) + AW.index(n) + 1) * P) for n in "vo")
    with ExitStack() as ctx:
        def buf(name, shape, dt=F32):
            return ctx.enter_context(nc.sbuf_tensor(f"guard_{name}", shape, dt))

        sem, used_before = phase_semaphores(nc, ctx, phase, "guard")
        key_hi, key_lo = buf("key_hi", [DC, B], F32R), buf("key_lo", [DC, B], F32R)
        zeros, bad, ones, flag = buf("zeros", [P, 2 * NG]), buf("bad", [P, 1]), buf("ones", [P, P]), ps[0][:, 256:257].bitcast(I32)
        found = buf("found", [P, 1])
        v_mean, v_hi, v_lo = buf("v_mean", [P, B]), buf("v_hi", [P, B], F32R), buf("v_lo", [P, B], F32R)
        y = buf("y", [B, D])
        steps, ones_set, means_made, mean_copied = sem("steps"), sem("ones_set"), sem("means_made"), sem("mean_copied")
        y_made, y_spread, y_added = sem("y_made"), sem("y_spread"), sem("y_added")
        block = ctx.enter_context(nc.Block())

        @block.gpsimd
        def _(pool):
            pool.sem_clear(used_before)
            pool.memset(ones[:, :], 1.0).then_inc(ones_set, 1)

        @block.vector
        def _(dve):
            dve.tensor_copy(key_hi[:, :], sb["key_sums"][:, :]).then_inc(steps, 1)
            dve.tensor_scalar(zeros[:, :], sb["lo_sums"][:, :], 0.0, None, ALU.mult).then_inc(steps, 1)
            dve.wait_ge(steps, 2)
            dve.tensor_tensor(key_lo[:, :], sb["key_sums"][:, :], key_hi[:, :].bitcast(F32), ALU.subtract)\
                .then_inc(steps, 1)
            dve.tensor_reduce(bad[:, :], zeros[:, :], AX.X, ALU.add).then_inc(steps, 1)
            dve.wait_ge(means_made, 1)
            dve.tensor_copy(found[:, :], ps[1][:, 0:1]).then_inc(steps, 1)
            dve.wait_ge(mean_copied, 2)
            dve.tensor_tensor(v_lo[:, :], v_mean[:, :], v_hi[:, :].bitcast(F32), ALU.subtract).then_inc(steps, 1)
            dve.wait_ge(steps, 6)
            dve.tensor_tensor(flag[:, :], found[:, :], found[:, :], ALU.not_equal).then_inc(steps, 1)
            dve.wait_ge(y_made, 1)
            dve.tensor_tensor(y[:, :], ps[2][0:B, 0:D], sb["rows"][0:B, a * P:(a + 1) * P], ALU.add)\
                .then_inc(steps, 1)
            for g in range(NG):
                dve.wait_ge(y_spread, g + 1)
                cols = slice(g * GT, (g + 1) * GT)
                dve.tensor_tensor(sb["x_before"][:, cols], ps[1 + g % 7][:, :], sb["x_before"][:, cols], ALU.add)\
                    .then_inc(y_added, 1)
            dve.wait_ge(steps, 8)
            dve.wait_ge(y_added, NG)
            dve.copy_predicated(sb["x"][:, :], flag.broadcast_to([P, B * D]), sb["x_before"][:, :])

        @block.tensor
        def _(pe):
            def split_matmul(out, l, r):
                pe.matmul(out, l[0], r[0], start=True, stop=False)
                pe.matmul(out, l[0], r[1], start=False, stop=False)
                return pe.matmul(out, l[1], r[0], start=False, stop=True)

            pe.wait_ge(ones_set, 1)
            pe.wait_ge(steps, 4)
            split_matmul(ps[0][:, 0:B], (sb["w_hi"][0:DC, wv], sb["w_lo"][0:DC, wv]), (key_hi[:, :], key_lo[:, :]))
            pe.matmul(ps[1][:, 0:1], ones[:, :], bad[:, :], start=True, stop=True).then_inc(means_made, 1)
            pe.wait_ge(steps, 6)
            split_matmul(ps[2][0:B, 0:D], (v_hi[:, :], v_lo[:, :]), (sb["w_hi"][:, wo], sb["w_lo"][:, wo]))\
                .then_inc(y_made, 1)
            pe.wait_ge(steps, 8)
            for b in range(B):
                if b == 7 * GB:
                    pe.wait_ge(y_added, 1)
                mm = pe.matmul(ps[1 + (b // GB) % 7][:, (b % GB) * P:(b % GB + 1) * P],
                               sb["ident"][0:B, b:b + 1].broadcast_to([B, P]), y[:, :], start=True, stop=True)
                if b % GB == GB - 1:
                    mm.then_inc(y_spread, 1)

        @block.scalar
        def _(act):
            act.wait_ge(means_made, 1)
            act.activation(v_mean[:, :], ps[0][:, 0:B], ACT.Identity, scale=1.0 / P,
                           bias=sb["cols"][:, COL_V0:COL_V0 + 1]).then_inc(mean_copied, 1)
            act.wait_ge(mean_copied, 1)
            act.activation(v_hi[:, :], v_mean[:, :], ACT.Copy).then_inc(mean_copied, 1)


def gated_experts(nc, phase, sb, ps, ready):
    NB = E0 // 2 + 1
    X = sb["x"]
    H1, H3, GATE, YT, TR, LG = ps[0:2], ps[2:4], ps[4], ps[5], ps[6], ps[7]
    cr = sb["const_r"]
    earlier = sb["const"][:, C_EARLIER - N_CONST_R:C_EARLIER - N_CONST_R + E0 * E0].rearrange("p (a b) -> p a b", b=E0)
    router_b = sb["rows"][:, R_ROUTER0:R_ROUTER0 + E0]

    with ExitStack() as ctx:
        def buf(name, shape, dt=F32):
            return ctx.enter_context(nc.sbuf_tensor(f"ffn0_{name}", shape, dt))

        sem, used_before = phase_semaphores(nc, ctx, phase, "ffn0")
        raw = sb["raw_ffn0"]
        w_hi, w_lo = buf("w_hi", [P, W_FFN0], F32R), buf("w_lo", [P, W_FFN0], F32R)
        stats, mean_var = buf("stats", [P, GB, 6]), buf("mean_var", [P, GB, 2])
        var_eps, rstd, power = buf("var_eps", [P, GB]), buf("rstd", [P, GB]), buf("power", [P, GB])
        xn = buf("xn", [P, GB, D])
        x_hi = [buf(f"x_hi{i}", [P, GT], F32R) for i in range(2)]
        x_lo = [buf(f"x_lo{i}", [P, GT], F32R) for i in range(2)]
        logits, shifted = buf("logits", [P, GB, E0]), buf("shifted", [P, GB, E0])
        top, exps = buf("top", [P, GB]), buf("exps", [P, GB, E0])
        above, equal = buf("above", [P, GB, E0, E0]), buf("equal", [P, GB, E0, E0])
        rank, chosen = buf("rank", [P, GB, E0]), buf("chosen", [P, GB, E0])
        total, recip, gates = buf("total", [P, GB]), buf("recip", [P, GB]), buf("gates", [P, GB, E0])
        gate_parts = buf("gate_parts", [P, GB, 2 * E0], F32R)
        g_parts = [buf(f"g_parts{i}", [2 * E0, GT], F32R) for i in range(2)]
        silu = [buf(f"silu{i}", [P, GT]) for i in range(2)]
        product = [buf(f"product{i}", [P, GT]) for i in range(2)]
        hidden = [buf(f"hidden{i}", [P, GT]) for i in range(2)]
        h_hi = [buf(f"h_hi{i}", [P, GT], F32R) for i in range(2)]
        h_lo = [buf(f"h_lo{i}", [P, GT], F32R) for i in range(2)]
        y = buf("y", [P, GT])

        split, split_lo = sem("weights_hi_done"), sem("weights_lo_done")
        x_transposed, logits_made, g_transposed = sem("x_transposed"), sem("logits_made"), sem("g_transposed")
        h1_made, h3_made, gate_spread = sem("h1_made"), sem("h3_made"), sem("gate_spread")
        y_summed, y_back = sem("y_summed"), sem("y_back")
        x_hi_done, exps_done = sem("x_hi_done"), sem("exps_done")
        silu_done, h_hi_done, y_copied = sem("silu_done"), sem("h_hi_done"), sem("y_copied")
        stats_done, mean_done, xn_done = sem("stats_done"), sem("mean_done"), sem("xn_done")
        tr_read = sem("tr_read")
        routed = sem("routed")
        product_done, hidden_done = sem("product_done"), sem("hidden_done")
        power_done, var_done, rstd_done = sem("power_done"), sem("var_done"), sem("rstd_done")
        h_lo_done, passed = sem("h_lo_done"), sem("passed")
        product_summed = sem("product_summed")
        RS = 13

        turn = {}
        for n in range(-2, NG + 1):
            for name, G in (("x", n + 1), ("o", n - 1), ("g", n + 1)):
                if 0 <= G < NG:
                    turn[name, G] = len(turn)

        block = ctx.enter_context(nc.Block())

        def run(engine, slot):
            for n in range(-2, 2):
                slot(0, n)
            with engine.Fori(0, 2) as it:
                for n in range(2, 4):
                    slot(it, n)
            for n in range(6, NG + 1):
                slot(0, n)

        def there(it, G):
            return not isinstance(it, int) or 0 <= G < NG

        def group_columns(it, G):
            return X[:, bass.ds(it * (2 * GT) + G * GT, GT)]

        @block.tensor
        def _(pe):
            def split_matmul(out, l, r, start=True, stop=True):
                pe.matmul(out, l[0], r[0], start=start, stop=False)
                pe.matmul(out, l[0], r[1], start=False, stop=False)
                return pe.matmul(out, l[1], r[0], start=False, stop=stop)

            def weight(block, width=P):
                return w_hi[:, block * P:block * P + width], w_lo[:, block * P:block * P + width]

            def xs(n, cols=slice(0, GT)):
                return x_hi[n % 2][:, cols], x_lo[n % 2][:, cols]

            def hidden_rows(it, n, k):
                i = NB * n + k
                if k == 0:
                    pe.wait_ge(tr_read, it * 6 + (turn['x', n] + 1))
                if i - 1 > 0:
                    pe.wait_ge(silu_done, it * (2 * NB) + (i - 1))
                split_matmul(H1[i % 2][:, :], weight(k), xs(n)).then_inc(h1_made, 1)
                if i - 1 > 0:
                    pe.wait_ge(hidden_done, it * (2 * NB) + (i - 1))
                split_matmul(H3[i % 2][:, :], weight(NB + k), xs(n)).then_inc(h3_made, 1)

            def spread_gate(it, n, k):
                if k == 0:
                    pe.wait_ge(tr_read, it * 6 + (turn['g', n] + 1))
                if NB * n + k > 0:
                    pe.wait_ge(hidden_done, it * (2 * NB) + (NB * n + k))
                sel = cr[0:2 * E0, C_PAIR + k * P:C_PAIR + (k + 1) * P]
                pe.matmul(GATE[:, :], sel, g_parts[n % 2][:, :], start=True, stop=True).then_inc(gate_spread, 1)

            def down(it, n, k):
                i = NB * n + k
                pe.wait_ge(h_lo_done, it * (2 * NB) + (i + 1))
                if k == 0:
                    if n > 0:
                        pe.wait_ge(y_copied, it * 2 + n)
                split_matmul(YT[:, :], weight(2 * NB + k), (h_hi[i % 2][:, :], h_lo[i % 2][:, :]),
                             start=k == 0, stop=k == NB - 1).then_inc(y_summed, 1)

            def transpose_x(it, n):
                pe.wait_ge(xn_done, it * (2 * GB) + (GB * (n + 1)))
                if turn['x', n] > 0:
                    pe.wait_ge(tr_read, it * 6 + turn['x', n])
                for b in range(GB):
                    mm = pe.transpose(TR[:, b * P:(b + 1) * P], xn[:, b, :], sb["ident"][:, :])
                mm.then_inc(x_transposed, 1)

            def make_logits(it, n):
                pe.wait_ge(tr_read, it * 6 + (turn['x', n] + 1))
                if RS * (n - 1) + 1 > 0:
                    pe.wait_ge(routed, it * (2 * RS) + (RS * (n - 1) + 1))
                for b in range(GB):
                    mm = split_matmul(LG[:, b * E0:(b + 1) * E0], xs(n, slice(b * P, (b + 1) * P)), weight(3 * NB, E0))
                mm.then_inc(logits_made, 1)

            def transpose_gates(it, n):
                pe.wait_ge(routed, it * (2 * RS) + (RS * (n + 1)))
                pe.wait_ge(tr_read, it * 6 + turn['g', n])
                for b in range(GB):
                    mm = pe.transpose(TR[0:2 * E0, b * P:(b + 1) * P], gate_parts[:, b, :].bitcast(F32), sb["ident"][:, :])
                mm.then_inc(g_transposed, 1)

            def transpose_back(it, n):
                pe.wait_ge(y_copied, it * 2 + (n + 1))
                pe.wait_ge(tr_read, it * 6 + turn['o', n])
                for b in range(GB):
                    mm = pe.transpose(TR[:, b * P:(b + 1) * P], y[:, b * P:(b + 1) * P], sb["ident"][:, :])
                mm.then_inc(y_back, 1)

            def slot(it, n):
                for k in range(NB):
                    if there(it, n):
                        hidden_rows(it, n, k)
                    if k == 0 and there(it, n + 1):
                        transpose_x(it, n + 1)
                    if k >= 2 and there(it, n):
                        down(it, n, k - 2)
                    elif k < 2 and there(it, n - 1):
                        down(it, n - 1, NB + k - 2)
                    if k < NB - 1 and there(it, n):
                        spread_gate(it, n, k)
                    if k == 1 and there(it, n + 1):
                        make_logits(it, n + 1)
                    if k == 2 and there(it, n - 1):
                        transpose_back(it, n - 1)
                    if k == NB - 1 and there(it, n + 1):
                        transpose_gates(it, n + 1)

            pe.wait_ge(split_lo, 1)
            run(pe, slot)

        @block.scalar
        def _(act):
            def copy(out, src, done):
                act.activation(out, src, ACT.Copy).then_inc(done, 1)

            def make_silu(it, n, k):
                i = NB * n + k
                act.wait_ge(h1_made, it * (2 * NB) + (i + 1))
                if i - 1 > 0:
                    act.wait_ge(hidden_done, it * (2 * NB) + (i - 1))
                act.activation(silu[i % 2][:, :], H1[i % 2][:, :], ACT.Silu).then_inc(silu_done, 1)

            def hidden_hi(it, n, k):
                i = NB * n + k
                act.wait_ge(hidden_done, it * (2 * NB) + (i + 1))
                if i - 1 > 0:
                    act.wait_ge(y_summed, it * (2 * NB) + (i - 1))
                copy(h_hi[i % 2][:, :], hidden[i % 2][:, :], h_hi_done)

            def slot(it, n):
                for k in range(NB):
                    if there(it, n):
                        make_silu(it, n, k)
                    if k >= 1 and there(it, n):
                        hidden_hi(it, n, k - 1)
                    elif k == 0 and there(it, n - 1):
                        hidden_hi(it, n - 1, NB - 1)
                    if k == 0 and there(it, n + 1):
                        act.wait_ge(x_transposed, it * 2 + (n + 2))
                        if NB * n > 0:
                            act.wait_ge(h3_made, it * (2 * NB) + (NB * n))
                        copy(x_hi[(n + 1) % 2][:, :], TR[:, :], x_hi_done)
                    if k == 1 and there(it, n - 1):
                        act.wait_ge(y_summed, it * (2 * NB) + (NB * n))
                        if n - 1 > 0:
                            act.wait_ge(y_back, it * 2 + (n - 1))
                        copy(y[:, :], YT[:, :], y_copied)
                    if k == 2 and there(it, n + 1):
                        act.wait_ge(routed, it * (2 * RS) + (RS * (n + 1) + 3))
                        act.activation(exps[:, :, :], shifted[:, :, :], ACT.Exp).then_inc(exps_done, 1)

            run(act, slot)

        @block.vector
        def _(dve):
            def hidden_products(it, n, k):
                i = NB * n + k
                dve.wait_ge(silu_done, it * (2 * NB) + (i + 1))
                dve.wait_ge(h3_made, it * (2 * NB) + (i + 1))
                if k == NB - 1:
                    dve.wait_ge(h_lo_done, it * (2 * NB) + (i - 1))
                    dve.tensor_tensor(hidden[i % 2][:, :], silu[i % 2][:, :], H3[i % 2][:, :], ALU.mult)\
                        .then_inc(hidden_done, 1)
                    return
                if i > 0:
                    dve.wait_ge(hidden_done, it * (2 * NB) + i)
                dve.tensor_tensor(product[i % 2][:, :], silu[i % 2][:, :], H3[i % 2][:, :], ALU.mult)\
                    .then_inc(product_done, 1)
                dve.wait_ge(product_done, it * 8 + (4 * n + k + 1))
                dve.wait_ge(gate_spread, it * 8 + (4 * n + k + 1))
                if i - 1 > 0:
                    dve.wait_ge(h_lo_done, it * (2 * NB) + (i - 1))
                dve.tensor_tensor(hidden[i % 2][:, :], product[i % 2][:, :], GATE[:, :], ALU.mult)\
                    .then_inc(hidden_done, 1)

            def by_expert(x):
                return x.unsqueeze(2).broadcast_to([P, GB, E0])

            def route(it, n, steps):
                base = RS * n
                l = logits[:, :, :]
                mine = l.unsqueeze(3).broadcast_to([P, GB, E0, E0])
                other = l.unsqueeze(2).broadcast_to([P, GB, E0, E0])
                for s in steps:
                    if s == 0:
                        dve.wait_ge(logits_made, it * 2 + (n + 1))
                    if s == 7:
                        dve.wait_ge(exps_done, it * 2 + (n + 1))
                    if s == 11:
                        if n > 0:
                            dve.wait_ge(g_transposed, it * 2 + n)
                    if base + s > 0:
                        dve.wait_ge(routed, it * (2 * RS) + (base + s))
                    if s == 0:
                        op = dve.tensor_tensor(l, LG[:, 0:GB * E0].rearrange("p (b e) -> p b e", e=E0),
                                               router_b.unsqueeze(1).broadcast_to([P, GB, E0]), ALU.add)
                    elif s == 1:
                        op = dve.tensor_reduce(top[:, :], l, AX.X, ALU.max)
                    elif s == 2:
                        op = dve.tensor_tensor(shifted[:, :, :], l, by_expert(top[:, :]), ALU.subtract)
                    elif s == 3:
                        op = dve.tensor_tensor(equal[:, :, :, :], other, mine, ALU.is_equal)
                    elif s == 4:
                        op = dve.tensor_tensor(equal[:, :, :, :], equal[:, :, :, :],
                                               earlier.unsqueeze(1).broadcast_to([P, GB, E0, E0]), ALU.mult)
                    elif s == 5:
                        op = dve.tensor_tensor(above[:, :, :, :], other, mine, ALU.is_gt)
                    elif s == 6:
                        dve.tensor_tensor(above[:, :, :, :], above[:, :, :, :], equal[:, :, :, :], ALU.add)\
                            .then_inc(product_summed, 1)
                        dve.wait_ge(product_summed, it * 2 + (n + 1))
                        op = dve.tensor_reduce(rank[:, :, :], above[:, :, :, :], AX.X, ALU.add)
                    elif s == 7:
                        op = dve.scalar_tensor_tensor(chosen[:, :, :], rank[:, :, :], 2.0, exps[:, :, :],
                                                      ALU.is_lt, ALU.mult)
                    elif s == 8:
                        op = dve.tensor_reduce(total[:, :], chosen[:, :, :], AX.X, ALU.add)
                    elif s == 9:
                        op = dve.reciprocal(recip[:, :], total[:, :])
                    elif s == 10:
                        op = dve.tensor_tensor(gates[:, :, :], chosen[:, :, :], by_expert(recip[:, :]), ALU.mult)
                    elif s == 11:
                        op = dve.tensor_copy(gate_parts[:, :, 0:E0], gates[:, :, :])
                    else:
                        op = dve.tensor_tensor(gate_parts[:, :, E0:2 * E0], gates[:, :, :],
                                               gate_parts[:, :, 0:E0].bitcast(F32), ALU.subtract)
                    op.then_inc(routed, 1)

            def moments(it, G):
                if GB * G > 0:
                    dve.wait_ge(xn_done, it * (2 * GB) + (GB * G))
                if GB * G > 0:
                    dve.wait_ge(mean_done, it * (2 * GB) + (GB * G))
                if G > 0:
                    dve.wait_ge(rstd_done, it * 2 + G)
                for b in range(GB):
                    dve.bn_stats(stats[:, b, :], X[:, bass.ds(it * (2 * GT) + G * GT + b * P, P)])\
                        .then_inc(stats_done, 1)
                dve.wait_ge(stats_done, it * (2 * GB) + (GB * (G + 1)))
                dve.sem_inc(passed, 1)
                for b in range(GB):
                    dve.bn_aggr(mean_var[:, b, :], stats[:, b, :]).then_inc(mean_done, 1)

            def layernorm(it, G):
                dve.wait_ge(rstd_done, it * 2 + (G + 1))
                dve.wait_ge(mean_done, it * (2 * GB) + (GB * (G + 1)))
                if G > 0:
                    dve.wait_ge(x_transposed, it * 2 + G)
                for b in range(GB):
                    dve.tensor_scalar(xn[:, b, :], X[:, bass.ds(it * (2 * GT) + G * GT + b * P, P)],
                                      mean_var[:, b, 0:1], rstd[:, b:b + 1], ALU.subtract, ALU.mult)\
                        .then_inc(xn_done, 1)

            def slot(it, n):
                for k in range(NB):
                    if there(it, n):
                        hidden_products(it, n, k)
                    if k == 0 and there(it, n + 1):
                        dve.wait_ge(x_hi_done, it * 2 + (n + 2))
                        dve.tensor_tensor(x_lo[(n + 1) % 2][:, :], TR[:, :], x_hi[(n + 1) % 2][:, :].bitcast(F32),
                                          ALU.subtract).then_inc(tr_read, 1)
                    if k == 1 and there(it, n + 1):
                        route(it, n + 1, range(0, 5))
                    if k == 2 and there(it, n + 1):
                        route(it, n + 1, range(5, 7))
                    if k == 2 and there(it, n - 1):
                        dve.wait_ge(y_back, it * 2 + n)
                        dve.wait_ge(xn_done, it * (2 * GB) + (GB * n))
                        x = group_columns(it, n - 1)
                        dve.tensor_tensor(x, TR[:, :], x, ALU.add).then_inc(tr_read, 1)
                    if k == 3 and there(it, n + 1):
                        route(it, n + 1, range(7, RS))
                    if k == 3 and there(it, n + 2):
                        moments(it, n + 2)
                    if k == NB - 1 and there(it, n + 1):
                        dve.wait_ge(g_transposed, it * 2 + (n + 2))
                        if 4 * n > 0:
                            dve.wait_ge(gate_spread, it * 8 + (4 * n))
                        dve.tensor_copy(g_parts[(n + 1) % 2][:, :], TR[0:2 * E0, :]).then_inc(tr_read, 1)
                    if k == NB - 1 and there(it, n + 2):
                        layernorm(it, n + 2)

            dve.wait_ge(ready["ffn0"], 16)
            dve.tensor_copy(w_hi[:, :], raw[:, :]).then_inc(split, 1)
            dve.wait_ge(split, 1)
            dve.tensor_tensor(w_lo[:, :], raw[:, :], w_hi[:, :].bitcast(F32), ALU.subtract).then_inc(split_lo, 1)
            run(dve, slot)

        @block.gpsimd
        def _(pool):
            def hidden_lo(it, n, k):
                i = NB * n + k
                pool.wait_ge(h_hi_done, it * (2 * NB) + (i + 1))
                if i - 1 > 0:
                    pool.wait_ge(y_summed, it * (2 * NB) + (i - 1))
                pool.tensor_tensor(h_lo[i % 2][:, :], hidden[i % 2][:, :], h_hi[i % 2][:, :].bitcast(F32),
                                   ALU.subtract).then_inc(h_lo_done, 1)

            def reciprocal_deviation(it, G):
                pool.wait_ge(mean_done, it * (2 * GB) + (GB * (G + 1)))
                if GB * G > 0:
                    pool.wait_ge(xn_done, it * (2 * GB) + (GB * G))
                if G > 0:
                    pool.wait_ge(rstd_done, it * 2 + G)
                pool.sem_inc(passed, 1)
                pool.tensor_scalar(var_eps[:, :], mean_var[:, :, 1], LN_EPS, 1.0, ALU.add, ALU.mult)\
                    .then_inc(var_done, 1)
                pool.wait_ge(var_done, it * 2 + (G + 1))
                pool.tensor_tensor(rstd[:, :], var_eps[:, :], power[:, :], ALU.pow).then_inc(rstd_done, 1)

            def slot(it, n):
                for k in range(NB):
                    if k >= 1 and there(it, n):
                        hidden_lo(it, n, k - 1)
                    elif k == 0 and there(it, n - 1):
                        hidden_lo(it, n - 1, NB - 1)
                    if k == 3 and there(it, n + 2):
                        reciprocal_deviation(it, n + 2)

            pool.sem_clear(used_before)
            pool.memset(power[:, :], -0.5).then_inc(power_done, 1)
            pool.wait_ge(power_done, 1)
            run(pool, slot)


def relu_experts(nc, phase, sb, ps, ready):
    NB = E1 * C1
    X = sb["x"]
    HT, YT, GATE, TR, LG, BT = ps[0:2], ps[2:4], ps[4], ps[5], ps[6], ps[7]
    cr = sb["const_r"]
    earlier = sb["const"][:, C_EARLIER - N_CONST_R:C_EARLIER - N_CONST_R + E1 * E1].rearrange("p (a b) -> p a b", b=E1)
    router_b = sb["rows"][:, R_ROUTER1:R_ROUTER1 + E1]

    with ExitStack() as ctx:
        def buf(name, shape, dt=F32):
            return ctx.enter_context(nc.sbuf_tensor(f"ffn1_{name}", shape, dt))

        sem, used_before = phase_semaphores(nc, ctx, phase, "ffn1")
        raw = sb["raw_ffn1"]
        w_hi, w_lo = buf("w_hi", [P, W_FFN1], F32R), buf("w_lo", [P, W_FFN1], F32R)
        stats, mean_var = buf("stats", [P, GB, 6]), buf("mean_var", [P, GB, 2])
        var_eps, rstd, power = buf("var_eps", [P, GB]), buf("rstd", [P, GB]), buf("power", [P, GB])
        xn = buf("xn", [P, GB, D])
        x_hi = [buf(f"x_hi{i}", [P, GT], F32R) for i in range(2)]
        x_lo = [buf(f"x_lo{i}", [P, GT], F32R) for i in range(2)]
        logits, shifted = buf("logits", [P, GB, E1]), buf("shifted", [P, GB, E1])
        top, exps = buf("top", [P, GB]), buf("exps", [P, GB, E1])
        above, equal = buf("above", [P, GB, E1, E1]), buf("equal", [P, GB, E1, E1])
        rank, chosen = buf("rank", [P, GB, E1]), buf("chosen", [P, GB, E1])
        total, recip, gates = buf("total", [P, GB]), buf("recip", [P, GB]), buf("gates", [P, GB, E1])
        gate_parts = buf("gate_parts", [P, GB, 2 * E1], F32R)
        g_parts = [buf(f"g_parts{i}", [2 * E1, GT], F32R) for i in range(2)]
        scaled = [buf(f"scaled{i}", [P, GT]) for i in range(2)]
        hidden = [buf(f"hidden{i}", [P, GT]) for i in range(2)]
        h_hi = [buf(f"h_hi{i}", [P, GT], F32R) for i in range(2)]
        h_lo = [buf(f"h_lo{i}", [P, GT], F32R) for i in range(2)]
        gate = buf("gate", [P, GT])
        probs = buf("probs", [P, GB, E1])
        y = [buf(f"y{i}", [P, GT]) for i in range(2)]

        split, split_lo = sem("weights_hi_done"), sem("weights_lo_done")
        x_transposed, logits_made, g_transposed = sem("x_transposed"), sem("logits_made"), sem("g_transposed")
        hidden_made, gate_spread, bias_made = sem("hidden_made"), sem("gate_spread"), sem("bias_made")
        y_summed, y_back = sem("y_summed"), sem("y_back")
        x_hi_done, exps_done = sem("x_hi_done"), sem("exps_done")
        h_hi_done, y_started = sem("h_hi_done"), sem("y_started")
        stats_done, mean_done, xn_done = sem("stats_done"), sem("mean_done"), sem("xn_done")
        tr_read = sem("tr_read")
        routed = sem("routed")
        scaled_done, y_added, hidden_done = sem("scaled_done"), sem("y_added"), sem("hidden_done")
        power_done, var_done, rstd_done = sem("power_done"), sem("var_done"), sem("rstd_done")
        h_lo_done, passed = sem("h_lo_done"), sem("passed")
        gate_copied = sem("gate_copied")
        product_summed = sem("product_summed")
        RS = 15

        turn = {}
        for n in range(-2, NG + 1):
            for name, G in (("o", n - 1), ("x", n + 1), ("g", n + 1)):
                if 0 <= G < NG:
                    turn[name, G] = len(turn)

        def weight_parts(e):
            if e == 0:
                return [slice(2 * NB * P, W_FFN1)]
            return [slice((e - 1) * C1 * P, e * C1 * P), slice((NB + (e - 1) * C1) * P, (NB + e * C1) * P)]

        block = ctx.enter_context(nc.Block())

        def run(engine, slot):
            for n in range(-2, 2):
                slot(0, n)
            with engine.Fori(0, 2) as it:
                for n in range(2, 4):
                    slot(it, n)
            for n in range(6, NG + 1):
                slot(0, n)

        def there(it, G):
            return not isinstance(it, int) or 0 <= G < NG

        def group_columns(it, G):
            return X[:, bass.ds(it * (2 * GT) + G * GT, GT)]

        @block.tensor
        def _(pe):
            def split_matmul(out, l, r, start=True, stop=True):
                pe.matmul(out, l[0], r[0], start=start, stop=False)
                pe.matmul(out, l[0], r[1], start=False, stop=False)
                return pe.matmul(out, l[1], r[0], start=False, stop=stop)

            def weight(block, width=P):
                return w_hi[:, block * P:block * P + width], w_lo[:, block * P:block * P + width]

            def xs(n, cols=slice(0, GT)):
                return x_hi[n % 2][:, cols], x_lo[n % 2][:, cols]

            def hidden_rows(it, n, k):
                i = NB * n + k
                if k == 0:
                    pe.wait_ge(tr_read, it * 6 + (turn['x', n] + 1))
                if n == 0 and isinstance(it, int) and k % C1 == 0:
                    pe.wait_ge(split_lo, k // C1 + 2)
                if i - 1 > 0:
                    pe.wait_ge(hidden_done, it * (2 * NB) + (i - 1))
                split_matmul(HT[i % 2][:, :], weight(k), xs(n)).then_inc(hidden_made, 1)

            def spread_gate(it, n, e):
                if e == 0:
                    pe.wait_ge(tr_read, it * 6 + (turn['g', n] + 1))
                if E1 * n + e > 0:
                    pe.wait_ge(gate_copied, it * (2 * E1) + (E1 * n + e))
                sel = cr[0:2 * E1, C_ONE_ROW + e * P:C_ONE_ROW + (e + 1) * P]
                pe.matmul(GATE[:, :], sel, g_parts[n % 2][:, :], start=True, stop=True).then_inc(gate_spread, 1)

            def mixed_bias(it, n):
                if n > 0:
                    pe.wait_ge(y_started, it * 2 + n)
                c = (2 * NB) * P
                pe.matmul(BT[:, :], w_hi[0:2 * E1, c:c + P], g_parts[n % 2][:, :], start=True, stop=False)
                pe.matmul(BT[:, :], w_lo[0:2 * E1, c:c + P], g_parts[n % 2][:, :], start=False, stop=True)\
                    .then_inc(bias_made, 1)

            def down(it, n, k):
                i, e = NB * n + k, k // C1
                pe.wait_ge(h_lo_done, it * (2 * NB) + (i + 1))
                if k % C1 == 0:
                    if E1 * n + e - 1 > 0:
                        pe.wait_ge(scaled_done, it * (2 * E1) + (E1 * n + e - 1))
                mm = split_matmul(YT[e % 2][:, :], weight(NB + k), (h_hi[i % 2][:, :], h_lo[i % 2][:, :]),
                                  start=k % C1 == 0, stop=k % C1 == C1 - 1)
                mm.then_inc(y_summed, 1)

            def transpose_x(it, n):
                pe.wait_ge(xn_done, it * (2 * GB) + (GB * (n + 1)))
                if turn['x', n] > 0:
                    pe.wait_ge(tr_read, it * 6 + turn['x', n])
                for b in range(GB):
                    mm = pe.transpose(TR[:, b * P:(b + 1) * P], xn[:, b, :], sb["ident"][:, :])
                mm.then_inc(x_transposed, 1)

            def make_logits(it, n):
                pe.wait_ge(tr_read, it * 6 + (turn['x', n] + 1))
                if RS * (n - 1) + 1 > 0:
                    pe.wait_ge(routed, it * (2 * RS) + (RS * (n - 1) + 1))
                for b in range(GB):
                    mm = split_matmul(LG[:, b * E1:(b + 1) * E1], xs(n, slice(b * P, (b + 1) * P)), weight(2 * NB + 1, E1))
                mm.then_inc(logits_made, 1)

            def transpose_gates(it, n):
                pe.wait_ge(routed, it * (2 * RS) + (RS * (n + 1)))
                pe.wait_ge(tr_read, it * 6 + turn['g', n])
                for b in range(GB):
                    mm = pe.transpose(TR[0:2 * E1, b * P:(b + 1) * P], gate_parts[:, b, :].bitcast(F32), sb["ident"][:, :])
                mm.then_inc(g_transposed, 1)

            def transpose_back(it, n):
                pe.wait_ge(y_added, it * (2 * E1) + (E1 * (n + 1)))
                pe.wait_ge(tr_read, it * 6 + turn['o', n])
                for b in range(GB):
                    mm = pe.transpose(TR[:, b * P:(b + 1) * P], y[n % 2][:, b * P:(b + 1) * P], sb["ident"][:, :])
                mm.then_inc(y_back, 1)

            def slot(it, n):
                for k in range(NB):
                    e, c = k // C1, k % C1
                    if there(it, n):
                        hidden_rows(it, n, k)
                    if k >= 2 and there(it, n):
                        down(it, n, k - 2)
                    elif k < 2 and there(it, n - 1):
                        down(it, n - 1, NB + k - 2)
                    if c == 3 and there(it, n):
                        spread_gate(it, n, e)
                    if k == 2 and there(it, n):
                        mixed_bias(it, n)
                    if (e, c) == (2, 0) and there(it, n - 1):
                        transpose_back(it, n - 1)
                    if (e, c) == (2, 2) and there(it, n + 1):
                        transpose_x(it, n + 1)
                    if (e, c) == (3, 2) and there(it, n + 1):
                        make_logits(it, n + 1)
                    if (e, c) == (7, 0) and there(it, n + 1):
                        transpose_gates(it, n + 1)

            pe.wait_ge(split_lo, 1)
            run(pe, slot)

        @block.scalar
        def _(act):
            def copy(out, src, done):
                act.activation(out, src, ACT.Copy).then_inc(done, 1)

            def copy_gate(it, n, e):
                act.wait_ge(gate_spread, it * (2 * E1) + (E1 * n + e + 1))
                if E1 * n + e > 0:
                    act.wait_ge(scaled_done, it * (2 * E1) + (E1 * n + e))
                copy(gate[:, :], GATE[:, :], gate_copied)

            def rectify(it, n, k):
                i = NB * n + k
                act.wait_ge(hidden_made, it * (2 * NB) + (i + 1))
                if i - 1 > 0:
                    act.wait_ge(h_lo_done, it * (2 * NB) + (i - 1))
                act.activation(hidden[i % 2][:, :], HT[i % 2][:, :], ACT.Relu,
                               bias=sb["cols"][:, N_COLS - NB + k:N_COLS - NB + k + 1]).then_inc(hidden_done, 1)
                if i - 1 > 0:
                    act.wait_ge(y_summed, it * (2 * NB) + (i - 1))
                act.wait_ge(hidden_done, it * (2 * NB) + (i + 1))
                copy(h_hi[i % 2][:, :], hidden[i % 2][:, :], h_hi_done)

            def slot(it, n):
                for k in range(NB):
                    e, c = k // C1, k % C1
                    if there(it, n):
                        rectify(it, n, k)
                    if c == 0 and e >= 1 and there(it, n):
                        copy_gate(it, n, e - 1)
                    if k == 0 and there(it, n - 1):
                        copy_gate(it, n - 1, E1 - 1)
                    if k == 3 and there(it, n):
                        act.wait_ge(bias_made, it * 2 + (n + 1))
                        if n - 1 > 0:
                            act.wait_ge(y_back, it * 2 + (n - 1))
                        copy(y[n % 2][:, :], BT[:, :], y_started)
                    if (e, c) == (2, 2) and there(it, n + 1):
                        act.wait_ge(x_transposed, it * 2 + (n + 2))
                        if NB * n > 0:
                            act.wait_ge(hidden_made, it * (2 * NB) + (NB * n))
                        copy(x_hi[(n + 1) % 2][:, :], TR[:, :], x_hi_done)
                    if (e, c) == (4, 1) and there(it, n + 1):
                        act.wait_ge(routed, it * (2 * RS) + (RS * (n + 1) + 3))
                        act.activation(exps[:, :, :], shifted[:, :, :], ACT.Exp).then_inc(exps_done, 1)

            act.wait_ge(ready["ffn1"], 16)
            for e in range(E1 + 1):
                for part in weight_parts(e):
                    op = act.activation(w_hi[:, part], raw[:, part], ACT.Copy)
                    op.then_inc(split, 1)
            run(act, slot)

        @block.vector
        def _(dve):
            def hidden_lo(it, n, k):
                i = NB * n + k
                dve.wait_ge(h_hi_done, it * (2 * NB) + (i + 1))
                if i - 1 > 0:
                    dve.wait_ge(y_summed, it * (2 * NB) + (i - 1))
                dve.tensor_tensor(h_lo[i % 2][:, :], hidden[i % 2][:, :], h_hi[i % 2][:, :].bitcast(F32),
                                  ALU.subtract).then_inc(h_lo_done, 1)

            def scale_expert(it, n, e):
                i = E1 * n + e
                dve.wait_ge(gate_copied, it * (2 * E1) + (i + 1))
                dve.wait_ge(y_summed, it * (2 * NB) + (NB * n + C1 * (e + 1)))
                if i - 1 > 0:
                    dve.wait_ge(y_added, it * (2 * E1) + (i - 1))
                dve.tensor_tensor(scaled[i % 2][:, :], gate[:, :], YT[e % 2][:, :], ALU.mult)\
                    .then_inc(scaled_done, 1)

            def split_weights(e):
                for i, part in enumerate(weight_parts(e)):
                    dve.wait_ge(split, max(0, 2 * e - 1) + i + 1)
                    op = dve.tensor_tensor(w_lo[:, part], raw[:, part], w_hi[:, part].bitcast(F32), ALU.subtract)
                op.then_inc(split_lo, 1)

            def by_expert(x):
                return x.unsqueeze(2).broadcast_to([P, GB, E1])

            def route(it, n, steps):
                base = RS * n
                l = logits[:, :, :]
                mine = probs[:, :, :].unsqueeze(3).broadcast_to([P, GB, E1, E1])
                other = probs[:, :, :].unsqueeze(2).broadcast_to([P, GB, E1, E1])
                for s in steps:
                    if s == 0:
                        dve.wait_ge(logits_made, it * 2 + (n + 1))
                    if s == 3:
                        dve.wait_ge(exps_done, it * 2 + (n + 1))
                    if s == 13:
                        if n > 0:
                            dve.wait_ge(g_transposed, it * 2 + n)
                    if base + s > 0:
                        dve.wait_ge(routed, it * (2 * RS) + (base + s))
                    if s == 0:
                        op = dve.tensor_tensor(l, LG[:, 0:GB * E1].rearrange("p (b e) -> p b e", e=E1),
                                               router_b.unsqueeze(1).broadcast_to([P, GB, E1]), ALU.add)
                    elif s == 1:
                        op = dve.tensor_reduce(top[:, :], l, AX.X, ALU.max)
                    elif s == 2:
                        op = dve.tensor_tensor(shifted[:, :, :], l, by_expert(top[:, :]), ALU.subtract)
                    elif s in (3, 10):
                        op = dve.tensor_reduce(total[:, :], exps[:, :, :] if s == 3 else chosen[:, :, :], AX.X, ALU.add)
                    elif s in (4, 11):
                        op = dve.reciprocal(recip[:, :], total[:, :])
                    elif s == 5:
                        op = dve.tensor_tensor(probs[:, :, :], exps[:, :, :], by_expert(recip[:, :]), ALU.mult)
                    elif s == 6:
                        op = dve.tensor_tensor(equal[:, :, :, :], other, mine, ALU.is_equal)
                    elif s == 7:
                        dve.tensor_tensor(equal[:, :, :, :], equal[:, :, :, :],
                                          earlier.unsqueeze(1).broadcast_to([P, GB, E1, E1]), ALU.mult)\
                            .then_inc(product_summed, 1)
                        op = dve.tensor_tensor(above[:, :, :, :], other, mine, ALU.is_gt)
                    elif s == 8:
                        dve.tensor_tensor(above[:, :, :, :], above[:, :, :, :], equal[:, :, :, :], ALU.add)\
                            .then_inc(product_summed, 1)
                        dve.wait_ge(product_summed, it * 4 + (2 * n + 2))
                        op = dve.tensor_reduce(rank[:, :, :], above[:, :, :, :], AX.X, ALU.add)
                    elif s == 9:
                        op = dve.scalar_tensor_tensor(chosen[:, :, :], rank[:, :, :], 2.0, probs[:, :, :],
                                                      ALU.is_lt, ALU.mult)
                    elif s == 12:
                        op = dve.tensor_tensor(gates[:, :, :], chosen[:, :, :], by_expert(recip[:, :]), ALU.mult)
                    elif s == 13:
                        op = dve.tensor_copy(gate_parts[:, :, 0:E1], gates[:, :, :])
                    else:
                        op = dve.tensor_tensor(gate_parts[:, :, E1:2 * E1], gates[:, :, :],
                                               gate_parts[:, :, 0:E1].bitcast(F32), ALU.subtract)
                    op.then_inc(routed, 1)

            def moments(it, G):
                if GB * G > 0:
                    dve.wait_ge(xn_done, it * (2 * GB) + (GB * G))
                if GB * G > 0:
                    dve.wait_ge(mean_done, it * (2 * GB) + (GB * G))
                if G > 0:
                    dve.wait_ge(rstd_done, it * 2 + G)
                for b in range(GB):
                    dve.bn_stats(stats[:, b, :], X[:, bass.ds(it * (2 * GT) + G * GT + b * P, P)])\
                        .then_inc(stats_done, 1)
                dve.wait_ge(stats_done, it * (2 * GB) + (GB * (G + 1)))
                dve.sem_inc(passed, 1)
                for b in range(GB):
                    dve.bn_aggr(mean_var[:, b, :], stats[:, b, :]).then_inc(mean_done, 1)

            def layernorm(it, G):
                dve.wait_ge(rstd_done, it * 2 + (G + 1))
                dve.wait_ge(mean_done, it * (2 * GB) + (GB * (G + 1)))
                if G > 0:
                    dve.wait_ge(x_transposed, it * 2 + G)
                for b in range(GB):
                    dve.tensor_scalar(xn[:, b, :], X[:, bass.ds(it * (2 * GT) + G * GT + b * P, P)],
                                      mean_var[:, b, 0:1], rstd[:, b:b + 1], ALU.subtract, ALU.mult)\
                        .then_inc(xn_done, 1)

            def slot(it, n):
                for k in range(NB):
                    e, c = k // C1, k % C1
                    if there(it, n):
                        hidden_lo(it, n, k)
                    if c == 2 and e >= 1 and there(it, n):
                        scale_expert(it, n, e - 1)
                    if k == 2 and there(it, n - 1):
                        scale_expert(it, n - 1, E1 - 1)
                    if (e, c) == (2, 0) and there(it, n - 1):
                        dve.wait_ge(y_back, it * 2 + n)
                        dve.wait_ge(xn_done, it * (2 * GB) + (GB * n))
                        x = group_columns(it, n - 1)
                        dve.tensor_tensor(x, TR[:, :], x, ALU.add).then_inc(tr_read, 1)
                    if (e, c) == (2, 3) and there(it, n + 1):
                        dve.wait_ge(x_hi_done, it * 2 + (n + 2))
                        dve.tensor_tensor(x_lo[(n + 1) % 2][:, :], TR[:, :], x_hi[(n + 1) % 2][:, :].bitcast(F32),
                                          ALU.subtract).then_inc(tr_read, 1)
                    if (e, c) == (4, 0) and there(it, n + 1):
                        route(it, n + 1, range(0, 3))
                    if (e, c) == (4, 3) and there(it, n + 1):
                        route(it, n + 1, range(3, 5))
                    if (e, c) == (5, 0) and there(it, n + 1):
                        route(it, n + 1, range(5, 7))
                    if (e, c) == (5, 1) and there(it, n + 1):
                        route(it, n + 1, range(7, 8))
                    if (e, c) == (5, 3) and there(it, n + 1):
                        route(it, n + 1, range(8, 10))
                    if (e, c) == (6, 1) and there(it, n + 1):
                        route(it, n + 1, range(10, RS))
                    if (e, c) == (3, 0) and there(it, n + 2):
                        moments(it, n + 2)
                    if n == -2 and (e, c) == (3, 1):
                        split_weights(1)
                    if n == -1 and e >= 1 and c == 3:
                        split_weights(e + 1)
                    if (e, c) == (6, 3) and there(it, n + 2):
                        layernorm(it, n + 2)
                    if (e, c) == (7, 1) and there(it, n + 1):
                        dve.wait_ge(g_transposed, it * 2 + (n + 2))
                        if E1 * n > 0:
                            dve.wait_ge(gate_spread, it * (2 * E1) + (E1 * n))
                        dve.tensor_copy(g_parts[(n + 1) % 2][:, :], TR[0:2 * E1, :]).then_inc(tr_read, 1)

            split_weights(0)
            run(dve, slot)

        @block.gpsimd
        def _(pool):
            def add_expert(it, n, e):
                i = E1 * n + e
                pool.wait_ge(scaled_done, it * (2 * E1) + (i + 1))
                pool.wait_ge(y_started, it * 2 + (n + 1))
                if i > 0:
                    pool.wait_ge(y_added, it * (2 * E1) + i)
                pool.tensor_tensor(y[n % 2][:, :], y[n % 2][:, :], scaled[i % 2][:, :], ALU.add).then_inc(y_added, 1)

            def reciprocal_deviation(it, G):
                pool.wait_ge(mean_done, it * (2 * GB) + (GB * (G + 1)))
                if GB * G > 0:
                    pool.wait_ge(xn_done, it * (2 * GB) + (GB * G))
                if G > 0:
                    pool.wait_ge(rstd_done, it * 2 + G)
                pool.sem_inc(passed, 1)
                pool.tensor_scalar(var_eps[:, :], mean_var[:, :, 1], LN_EPS, 1.0, ALU.add, ALU.mult)\
                    .then_inc(var_done, 1)
                pool.wait_ge(var_done, it * 2 + (G + 1))
                pool.tensor_tensor(rstd[:, :], var_eps[:, :], power[:, :], ALU.pow).then_inc(rstd_done, 1)

            def slot(it, n):
                for e in range(E1):
                    if e >= 1 and there(it, n):
                        add_expert(it, n, e - 1)
                    elif e == 0 and there(it, n - 1):
                        add_expert(it, n - 1, E1 - 1)
                    if e == 3 and there(it, n + 2):
                        reciprocal_deviation(it, n + 2)

            pool.sem_clear(used_before)
            pool.memset(power[:, :], -0.5).then_inc(power_done, 1)
            pool.wait_ge(power_done, 1)
            run(pool, slot)


def latent_attention(nc, phase, sb, ps, t, ready):
    kc, HL, DL = DC, 2, D // 2
    X = sb["x"]
    TR, PL, PC, KT, S, T, O, M = ps
    cr, cols = sb["const_r"], sb["cols"]
    ident, ident_r = sb["ident"][:, :], cr[:, C_ID:C_ID + P]
    diag = sb["const"][0:32, 0:HL]
    c = C_HEAD - N_CONST_R
    head_rows = sb["const"][:, c:c + HL]
    ctx_g, ctx_b, lat_g, lat_b, q_gamma, k_gamma = (cols[:, COL_LATENT + n:COL_LATENT + n + 1] for n in range(6))
    bo_hi, bo_lo = (sb[r][:, R_LATENT:R_LATENT + P] for r in ("rows_hi", "rows_lo"))

    turn = {}
    for n in range(-6, B + 2):
        for name, m in (("y", n - 2), ("m", n), ("o", n - 1)):
            if 0 <= m < B:
                turn[name, m] = len(turn)

    with ExitStack() as ctx:
        def buf(name, shape, dt=F32):
            return ctx.enter_context(nc.sbuf_tensor(f"latent_{name}", shape, dt))

        sem, used_before = phase_semaphores(nc, ctx, phase, "latent")
        raw = sb["raw_xattn1"]
        w_hi, w_lo = buf("w_hi", [P, W_LATENT], F32R), buf("w_lo", [P, W_LATENT], F32R)
        mask_rows = buf("mask_rows", [P, B * P], F32R)
        mask_cols, masked = buf("mask_cols", [P, B]), buf("masked", [P, 1])
        gamma, head_gamma = buf("gamma", [P, 1]), buf("head_gamma", [P, HL])
        ctx_in = buf("ctx_in", [P, GB, DC])
        stats, mean_var = buf("stats", [P, 2 * GB, 6]), buf("mean_var", [P, 2 * GB, 2])
        var_eps, rstd = buf("var_eps", [P, 2 * GB]), buf("rstd", [P, 2 * GB])
        power = buf("power", [P, 2 * GB])
        xn, cn = buf("xn", [P, GB, D]), buf("cn", [P, GB, DC])
        xf, cf = buf("xf", [P, GT]), buf("cf", [kc, GT])
        x_hi, x_lo = ([buf(f"x_{w}{i}", [P, GT], F32R) for i in range(2)] for w in ("hi", "lo"))
        c_hi, c_lo = ([buf(f"c_{w}{i}", [kc, GT], F32R) for i in range(2)] for w in ("hi", "lo"))
        squares = buf("squares", [P, 3 * P])
        norms, norms_kept, inverse = buf("norms", [P, 3 * HL]), buf("norms_kept", [P, 3 * HL]), buf("inverse", [P, 3 * HL])
        unit = [buf(f"unit{i}", [P, 3, P]) for i in range(2)]
        v = [buf(f"v{i}", [P, 2, HL, DL + 1]) for i in range(8)]
        q_heads = buf("q_heads", [P, HL, P])
        q_hi, q_lo, k_hi, k_lo = ([buf(f"{w}{i}", [P, 2 * P], F32R) for i in range(4)]
                                  for w in ("q_hi", "q_lo", "k_hi", "k_lo"))
        maxes = buf("maxes", [P, 32])
        neg_max = buf("neg_max", [32, HL, P], F32R)
        probs = [buf(f"probs{i}", [P, 2, HL * P]) for i in range(2)]
        recip, heads = buf("recip", [P, HL]), buf("heads", [P, HL, DL])
        o_hi, o_lo = buf("o_hi", [P, P], F32R), buf("o_lo", [P, P], F32R)

        x_transposed, c_transposed = sem("x_transposed"), sem("c_transposed")
        projected, keys_transposed = sem("projected"), sem("keys_transposed")
        scored, max_transposed, shifted = sem("scored"), sem("max_transposed"), sem("shifted")
        weighted, o_transposed, out_projected = sem("weighted"), sem("o_transposed"), sem("out_projected")
        affine_done, squares_done, v_done = sem("affine_done"), sem("squares_done"), sem("v_done")
        exp_done, k_hi_done, q_hi_done, o_hi_done = sem("exp_done"), sem("k_hi_done"), sem("q_hi_done"), sem("o_hi_done")
        setup_steps, masks_made = sem("setup_steps"), sem("masks_made")
        stats_done, mean_done, normal_done, hi_done = sem("stats_done"), sem("mean_done"), sem("normal_done"), sem("hi_done")
        norms_done, norms_bounded, unit_done = sem("norms_done"), sem("norms_bounded"), sem("unit_done")
        q_heads_done, k_lo_done = sem("q_heads_done"), sem("k_lo_done")
        max_done, m_read, recip_done, heads_done = sem("max_done"), sem("m_read"), sem("recip_done"), sem("heads_done")
        filled, var_done, rstd_done = sem("filled"), sem("var_done"), sem("rstd_done")
        lo_done, inverse_done, q_lo_done = sem("lo_done"), sem("inverse_done"), sem("q_lo_done")
        ctx_loaded, passed = sem("ctx_loaded"), sem("passed")
        SETUP = 5

        block = ctx.enter_context(nc.Block())

        def run(engine, slot):
            for n in range(-6, 2):
                slot(0, n)
            with engine.Fori(0, 3) as it:
                for n in range(2, 10):
                    slot(it, n)
            for n in range(26, B + 2):
                slot(0, n)

        def there(it, n):
            return not isinstance(it, int) or 0 <= n < B

        def group(it, G):
            return not isinstance(it, int) or 0 <= G < NG

        def split_parts(tiles, n):
            cols = slice((n % GB) * P, (n % GB + 1) * P)
            return tuple(x[(n // GB) % 2][:, cols] for x in tiles)

        @block.tensor
        def _(pe):
            def split_matmul(out, l, r, start=True, stop=True):
                pe.matmul(out, l[0], r[0], start=start, stop=False)
                pe.matmul(out, l[0], r[1], start=False, stop=False)
                return pe.matmul(out, l[1], r[0], start=False, stop=stop)

            def transpose_inputs(it, G):
                pe.wait_ge(normal_done, it * (4 * GB) + (2 * GB * G + GB))
                if 2 * G > 0:
                    pe.wait_ge(affine_done, it * 4 + (2 * G))
                for b in range(GB):
                    mm = pe.transpose(TR[:, b * P:(b + 1) * P], xn[:, b, :], ident)
                mm.then_inc(x_transposed, 1)

            def transpose_context(it, G):
                pe.wait_ge(normal_done, it * (4 * GB) + 2 * GB * (G + 1))
                pe.wait_ge(affine_done, it * 4 + (2 * G + 1))
                for b in range(GB):
                    mm = pe.transpose(TR[0:kc, b * P:(b + 1) * P], cn[:, b, :], ident)
                mm.then_inc(c_transposed, 1)

            def project(it, n):
                pe.wait_ge(lo_done, it * 4 + (2 * (n // GB) + 2))
                if 2 * n > 0:
                    pe.wait_ge(unit_done, it * 16 + (2 * n))
                if 2 * n > 0:
                    pe.wait_ge(v_done, it * 16 + (2 * n))
                split_matmul(PL[:, 0:3 * P], split_parts((x_hi, x_lo), n), (w_hi[:, 0:3 * P], w_lo[:, 0:3 * P]))
                split_matmul(PC[:, 0:2 * P], split_parts((c_hi, c_lo), n),
                             (w_hi[0:kc, 3 * P:5 * P], w_lo[0:kc, 3 * P:5 * P])).then_inc(projected, 1)

            def transpose_keys(it, n):
                pe.wait_ge(unit_done, it * 16 + (2 * n + 2))
                if n > 0:
                    pe.wait_ge(k_lo_done, it * 8 + n)
                for i in range(3):
                    mm = pe.transpose(KT[:, i * P:(i + 1) * P], unit[n % 2][:, i, :], ident)
                mm.then_inc(keys_transposed, 1)

            def scores(it, n):
                pe.wait_ge(q_lo_done, it * 8 + (n + 1))
                pe.wait_ge(k_lo_done, it * 8 + (n + 1))
                if n > 0:
                    pe.wait_ge(max_done, it * 8 + n)
                for h in range(HL):
                    pe.matmul(S[:, h * 2 * P:(h + 1) * 2 * P], q_hi[n % 4][:, h * P:(h + 1) * P], k_hi[n % 4][:, :],
                              start=True, stop=False)
                    mm = pe.matmul(S[:, h * 2 * P + P:(h + 1) * 2 * P], ident_r,
                                   mask_rows[:, bass.ds(it * (8 * P) + n * P, P)], start=False, stop=True)
                mm.then_inc(scored, 1)

            def key_scores(it, n):
                if 2 * n > 0:
                    pe.wait_ge(exp_done, it * 16 + (2 * n))
                q = (q_hi[n % 4][:, :], q_lo[n % 4][:, :])
                for i in range(2):
                    keys = slice(i * P, (i + 1) * P)
                    split_matmul(T[:, i * 2 * P:(i + 1) * 2 * P], (k_hi[n % 4][:, keys], k_lo[n % 4][:, keys]), q,
                                 start=i == 0, stop=False)

            def transpose_max(it, n):
                pe.wait_ge(max_done, it * 8 + (n + 1))
                if turn['m', n] > 0:
                    pe.wait_ge(m_read, it * 24 + turn['m', n])
                pe.transpose(M[0:32, 0:P], maxes[:, :], ident).then_inc(max_transposed, 1)

            def shift(it, n):
                pe.wait_ge(m_read, it * 24 + (turn['m', n] + 1))
                for i in range(2):
                    mm = pe.matmul(T[:, i * 2 * P:(i + 1) * 2 * P], cr[0:32, C_ONES:C_ONES + P],
                                   neg_max[:, :, :].rearrange("p h q -> p (h q)"), start=False, stop=i == 1)
                mm.then_inc(shifted, 1)

            def weigh(it, n):
                pe.wait_ge(exp_done, it * 16 + (2 * n + 2))
                pe.wait_ge(v_done, it * 16 + (2 * n + 2))
                if n > 0:
                    pe.wait_ge(heads_done, it * 8 + n)
                for h in range(HL):
                    for i in range(2):
                        mm = pe.matmul(O[:, h * (DL + 1):(h + 1) * (DL + 1)], probs[n % 2][:, i, h * P:(h + 1) * P],
                                       v[n % 8][:, i, h, :], start=i == 0, stop=i == 1)
                mm.then_inc(weighted, 1)

            def transpose_heads(it, n):
                pe.wait_ge(heads_done, it * 8 + (n + 1))
                pe.wait_ge(m_read, it * 24 + turn['o', n])
                pe.transpose(M[:, 0:P], heads[:, :, :].rearrange("p h d -> p (h d)"), ident).then_inc(o_transposed, 1)

            def out_project(it, n):
                pe.wait_ge(m_read, it * 24 + (turn['o', n] + 1))
                pe.wait_ge(m_read, it * 24 + turn['y', n])
                pe.matmul(M[:, 0:P], ident_r, bo_hi, start=True, stop=False)
                pe.matmul(M[:, 0:P], ident_r, bo_lo, start=False, stop=False)
                split_matmul(M[:, 0:P], (o_hi[:, :], o_lo[:, :]), (w_hi[:, 5 * P:6 * P], w_lo[:, 5 * P:6 * P]),
                             start=False).then_inc(out_projected, 1)

            def slot(it, n):
                G, b = n // GB, n % GB
                if there(it, n):
                    scores(it, n)
                    key_scores(it, n)
                if there(it, n + 3):
                    project(it, n + 3)
                if there(it, n - 2):
                    out_project(it, n - 2)
                if there(it, n + 2):
                    transpose_keys(it, n + 2)
                if there(it, n):
                    transpose_max(it, n)
                if there(it, n - 1):
                    weigh(it, n - 1)
                if b == 3 and group(it, G + 2):
                    transpose_inputs(it, G + 2)
                if b == 0 and group(it, G + 1):
                    transpose_context(it, G + 1)
                if there(it, n):
                    shift(it, n)
                if there(it, n - 1):
                    transpose_heads(it, n - 1)

            pe.wait_ge(setup_steps, SETUP)
            pe.wait_ge(masks_made, 1)
            pe.wait_ge(filled, 19)
            run(pe, slot)

        @block.scalar
        def _(act):
            def square(it, n):
                act.wait_ge(projected, it * 8 + (n + 1))
                if n > 0:
                    act.wait_ge(norms_done, it * 8 + n)
                act.activation(squares[:, 0:2 * P], PL[:, 0:2 * P], ACT.Square).then_inc(squares_done, 1)
                act.activation(squares[:, 2 * P:3 * P], PC[:, 0:P], ACT.Square).then_inc(squares_done, 1)

            def copy_values(it, n):
                if n - 7 > 0:
                    act.wait_ge(weighted, it * 8 + (n - 7))
                for i, src in ((1, PC[:, P:2 * P]), (0, PL[:, 2 * P:3 * P])):
                    act.activation(v[n % 8][:, i, :, 0:DL], src.rearrange("p (h d) -> p h d", h=HL), ACT.Copy)\
                        .then_inc(v_done, 1)

            def exps(it, n):
                act.wait_ge(shifted, it * 8 + (n + 1))
                if n - 1 > 0:
                    act.wait_ge(weighted, it * 8 + (n - 1))
                act.activation(probs[n % 2][:, 0, :], T[:, 0:2 * P], ACT.Exp, scale=DL ** -0.5).then_inc(exp_done, 1)
                act.activation(probs[n % 2][:, 1, :], T[:, 2 * P:4 * P], ACT.Exp, scale=DL ** -0.5,
                               bias=mask_cols[:, bass.ds(it * 8 + n, 1)]).then_inc(exp_done, 1)

            def key_hi(it, n):
                act.wait_ge(q_heads_done, it * 8 + (n + 1))
                if n - 3 > 0:
                    act.wait_ge(shifted, it * 8 + (n - 3))
                act.activation(k_hi[n % 4][:, :], KT[:, P:3 * P], ACT.Copy).then_inc(k_hi_done, 1)
                act.activation(q_hi[n % 4][:, :], q_heads[:, :, :].rearrange("p h q -> p (h q)"), ACT.Copy)\
                    .then_inc(q_hi_done, 1)

            def affine(it, G, i):
                act.wait_ge((x_transposed, c_transposed)[i], it * 2 + (G + 1))
                if 2 * G + i - 1 > 0:
                    act.wait_ge(hi_done, it * 4 + (2 * G + i - 1))
                if 2 * G + i - 1 > 0:
                    act.wait_ge(lo_done, it * 4 + (2 * G + i - 1))
                if i == 0:
                    act.activation(xf[:, :], TR[:, :], ACT.Identity, bias=lat_b, scale=lat_g).then_inc(affine_done, 1)
                else:
                    act.activation(cf[:, :], TR[0:kc, :], ACT.Identity, bias=ctx_b[0:kc, :], scale=ctx_g[0:kc, :])\
                        .then_inc(affine_done, 1)

            def slot(it, n):
                G, b = n // GB, n % GB
                if there(it, n + 3):
                    square(it, n + 3)
                if there(it, n + 2):
                    key_hi(it, n + 2)
                if there(it, n + 3):
                    copy_values(it, n + 3)
                if there(it, n):
                    exps(it, n)
                if b == 0 and group(it, G + 1):
                    affine(it, G + 1, 1)
                if there(it, n - 1):
                    act.wait_ge(o_transposed, it * 8 + n)
                    if n - 1 > 0:
                        act.wait_ge(out_projected, it * 8 + (n - 1))
                    act.activation(o_hi[:, :], M[:, 0:P], ACT.Copy).then_inc(o_hi_done, 1)
                if b == 3 and group(it, G + 2):
                    affine(it, G + 2, 0)

            act.wait_ge(filled, 19)
            act.wait_ge(ready["xattn1"], 48)
            act.activation(mask_rows[:, :], sb["mask_by_row"][:, :], ACT.Identity, scale=-MASKED,
                           bias=masked[:, :]).then_inc(masks_made, 1)
            run(act, slot)

        @block.vector
        def _(dve):
            def moments(it, G):
                if 2 * GB * G > 0:
                    dve.wait_ge(normal_done, it * (4 * GB) + (2 * GB * G))
                if 2 * GB * G > 0:
                    dve.wait_ge(mean_done, it * (4 * GB) + (2 * GB * G))
                if G > 0:
                    dve.wait_ge(rstd_done, it * 2 + G)
                dve.wait_ge(ctx_loaded, it * 32 + (16 * (G + 1)))
                for b in range(GB):
                    dve.bn_stats(stats[:, b, :], ctx_in[:, b, :]).then_inc(stats_done, 1)
                    dve.bn_stats(stats[:, GB + b, :], batch_columns(X, it, GB * G + b)).then_inc(stats_done, 1)
                dve.wait_ge(stats_done, it * (4 * GB) + (2 * GB * (G + 1)))
                dve.sem_inc(passed, 1)
                for b in range(2 * GB):
                    dve.bn_aggr(mean_var[:, b, :], stats[:, b, :]).then_inc(mean_done, 1)

            def normal(it, G, i):
                if i == 0:
                    dve.wait_ge(rstd_done, it * 2 + (G + 1))
                    dve.wait_ge(mean_done, it * (4 * GB) + 2 * GB * (G + 1))
                    if G > 0:
                        dve.wait_ge(x_transposed, it * 2 + G)
                elif G > 0:
                    dve.wait_ge(c_transposed, it * 2 + G)
                for b in range(GB):
                    if i == 0:
                        op = dve.tensor_scalar(xn[:, b, :], batch_columns(X, it, GB * G + b), mean_var[:, GB + b, 0:1],
                                               rstd[:, GB + b:GB + b + 1], ALU.subtract, ALU.mult)
                    else:
                        op = dve.tensor_scalar(cn[:, b, :], ctx_in[:, b, :], mean_var[:, b, 0:1],
                                               rstd[:, b:b + 1], ALU.subtract, ALU.mult)
                    op.then_inc(normal_done, 1)

            def input_hi(it, G, i):
                dve.wait_ge(affine_done, it * 4 + (2 * G + i + 1))
                if GB * (G - 1) > 0:
                    dve.wait_ge(projected, it * 8 + (GB * (G - 1)))
                out, src = ((x_hi, xf), (c_hi, cf))[i]
                dve.tensor_copy(out[G % 2][:, :], src[:, :]).then_inc(hi_done, 1)

            def sum_squares(it, n):
                dve.wait_ge(squares_done, it * 16 + (2 * n + 2))
                if n > 0:
                    dve.wait_ge(norms_bounded, it * 8 + n)
                dve.tensor_reduce(norms[:, :], squares[:, :].rearrange("p (h d) -> p h d", d=DL), AX.X, ALU.add)\
                    .then_inc(norms_done, 1)
                dve.wait_ge(norms_done, it * 8 + (n + 1))
                if n > 0:
                    dve.wait_ge(inverse_done, it * 8 + n)
                dve.tensor_scalar(norms_kept[:, :], norms[:, :], 1.0 / DL, RMS_EPS ** 2, ALU.mult, ALU.max)\
                    .then_inc(norms_bounded, 1)

            def normalise(it, n):
                dve.wait_ge(inverse_done, it * 8 + (n + 1))
                dve.wait_ge(v_done, it * 16 + (2 * n + 2))
                if n - 1 > 0:
                    dve.wait_ge(keys_transposed, it * 8 + (n - 1))
                for lo, hi, src in ((0, 2, PL[:, 0:2 * P]), (2, 3, PC[:, 0:P])):
                    dve.tensor_tensor(unit[n % 2][:, lo:hi, :].rearrange("p a (h d) -> p (a h) d", d=DL),
                                      src.rearrange("p (h d) -> p h d", d=DL),
                                      inverse[:, HL * lo:HL * hi].unsqueeze(2).broadcast_to([P, HL * (hi - lo), DL]),
                                      ALU.mult).then_inc(unit_done, 1)

            def split_heads(it, n):
                dve.wait_ge(keys_transposed, it * 8 + (n + 1))
                if n > 0:
                    dve.wait_ge(q_lo_done, it * 8 + n)
                dve.tensor_tensor(q_heads[:, :, :], KT[:, 0:P].unsqueeze(1).broadcast_to([P, HL, P]),
                                  head_gamma[:, :].unsqueeze(2).broadcast_to([P, HL, P]), ALU.mult)\
                    .then_inc(q_heads_done, 1)

            def largest(it, n):
                dve.wait_ge(scored, it * 8 + (n + 1))
                if n > 0:
                    dve.wait_ge(max_transposed, it * 8 + n)
                dve.tensor_reduce(maxes[:, 0:HL], S[:, :].rearrange("p (h k) -> p h k", h=HL), AX.X, ALU.max,
                                  negate=True).then_inc(max_done, 1)

            def add_output(it, n):
                dve.wait_ge(out_projected, it * 8 + (n + 1))
                dve.wait_ge(normal_done, it * (4 * GB) + 2 * GB * (n // GB + 1))
                x = batch_columns(X, it, n)
                dve.tensor_tensor(x, M[:, 0:P], x, ALU.add).then_inc(m_read, 1)

            def spread_max(it, n):
                dve.wait_ge(max_transposed, it * 8 + (n + 1))
                if n > 0:
                    dve.wait_ge(shifted, it * 8 + n)
                dve.tensor_tensor(neg_max[:, :, :], M[0:32, 0:P].unsqueeze(1).broadcast_to([32, HL, P]),
                                  diag.unsqueeze(2).broadcast_to([32, HL, P]), ALU.mult).then_inc(m_read, 1)

            def divide(it, n):
                dve.wait_ge(weighted, it * 8 + (n + 1))
                if n > 0:
                    dve.wait_ge(heads_done, it * 8 + n)
                    dve.wait_ge(o_transposed, it * 8 + n)
                o = O[:, 0:HL * (DL + 1)].rearrange("p (h c) -> p h c", h=HL)
                dve.reciprocal(recip[:, :], o[:, :, DL]).then_inc(recip_done, 1)
                dve.wait_ge(recip_done, it * 8 + (n + 1))
                dve.tensor_tensor(heads[:, :, :], o[:, :, 0:DL], recip[:, :].unsqueeze(2).broadcast_to([P, HL, DL]),
                                  ALU.mult).then_inc(heads_done, 1)

            def key_lo(it, n):
                dve.wait_ge(k_hi_done, it * 8 + (n + 1))
                if n - 3 > 0:
                    dve.wait_ge(shifted, it * 8 + (n - 3))
                dve.tensor_tensor(k_lo[n % 4][:, :], KT[:, P:3 * P], k_hi[n % 4][:, :].bitcast(F32),
                                  ALU.subtract).then_inc(k_lo_done, 1)

            def slot(it, n):
                G, b = n // GB, n % GB
                if there(it, n + 2):
                    normalise(it, n + 2)
                if there(it, n):
                    largest(it, n)
                if b == 2 and group(it, G + 2):
                    moments(it, G + 2)
                if b == 0 and group(it, G + 1):
                    input_hi(it, G + 1, 0)
                if there(it, n - 2):
                    add_output(it, n - 2)
                if there(it, n + 2):
                    split_heads(it, n + 2)
                if there(it, n):
                    spread_max(it, n)
                if there(it, n + 3):
                    sum_squares(it, n + 3)
                if there(it, n - 1):
                    divide(it, n - 1)
                if b == 3 and group(it, G + 2):
                    normal(it, G + 2, 1)
                if there(it, n + 2):
                    key_lo(it, n + 2)
                if there(it, n - 1):
                    dve.wait_ge(o_hi_done, it * 8 + n)
                    dve.tensor_tensor(o_lo[:, :], M[:, 0:P], o_hi[:, :].bitcast(F32), ALU.subtract).then_inc(m_read, 1)
                if b == 2 and group(it, G + 2):
                    normal(it, G + 2, 0)
                if b == 0 and group(it, G + 1):
                    input_hi(it, G + 1, 1)

            dve.wait_ge(ready["xattn1"], 48)
            dve.tensor_copy(w_hi[:, :], raw[:, :]).then_inc(setup_steps, 1)
            dve.tensor_tensor(gamma[:, :], q_gamma, k_gamma, ALU.mult).then_inc(setup_steps, 1)
            dve.tensor_scalar(mask_cols[:, :], sb["mask_by_col"][:, :], -1.0, -MASKED, ALU.add, ALU.mult)\
                .then_inc(setup_steps, 1)
            dve.wait_ge(setup_steps, 3)
            dve.tensor_tensor(w_lo[:, :], raw[:, :], w_hi[:, :].bitcast(F32), ALU.subtract).then_inc(setup_steps, 1)
            dve.tensor_scalar(head_gamma[:, :], head_rows, gamma[:, :], None, ALU.mult).then_inc(setup_steps, 1)
            run(dve, slot)

        @block.gpsimd
        def _(pool):
            def reciprocal_deviations(it, G):
                pool.wait_ge(mean_done, it * (4 * GB) + 2 * GB * (G + 1))
                if G > 0:
                    pool.wait_ge(normal_done, it * (4 * GB) + 2 * GB * G)
                    pool.wait_ge(rstd_done, it * 2 + G)
                pool.sem_inc(passed, 1)
                pool.tensor_scalar(var_eps[:, 0:GB], mean_var[:, 0:GB, 1], LN_EPS, 1.0, ALU.add, ALU.mult)\
                    .then_inc(var_done, 1)
                pool.tensor_scalar(var_eps[:, GB:], mean_var[:, GB:, 1], 1 + LN_EPS, LN_EPS ** 2, ALU.mult, ALU.add)\
                    .then_inc(var_done, 1)
                pool.wait_ge(var_done, it * 4 + (2 * G + 2))
                pool.tensor_tensor(rstd[:, :], var_eps[:, :], power[:, :], ALU.pow).then_inc(rstd_done, 1)

            def input_lo(it, G, i):
                pool.wait_ge(hi_done, it * 4 + (2 * G + i + 1))
                if GB * (G - 1) > 0:
                    pool.wait_ge(projected, it * 8 + (GB * (G - 1)))
                out, src, hi = ((x_lo, xf, x_hi), (c_lo, cf, c_hi))[i]
                pool.tensor_tensor(out[G % 2][:, :], src[:, :], hi[G % 2][:, :].bitcast(F32), ALU.subtract)\
                    .then_inc(lo_done, 1)

            def query_lo(it, n):
                pool.wait_ge(q_hi_done, it * 8 + (n + 1))
                if n - 3 > 0:
                    pool.wait_ge(shifted, it * 8 + (n - 3))
                pool.tensor_tensor(q_lo[n % 4][:, :], q_heads[:, :, :].rearrange("p h q -> p (h q)"),
                                   q_hi[n % 4][:, :].bitcast(F32), ALU.subtract).then_inc(q_lo_done, 1)

            def invert(it, n):
                pool.wait_ge(norms_bounded, it * 8 + (n + 1))
                if n > 0:
                    pool.wait_ge(unit_done, it * 16 + 2 * n)
                pool.tensor_tensor(inverse[:, :], norms_kept[:, :], power[:, 0:3 * HL], ALU.pow)\
                    .then_inc(inverse_done, 1)

            def slot(it, n):
                G, b = n // GB, n % GB
                if b == 0 and group(it, G + 1):
                    input_lo(it, G + 1, 0)
                if b == 2 and group(it, G + 2):
                    reciprocal_deviations(it, G + 2)
                if there(it, n + 3):
                    invert(it, n + 3)
                if there(it, n + 2):
                    query_lo(it, n + 2)
                if b == 0 and group(it, G + 1):
                    input_lo(it, G + 1, 1)

            pool.sem_clear(used_before)
            pool.memset(power[:, :], -0.5).then_inc(filled, 1)
            pool.memset(maxes[:, :], 0.0).then_inc(filled, 1)
            pool.memset(masked[:, :], MASKED).then_inc(filled, 1)
            for x in v:
                pool.memset(x[:, :, :, DL:DL + 1], 1.0).then_inc(filled, 2)
            pool.wait_ge(filled, 19)
            run(pool, slot)

        @block.sync
        def _(sp):
            sp.dma_start(ctx_in[:, :, :], t["ctx_768"][0:GB, :, :].rearrange("b p d -> p b d")).then_inc(ctx_loaded, 16)
            sp.wait_ge(ready["ffn0"], 16)
            sp.dma_start(sb["raw_ffn1"][:, :], t["w_ffn1"]).then_inc(ready["ffn1"], 16)
            with sp.Fori(1, NG) as G:
                sp.wait_ge(normal_done, G * (2 * GB))
                sp.dma_start(ctx_in[:, :, :], t["ctx_768"][bass.ds(G * GB, GB), :, :].rearrange("b p d -> p b d"))\
                    .then_inc(ctx_loaded, 16)


def store(nc, sb, out, sem):
    stored = sem("stored")
    with nc.Block() as block:
        @block.sync
        def _(sp):
            sp.dma_start(out.rearrange("b p d -> p b d"), sb["x"][:, :].rearrange("p (b d) -> p b d", d=D))\
                .then_inc(stored, 16)
            sp.wait_ge(stored, 16)


def decoder(nc, t, out):
    with ExitStack() as ctx:
        def buf(name, shape, dt=F32):
            return ctx.enter_context(nc.sbuf_tensor(name, shape, dt))

        def sem(name):
            return ctx.enter_context(nc.semaphore(name))

        sb = {
            "x": buf("x_all", [P, B * D]),
            "const_r": buf("const_r", [P, N_CONST_R], F32R),
            "ident": buf("ident", [P, P]),
            "const": buf("const", [P, N_CONST - N_CONST_R]),
            "cols": buf("cols", [P, N_COLS]),
            "rows": buf("rows", [P, N_ROWS]),
            "rows_hi": buf("rows_hi", [P, N_ROWS_R], F32R),
            "rows_lo": buf("rows_lo", [P, N_ROWS_R], F32R),
        }
        sb["mask_by_row"] = buf("mask_by_row", [P, B * P], U8)
        sb["mask_by_col"] = buf("mask_by_col", [P, B], U8)
        sb["raw_xattn1"] = buf("raw_xattn1", [P, W_LATENT])
        ps = [ctx.enter_context(nc.psum_tensor(f"bank{i}", [P, 512], F32)) for i in range(8)]
        ready = {name: sem(f"{name}_weights_in") for name in ("x", "ffn0", "xattn1", "ffn1")}
        with ExitStack() as early:
            def buf(name, shape, dt=F32):
                return early.enter_context(nc.sbuf_tensor(name, shape, dt))

            sb.update({
                "w_hi": buf("w_hi", [P, N_WEIGHTS], F32R),
                "w_lo": buf("w_lo", [P, N_WEIGHTS], F32R),
                "raw_ffn0": buf("raw_ffn0", [P, W_FFN0]),
                "v": [buf(f"values{i}", [P, GB, H, VW]) for i in range(2)],
                "units": [buf(f"unit{i}", [P, U, P], F32R) for i in range(12)],
                "maxes": buf("maxes", [P, U, 32]),
            })
            load_setup(nc, t["x"], t["weights"], t["cols"], t["rows"], t["consts"],
                       [("ffn0", "raw_ffn0", t["w_ffn0"]), ("xattn1", "raw_xattn1", t["w_xattn1"]),
                        ("xattn1", "mask_by_row", t["mask_by_row"]), ("xattn1", "mask_by_col", t["mask_by_col"])],
                       sb, sem, ready)
            attention(nc, 0, "self", sb, ps, None, ready["x"])
            with ExitStack() as kept:
                sb["x_before"] = kept.enter_context(nc.sbuf_tensor("x_before", [P, B * D], F32))
                sb["key_sums"] = kept.enter_context(nc.sbuf_tensor("key_sums", [DC, B], F32))
                sb["lo_sums"] = kept.enter_context(nc.sbuf_tensor("lo_sums", [P, 2 * NG], F32))
                attention(nc, 1, "cross", sb, ps, t["ctx_768"])
                uniform_guard(nc, 2, sb, ps)
            gated_experts(nc, 3, sb, ps, ready)
            attention(nc, 4, "causal", sb, ps)
        sb["raw_ffn1"] = ctx.enter_context(nc.sbuf_tensor("raw_ffn1", [P, W_FFN1], F32))
        latent_attention(nc, 5, sb, ps, t, ready)
        relu_experts(nc, 6, sb, ps, ready)
        store(nc, sb, out, sem)


def shape_constants():
    c = np.zeros((P, N_CONST), np.float32)
    eye = np.eye(P, dtype=np.float32)
    c[:, C_ID:C_ID + P] = eye
    for u in range(U):
        c[32 * u:32 * u + 32, C_ONES + u * P:C_ONES + (u + 1) * P] = 1.0
        for g in range(U):
            c[32 * u + g, C_DIAG + g] = 1.0
            c[32 * u + DH * g:32 * u + DH * (g + 1), C_SLOT + g] = 1.0
    e = np.arange(E0)
    c[:, C_EARLIER:C_EARLIER + E0 * E0] = (e[None, :] < e[:, None]).astype(np.float32).reshape(1, -1)
    for h in range(2):
        c[h * P // 2:(h + 1) * P // 2, C_HEAD + h] = 1.0
    for e in range(E1):
        c[[e, E1 + e], C_ONE_ROW + e * P:C_ONE_ROW + (e + 1) * P] = 1.0
    for k in range(E0 // 2):
        c[[2 * k, E0 + 2 * k], C_PAIR + k * P:C_PAIR + k * P + P // 2] = 1.0
        c[[2 * k + 1, E0 + 2 * k + 1], C_PAIR + k * P + P // 2:C_PAIR + (k + 1) * P] = 1.0
    hidden = np.triu(np.ones((P, P), np.float32), 1) * np.float32(MASKED)
    c[:, C_MASK:C_MASK + P] = hidden
    c[:, C_MASK + P:C_MASK + 2 * P] = hidden.T
    rate = (np.float32(1.0) / np.float32(10000.0) ** (np.arange(0, DH, 2, dtype=np.float32) / np.float32(DH)))
    ch = np.arange(D)
    angle = (rate[ch % (DH // 2)][:, None] * np.arange(P, dtype=np.float32)[None, :]).astype(np.float32)
    sign = np.where(ch % DH < DH // 2, -1, 1).astype(np.float32)[:, None]
    c[:, C_ROPE:C_ROPE + P] = np.cos(angle)
    c[:, C_ROPE + P:C_ROPE + 2 * P] = sign * np.sin(angle)
    angle = (rate[ch % DH // 2] * (ch // DH).astype(np.float32)).astype(np.float32)
    sign = np.where(ch % 2 == 0, -1, 1).astype(np.float32)
    for n, table in enumerate((np.cos(angle), sign * np.sin(angle))):
        c[:, C_TURN + n * P:C_TURN + (n + 1) * P] = table[None, :]
        c[:, C_TURN_COL + n] = table
    return c


def packed(i):
    ch = np.arange(D)
    half = ch // DH * DH + (ch % DH + DH // 2) % DH
    pair = ch ^ 1
    rows_of = lambda v: np.broadcast_to(v, (P, len(v)))
    pad = lambda w: np.concatenate([w, np.zeros((P - len(w),) + w.shape[1:], w.dtype)])
    wq, wk, wv, wo = (i["L0_attn_" + n].T for n in ("Wq", "Wk", "Wv", "Wo"))
    bq, bk = i["L0_attn_bq"], i["L0_attn_bk"]
    w = [wq, wq[:, half], wk, wk[:, half], wv, wo]
    cols = [bq, bq[half], bk, bk[half]]
    bo, bv = [i["L0_attn_bo"]], [i["L0_attn_bv"]]
    xq, xk, xv, xo = (i["L0_xattn_" + n] for n in ("Wq", "Wk", "Wv", "Wo"))
    w += [xq, xq, pad(xk), pad(xk), pad(xv), xo]
    cols += [i["L0_xattn_bq"]] * 2 + [i["L0_xattn_bk"]] * 2
    bo += [i["L0_xattn_bo"]]
    bv += [i["L0_xattn_bv"]]
    q, k, v = (i["L1_attn_W_attn"][:, n * D:(n + 1) * D] for n in range(3))
    bq, bk, bv1 = (i["L1_attn_b_attn"][n * D:(n + 1) * D] for n in range(3))
    w += [q, q[:, pair], k, k[:, pair], v, i["L1_attn_W_proj"]]
    cols += [bq, bq[pair], bk, bk[pair]]
    bo += [i["L1_attn_b_proj"]]
    bv += [bv1]
    
    twice = lambda v: np.concatenate([v, v])
    xa = {n: i["L1_xattn_" + n] for n in ("ln_x_g", "ln_x_b", "ln_l_g", "ln_l_b", "qn_g", "kn_g", "Wq", "Wkv", "Wlkv", "Wo", "bo")}
    cols += [pad(xa["ln_x_g"]), pad(xa["ln_x_b"]), xa["ln_l_g"], xa["ln_l_b"], twice(xa["qn_g"]), twice(xa["kn_g"]),
             i["L0_xattn_bv"]]
    rows = bo + [xa["bo"]] + bv + [i["L0_ffn_router_b"], i["L1_ffn_router_b"]]
    w_xattn1 = np.concatenate([xa["Wq"].T, xa["Wlkv"].T, pad(xa["Wkv"].T), xa["Wo"].T], 1)
    mask = i["mask_BxS2_bk0"]
    cols += list(i["L1_ffn_b1"].reshape(E1 * C1, P))
    w_ffn1 = np.concatenate([i["L1_ffn_w1"].transpose(1, 0, 2).reshape(D, E1 * F1),
                             i["L1_ffn_w2"].reshape(E1 * C1, P, D).transpose(1, 0, 2).reshape(P, -1),
                             pad(np.concatenate([i["L1_ffn_b2"]] * 2)), i["L1_ffn_router_w"]], 1)

    def experts(routed, shared):
        both = np.concatenate([i["L0_ffn_routed_" + routed], i["L0_ffn_shared_" + shared]])
        return both.transpose(1, 0, 2).reshape(D, -1)

    w2 = np.concatenate([i["L0_ffn_routed_w2"], i["L0_ffn_shared_w2"]]).reshape(-1, P, D)
    w_ffn0 = np.concatenate([experts("w1", "w1"), experts("w3", "w3"), w2.transpose(1, 0, 2).reshape(P, -1),
                             i["L0_ffn_router_w"]], 1)
    return {
        "w_xattn1": w_xattn1,
        "mask_by_row": rows_of(mask.reshape(-1)), "mask_by_col": mask.T,
        "w_ffn0": w_ffn0, "w_ffn1": w_ffn1,
        "x": i["x"], "ctx_768": i["ctx_768"],
        "weights": np.concatenate(w, 1),
        "cols": np.stack(cols, 1),
        "rows": np.concatenate([rows_of(r) for r in rows], 1),
        "consts": shape_constants(),
    }


def kernel(**inputs):
    import concourse.bacc as bacc
    from concourse.bass_utils import run_bass_kernel_spmd

    nc = bacc.Bacc("TRN2", target_bir_lowering=False, num_devices=1)
    arrays, drams = {}, {}
    for name, a in packed({k: np.asarray(v) for k, v in inputs.items()}).items():
        a = np.ascontiguousarray(a)
        arrays[f"in_{name}"] = a
        drams[name] = nc.dram_tensor(f"in_{name}", a.shape, mybir.dt.from_np(a.dtype), kind="ExternalInput").ap()
    out = nc.dram_tensor("out_x", (B, P, D), F32, kind="ExternalOutput").ap()
    decoder(nc, drams, out)
    result = run_bass_kernel_spmd(nc, [arrays], core_ids=[0])
    return result.results[0]["out_x"]
```
